# Optimizing a Trainium2 kernel written in Bass

```python
import numpy as np
import jax
import jax.numpy as jnp

def _softmax(x, axis=-1):
    return jax.nn.softmax(x, axis=axis)

def _gelu(x):
    return jax.nn.gelu(x, approximate=True)

def _silu(x):
    return jax.nn.silu(x)

def _sigmoid(x):
    return jax.nn.sigmoid(x)

def _layernorm(x, axis=-1, eps=1e-05):
    m = jnp.mean(x, axis=axis, keepdims=True)
    v = jnp.var(x, axis=axis, keepdims=True)
    return (x - m) / jnp.sqrt(v + eps)

def _scatter_add(tgt, idx, src, axis=0):
    return tgt.at[idx].add(src)

def _segment_sum(src, seg, n):
    return jax.ops.segment_sum(src, seg, n)
kernel_name = 'mk_vit_tower_d2_tok_img1024_r4_277f42'

def setup_inputs(seed: int=0):
    np.random.seed(seed)
    _w = jnp.asarray

    def _rec_inputs():
        import jax
        import jax.numpy as jnp
        _rk = jax.random.key(seed)
        x = -0.000125008 + 0.999885 * jax.random.normal(jax.random.fold_in(_rk, 1), (8, 512, 256, 4), jnp.float32)
        return x
    x = _rec_inputs()

    def _L0_tok_setup():
        import jax, jax.numpy as jnp
        import numpy as np
        key = jax.random.key(seed)
        k1, k2, k3 = jax.random.split(key, 3)
        B, H, I, O, Dp1 = (4, 512, 256, 256, 4)
        x = jax.random.normal(k1, (B, H, I, Dp1), dtype=jnp.float32)
        weight = 0.1 * jax.random.normal(k2, (O, Dp1), dtype=jnp.float32)
        weighted_sum = 0.1 * jax.random.normal(k3, (O, I), dtype=jnp.float32)
        return {'x': x, 'weight': weight, 'weighted_sum': weighted_sum}
    _L0_tok_all = _L0_tok_setup()
    _L0_tok_in = {k: v for k, v in _L0_tok_all.items() if k in ('weight', 'weighted_sum')}
    del _L0_tok_all

    def _L0_attn_setup():
        import jax, jax.numpy as jnp
        import numpy as np
        B, L, D_MODEL = (2, 256, 256)
        EXPAND = 2
        D_INNER = EXPAND * D_MODEL
        D_STATE = 16
        D_CONV = 4
        DT_RANK = D_MODEL // 16

        def _mamba(x, W_in, conv_w, conv_b, W_xproj, W_dt, b_dt, A_log, D_skip, W_out):
            b, l, _ = x.shape
            xz = jnp.einsum('bld,de->ble', x, W_in)
            x_in, z = jnp.split(xz, 2, axis=-1)
            xt = jnp.transpose(x_in, (0, 2, 1))
            xt = jnp.pad(xt, ((0, 0), (0, 0), (D_CONV - 1, 0)))
            conv = jax.lax.conv_general_dilated(xt, conv_w, window_strides=(1,), padding='VALID', dimension_numbers=('NCH', 'OIH', 'NCH'), feature_group_count=D_INNER)
            conv = conv + conv_b[None, :, None]
            u = jax.nn.silu(jnp.transpose(conv, (0, 2, 1)))
            x_dbl = jnp.einsum('bld,de->ble', u, W_xproj)
            dt_lr = x_dbl[..., :DT_RANK]
            Bm = x_dbl[..., DT_RANK:DT_RANK + D_STATE]
            Cm = x_dbl[..., DT_RANK + D_STATE:]
            delta = jax.nn.softplus(jnp.einsum('blr,rd->bld', dt_lr, W_dt) + b_dt)
            A = -jnp.exp(A_log)
            dA = jnp.exp(jnp.einsum('bld,dn->bldn', delta, A))
            dBu = (delta * u)[..., None] * Bm[:, :, None, :]

            def step(h, inp):
                dA_t, dBu_t, C_t = inp
                h = dA_t * h + dBu_t
                y_t = jnp.einsum('bdn,bn->bd', h, C_t)
                return (h, y_t)
            h0 = jnp.zeros((b, D_INNER, D_STATE), x.dtype)
            _, ys = jax.lax.scan(step, h0, (jnp.swapaxes(dA, 0, 1), jnp.swapaxes(dBu, 0, 1), jnp.swapaxes(Cm, 0, 1)))
            y = jnp.swapaxes(ys, 0, 1)
            y = y + D_skip * u
            y = y * jax.nn.silu(z)
            out = jnp.einsum('bld,de->ble', y, W_out)
            return out
        key = jax.random.key(seed)
        ks = jax.random.split(key, 8)
        s = 0.02
        x = jax.random.normal(ks[0], (B, L, D_MODEL), jnp.float32)
        W_in = jax.random.normal(ks[1], (D_MODEL, 2 * D_INNER), jnp.float32) * s
        conv_w = jax.random.normal(ks[2], (D_INNER, 1, D_CONV), jnp.float32) * 0.2
        conv_b = jnp.zeros((D_INNER,), jnp.float32)
        W_xproj = jax.random.normal(ks[3], (D_INNER, DT_RANK + 2 * D_STATE), jnp.float32) * s
        W_dt = jax.random.normal(ks[4], (DT_RANK, D_INNER), jnp.float32) * DT_RANK ** (-0.5)
        b_dt = jnp.full((D_INNER,), -4.6, jnp.float32)
        A_log = jnp.log(jnp.broadcast_to(jnp.arange(1, D_STATE + 1, dtype=jnp.float32), (D_INNER, D_STATE)))
        D_skip = jnp.ones((D_INNER,), jnp.float32)
        W_out = jax.random.normal(ks[5], (D_INNER, D_MODEL), jnp.float32) * s
        return dict(x=x, W_in=W_in, conv_w=conv_w, conv_b=conv_b, W_xproj=W_xproj, W_dt=W_dt, b_dt=b_dt, A_log=A_log, D_skip=D_skip, W_out=W_out)
    _L0_attn_all = _L0_attn_setup()
    _L0_attn_in = {k: v for k, v in _L0_attn_all.items() if k in ('W_in', 'conv_w', 'conv_b', 'W_xproj', 'W_dt', 'b_dt', 'A_log', 'D_skip', 'W_out')}
    del _L0_attn_all

    def _L0_ffn_setup():
        import jax, jax.numpy as jnp
        import numpy as np
        TOP_K = 4
        N_GROUP = 4
        TOPK_GROUP = 2
        ROUTED_SCALING = 2.5

        def _route(x, gate_weight):
            scores = jax.nn.sigmoid(x @ gate_weight.T)
            T, E = scores.shape
            gs = E // N_GROUP
            top2, _ = jax.lax.top_k(scores.reshape(T, N_GROUP, gs), 2)
            group_scores = top2.sum(-1)
            _, gidx = jax.lax.top_k(group_scores, TOPK_GROUP)
            gmask = jax.nn.one_hot(gidx, N_GROUP, dtype=jnp.float32).sum(1)
            smask = jnp.repeat(gmask, gs, axis=1) > 0.5
            masked = jnp.where(smask, scores, 0.0)
            topk_idx = jax.lax.top_k(masked, TOP_K)[1]
            topk_w = jnp.take_along_axis(scores, topk_idx, axis=1)
            topk_w = topk_w / (topk_w.sum(-1, keepdims=True) + 1e-20)
            topk_w = topk_w * ROUTED_SCALING
            combine = jnp.zeros((T, E), jnp.float32).at[jnp.arange(T)[:, None], topk_idx].add(topk_w)
            return combine
        key = jax.random.key(seed)
        ks = jax.random.split(key, 6)
        B, S, H = (2, 256, 256)
        E, I, Is = (16, 128, 512)
        g = lambda k, shape, scale: jax.random.normal(k, shape, dtype=jnp.float32) * scale
        return {'hidden_states': g(ks[0], (B, S, H), 1.0), 'gate_weight': g(ks[1], (E, H), 0.02), 'expert_up': g(ks[2], (E, H, I), 0.02), 'expert_down': g(ks[3], (E, I, H), 0.02), 'shared_up': g(ks[4], (H, Is), 0.02), 'shared_down': g(ks[5], (Is, H), 0.02)}
    _L0_ffn_all = _L0_ffn_setup()
    _L0_ffn_in = {k: v for k, v in _L0_ffn_all.items() if k in ('gate_weight', 'expert_up', 'expert_down', 'shared_up', 'shared_down')}
    del _L0_ffn_all

    def _L1_attn_setup():
        import jax, jax.numpy as jnp
        import numpy as np
        T, B, E, H = (256, 2, 256, 16)
        D = E // H
        R = 2 * T - 1

        def _rel_shift(x):
            b, h, q, r = x.shape
            zp = jnp.zeros((b, h, q, 1), x.dtype)
            xp = jnp.concatenate([zp, x], axis=3)
            xp = xp.reshape(b, h, r + 1, q)[:, :, 1:, :]
            return xp.reshape(b, h, q, r)
        key = jax.random.key(seed)
        ks = jax.random.split(key, 8)
        std = (2.0 / (E + E)) ** 0.5
        return {'x': jax.random.normal(ks[0], (T, B, E), jnp.float32), 'pos': jax.random.normal(ks[1], (R, 1, E), jnp.float32), 'in_proj_weight': jax.random.normal(ks[2], (3 * E, E), jnp.float32) * std, 'in_proj_bias': jnp.zeros((3 * E,), jnp.float32), 'pos_proj_weight': jax.random.normal(ks[3], (E, E), jnp.float32) * std, 'pos_proj_bias': jnp.zeros((E,), jnp.float32), 'out_proj_weight': jax.random.normal(ks[4], (E, E), jnp.float32) * std, 'out_proj_bias': jnp.zeros((E,), jnp.float32), 'r_w_bias': jax.random.normal(ks[5], (H, D), jnp.float32) * 0.02, 'r_r_bias': jax.random.normal(ks[6], (H, D), jnp.float32) * 0.02}
    _L1_attn_all = _L1_attn_setup()
    _L1_attn_in = {k: v for k, v in _L1_attn_all.items() if k in ('pos', 'in_proj_weight', 'in_proj_bias', 'pos_proj_weight', 'pos_proj_bias', 'out_proj_weight', 'out_proj_bias', 'r_w_bias', 'r_r_bias')}
    del _L1_attn_all

    def _L1_ffn_setup():
        import jax, jax.numpy as jnp
        import numpy as np
        B, S, H, F, E = (8, 512, 256, 1024, 8)
        INIT_LAMBDA = 0.2
        key = jax.random.key(seed)
        ks = jax.random.split(key, 12)
        std = 0.02
        return {'hidden_states': jax.random.normal(ks[0], (B, S, H), jnp.float32), 'gate_w1': jax.random.normal(ks[1], (H, H), jnp.float32) * 0.01, 'gate_b1': jnp.zeros((H,), jnp.float32), 'gate_w2': jax.random.normal(ks[2], (E, H), jnp.float32) * 0.01, 'gate_b2': jnp.full((E,), INIT_LAMBDA, jnp.float32), 'W1': jax.random.normal(ks[3], (F, H), jnp.float32) * std, 'b1': jax.random.normal(ks[4], (F,), jnp.float32) * std, 'W2': jax.random.normal(ks[5], (H, F), jnp.float32) * std, 'b2': jax.random.normal(ks[6], (H,), jnp.float32) * std, 'TW1': jax.random.normal(ks[7], (E, F, H), jnp.float32) * std, 'Tb1': jax.random.normal(ks[8], (E, F), jnp.float32) * std, 'TW2': jax.random.normal(ks[9], (E, H, F), jnp.float32) * std, 'Tb2': jax.random.normal(ks[10], (E, H), jnp.float32) * std}
    _L1_ffn_all = _L1_ffn_setup()
    _L1_ffn_in = {k: v for k, v in _L1_ffn_all.items() if k in ('gate_w1', 'gate_b1', 'gate_w2', 'gate_b2', 'W1', 'b1', 'W2', 'b2', 'TW1', 'Tb1', 'TW2', 'Tb2')}
    del _L1_ffn_all
    return {'x': x, 'L0_tok_weight': _L0_tok_in['weight'], 'L0_tok_weighted_sum': _L0_tok_in['weighted_sum'], 'L0_attn_W_in': _L0_attn_in['W_in'], 'L0_attn_conv_w': _L0_attn_in['conv_w'], 'L0_attn_conv_b': _L0_attn_in['conv_b'], 'L0_attn_W_xproj': _L0_attn_in['W_xproj'], 'L0_attn_W_dt': _L0_attn_in['W_dt'], 'L0_attn_b_dt': _L0_attn_in['b_dt'], 'L0_attn_A_log': _L0_attn_in['A_log'], 'L0_attn_D_skip': _L0_attn_in['D_skip'], 'L0_attn_W_out': _L0_attn_in['W_out'], 'L0_ffn_gate_weight': _L0_ffn_in['gate_weight'], 'L0_ffn_expert_up': _L0_ffn_in['expert_up'], 'L0_ffn_expert_down': _L0_ffn_in['expert_down'], 'L0_ffn_shared_up': _L0_ffn_in['shared_up'], 'L0_ffn_shared_down': _L0_ffn_in['shared_down'], 'L1_attn_pos': _L1_attn_in['pos'], 'L1_attn_in_proj_weight': _L1_attn_in['in_proj_weight'], 'L1_attn_in_proj_bias': _L1_attn_in['in_proj_bias'], 'L1_attn_pos_proj_weight': _L1_attn_in['pos_proj_weight'], 'L1_attn_pos_proj_bias': _L1_attn_in['pos_proj_bias'], 'L1_attn_out_proj_weight': _L1_attn_in['out_proj_weight'], 'L1_attn_out_proj_bias': _L1_attn_in['out_proj_bias'], 'L1_attn_r_w_bias': _L1_attn_in['r_w_bias'], 'L1_attn_r_r_bias': _L1_attn_in['r_r_bias'], 'L1_ffn_gate_w1': _L1_ffn_in['gate_w1'], 'L1_ffn_gate_b1': _L1_ffn_in['gate_b1'], 'L1_ffn_gate_w2': _L1_ffn_in['gate_w2'], 'L1_ffn_gate_b2': _L1_ffn_in['gate_b2'], 'L1_ffn_W1': _L1_ffn_in['W1'], 'L1_ffn_b1': _L1_ffn_in['b1'], 'L1_ffn_W2': _L1_ffn_in['W2'], 'L1_ffn_b2': _L1_ffn_in['b2'], 'L1_ffn_TW1': _L1_ffn_in['TW1'], 'L1_ffn_Tb1': _L1_ffn_in['Tb1'], 'L1_ffn_TW2': _L1_ffn_in['TW2'], 'L1_ffn_Tb2': _L1_ffn_in['Tb2']}

def reference(x, L0_tok_weight, L0_tok_weighted_sum, L0_attn_W_in, L0_attn_conv_w, L0_attn_conv_b, L0_attn_W_xproj, L0_attn_W_dt, L0_attn_b_dt, L0_attn_A_log, L0_attn_D_skip, L0_attn_W_out, L0_ffn_gate_weight, L0_ffn_expert_up, L0_ffn_expert_down, L0_ffn_shared_up, L0_ffn_shared_down, L1_attn_pos, L1_attn_in_proj_weight, L1_attn_in_proj_bias, L1_attn_pos_proj_weight, L1_attn_pos_proj_bias, L1_attn_out_proj_weight, L1_attn_out_proj_bias, L1_attn_r_w_bias, L1_attn_r_r_bias, L1_ffn_gate_w1, L1_ffn_gate_b1, L1_ffn_gate_w2, L1_ffn_gate_b2, L1_ffn_W1, L1_ffn_b1, L1_ffn_W2, L1_ffn_b2, L1_ffn_TW1, L1_ffn_Tb1, L1_ffn_TW2, L1_ffn_Tb2):
    import jax
    import jax.numpy as jnp

    def _L0_tok_ref(x, weight, weighted_sum):
        import jax, jax.numpy as jnp
        import numpy as np
        return jnp.einsum('bhid,oi,od->bho', x, weighted_sum, weight)

    def _L0_attn_ref(x, W_in, conv_w, conv_b, W_xproj, W_dt, b_dt, A_log, D_skip, W_out):
        import jax, jax.numpy as jnp
        import numpy as np
        B, L, D_MODEL = (2, 256, 256)
        EXPAND = 2
        D_INNER = EXPAND * D_MODEL
        D_STATE = 16
        D_CONV = 4
        DT_RANK = D_MODEL // 16

        def _mamba(x, W_in, conv_w, conv_b, W_xproj, W_dt, b_dt, A_log, D_skip, W_out):
            b, l, _ = x.shape
            xz = jnp.einsum('bld,de->ble', x, W_in)
            x_in, z = jnp.split(xz, 2, axis=-1)
            xt = jnp.transpose(x_in, (0, 2, 1))
            xt = jnp.pad(xt, ((0, 0), (0, 0), (D_CONV - 1, 0)))
            conv = jax.lax.conv_general_dilated(xt, conv_w, window_strides=(1,), padding='VALID', dimension_numbers=('NCH', 'OIH', 'NCH'), feature_group_count=D_INNER)
            conv = conv + conv_b[None, :, None]
            u = jax.nn.silu(jnp.transpose(conv, (0, 2, 1)))
            x_dbl = jnp.einsum('bld,de->ble', u, W_xproj)
            dt_lr = x_dbl[..., :DT_RANK]
            Bm = x_dbl[..., DT_RANK:DT_RANK + D_STATE]
            Cm = x_dbl[..., DT_RANK + D_STATE:]
            delta = jax.nn.softplus(jnp.einsum('blr,rd->bld', dt_lr, W_dt) + b_dt)
            A = -jnp.exp(A_log)
            dA = jnp.exp(jnp.einsum('bld,dn->bldn', delta, A))
            dBu = (delta * u)[..., None] * Bm[:, :, None, :]

            def step(h, inp):
                dA_t, dBu_t, C_t = inp
                h = dA_t * h + dBu_t
                y_t = jnp.einsum('bdn,bn->bd', h, C_t)
                return (h, y_t)
            h0 = jnp.zeros((b, D_INNER, D_STATE), x.dtype)
            _, ys = jax.lax.scan(step, h0, (jnp.swapaxes(dA, 0, 1), jnp.swapaxes(dBu, 0, 1), jnp.swapaxes(Cm, 0, 1)))
            y = jnp.swapaxes(ys, 0, 1)
            y = y + D_skip * u
            y = y * jax.nn.silu(z)
            out = jnp.einsum('bld,de->ble', y, W_out)
            return out
        return _mamba(x, W_in, conv_w, conv_b, W_xproj, W_dt, b_dt, A_log, D_skip, W_out)

    def _L0_ffn_ref(hidden_states, gate_weight, expert_up, expert_down, shared_up, shared_down):
        import jax, jax.numpy as jnp
        import numpy as np
        TOP_K = 4
        N_GROUP = 4
        TOPK_GROUP = 2
        ROUTED_SCALING = 2.5

        def _route(x, gate_weight):
            scores = jax.nn.sigmoid(x @ gate_weight.T)
            T, E = scores.shape
            gs = E // N_GROUP
            top2, _ = jax.lax.top_k(scores.reshape(T, N_GROUP, gs), 2)
            group_scores = top2.sum(-1)
            _, gidx = jax.lax.top_k(group_scores, TOPK_GROUP)
            gmask = jax.nn.one_hot(gidx, N_GROUP, dtype=jnp.float32).sum(1)
            smask = jnp.repeat(gmask, gs, axis=1) > 0.5
            masked = jnp.where(smask, scores, 0.0)
            topk_idx = jax.lax.top_k(masked, TOP_K)[1]
            topk_w = jnp.take_along_axis(scores, topk_idx, axis=1)
            topk_w = topk_w / (topk_w.sum(-1, keepdims=True) + 1e-20)
            topk_w = topk_w * ROUTED_SCALING
            combine = jnp.zeros((T, E), jnp.float32).at[jnp.arange(T)[:, None], topk_idx].add(topk_w)
            return combine
        B, S, H = hidden_states.shape
        x = hidden_states.reshape(-1, H)
        combine = _route(x.astype(jnp.float32), gate_weight)
        up = jnp.einsum('th,ehi->eti', x, expert_up)
        down = jnp.einsum('eti,eih->eth', jax.nn.silu(up), expert_down)
        moe_out = jnp.einsum('te,eth->th', combine, down)
        shared = jax.nn.silu(x @ shared_up) @ shared_down
        return (moe_out + shared).reshape(B, S, H)

    def _L1_attn_ref(x, pos, in_proj_weight, in_proj_bias, pos_proj_weight, pos_proj_bias, out_proj_weight, out_proj_bias, r_w_bias, r_r_bias):
        import jax, jax.numpy as jnp
        import numpy as np
        T, B, E, H = (256, 2, 256, 16)
        D = E // H
        R = 2 * T - 1

        def _rel_shift(x):
            b, h, q, r = x.shape
            zp = jnp.zeros((b, h, q, 1), x.dtype)
            xp = jnp.concatenate([zp, x], axis=3)
            xp = xp.reshape(b, h, r + 1, q)[:, :, 1:, :]
            return xp.reshape(b, h, q, r)
        t, b, e = x.shape
        h, d = r_w_bias.shape
        qkv = x @ in_proj_weight.T + in_proj_bias
        q, k, v = jnp.split(qkv, 3, axis=-1)
        q = q.reshape(t, b, h, d)
        k = k.reshape(t, b, h, d)
        v = v.reshape(t, b, h, d)
        p = (pos @ pos_proj_weight.T + pos_proj_bias).reshape(-1, h, d)
        scale = 1.0 / jnp.sqrt(jnp.asarray(d, x.dtype))
        ac = jnp.einsum('tbhd,sbhd->bhts', q + r_w_bias, k)
        bd = jnp.einsum('tbhd,rhd->bhtr', q + r_r_bias, p)
        bd = _rel_shift(bd)[..., :t]
        attn = jax.nn.softmax((ac + bd) * scale, axis=-1)
        ctx = jnp.einsum('bhts,sbhd->tbhd', attn, v).reshape(t, b, e)
        return ctx @ out_proj_weight.T + out_proj_bias

    def _L1_ffn_ref(hidden_states, gate_w1, gate_b1, gate_w2, gate_b2, W1, b1, W2, b2, TW1, Tb1, TW2, Tb2):
        import jax, jax.numpy as jnp
        import numpy as np
        B, S, H, F, E = (8, 512, 256, 1024, 8)
        INIT_LAMBDA = 0.2
        x = hidden_states
        h = jax.nn.relu(jnp.einsum('bsh,oh->bso', x, gate_w1) + gate_b1)
        g = jnp.einsum('bso,eo->bse', h, gate_w2) + gate_b2
        g = g.mean(axis=1)
        mW1 = W1 + jnp.einsum('be,efh->bfh', g, TW1)
        mb1 = b1 + g @ Tb1
        mW2 = W2 + jnp.einsum('be,ehf->bhf', g, TW2)
        mb2 = b2 + g @ Tb2
        u = jax.nn.gelu(jnp.einsum('bsh,bfh->bsf', x, mW1) + mb1[:, None, :])
        out = jnp.einsum('bsf,bhf->bsh', u, mW2) + mb2[:, None, :]
        return out
    h = _L0_tok_ref(x, L0_tok_weight, L0_tok_weighted_sum)
    h = h + _L0_attn_ref(_layernorm(h, axis=-1), L0_attn_W_in, L0_attn_conv_w, L0_attn_conv_b, L0_attn_W_xproj, L0_attn_W_dt, L0_attn_b_dt, L0_attn_A_log, L0_attn_D_skip, L0_attn_W_out)
    h = h + _L0_ffn_ref(_layernorm(h, axis=-1), L0_ffn_gate_weight, L0_ffn_expert_up, L0_ffn_expert_down, L0_ffn_shared_up, L0_ffn_shared_down)
    h = h + _L1_attn_ref(_layernorm(h, axis=-1), L1_attn_pos, L1_attn_in_proj_weight, L1_attn_in_proj_bias, L1_attn_pos_proj_weight, L1_attn_pos_proj_bias, L1_attn_out_proj_weight, L1_attn_out_proj_bias, L1_attn_r_w_bias, L1_attn_r_r_bias)
    h = h + _L1_ffn_ref(_layernorm(h, axis=-1), L1_ffn_gate_w1, L1_ffn_gate_b1, L1_ffn_gate_w2, L1_ffn_gate_b2, L1_ffn_W1, L1_ffn_b1, L1_ffn_W2, L1_ffn_b2, L1_ffn_TW1, L1_ffn_Tb1, L1_ffn_TW2, L1_ffn_Tb2)
    return h

_drawn_inputs = setup_inputs


def setup_inputs(seed=0):
    import zlib

    import numpy as np

    out = dict(_drawn_inputs(seed))
    spreads = {'L0_attn_conv_b': (0.0, 0.269),
     'L0_attn_b_dt': (-4.599999904632568, 0.6),
     'L0_attn_D_skip': (1.0, 0.6),
     'L1_attn_in_proj_bias': (0.0, 0.1),
     'L1_attn_pos_proj_bias': (0.0, 2.0),
     'L1_attn_out_proj_bias': (0.0, 0.1),
     'L1_ffn_gate_b1': (0.0, 0.8),
     'L1_ffn_gate_b2': (0.20000000298023224, 0.2)}
    factors = {'L0_attn_W_xproj': 8.0,
     'L0_attn_W_dt': 8.0,
     'L0_attn_A_log': 38.257,
     'L1_attn_r_w_bias': 5.171,
     'L1_attn_r_r_bias': 5.29,
     'L1_ffn_gate_w1': 8.0,
     'L1_ffn_gate_w2': 4.955,
     'L1_ffn_b1': 4.625,
     'L1_ffn_Tb1': 7.155,
     'L1_ffn_Tb2': 3.044,
     'L1_ffn_b2': 2.825}
    for name, (base, spread) in spreads.items():
        noise = np.random.default_rng([zlib.crc32(name.encode()), seed]).standard_normal(out[name].shape)
        drawn = base * np.exp(spread * noise) if base else spread * noise
        out[name] = jnp.asarray(drawn.astype(out[name].dtype))
    for name, factor in factors.items():
        out[name] = (out[name] * factor).astype(out[name].dtype)
    return out
```

```python
from contextlib import ExitStack

import numpy as np
import concourse.bass as bass
from concourse import mybir

F32 = mybir.dt.float32
BF16 = mybir.dt.bfloat16
ALU = mybir.AluOpType
ACT = mybir.ActivationFunctionType
AX = mybir.AxisListType

P = 128
B, S, H = 8, 512, 256
HC = H // P
TOKD = 4
XC = H * TOKD // P
DI = 2 * H
DC = DI // P
NS = 16
TAPS = 4
E = 16
EI = 128
SC = 4
NG = 4
TOPK = 4
KSTEP = 2 * NS
MOE = E + SC
EPS = 1e-5


class Steps:

    def __init__(self, sem, names):
        self.sem = sem
        self.names = list(names)
        self.index = {n: k + 1 for k, n in enumerate(self.names)}
        assert len(self.index) == len(self.names)

    def at(self, rnd, name):
        return rnd * len(self.names) + self.index[name]


def tok_cols(b):
    return slice(b * S, (b + 1) * S) if isinstance(b, int) else bass.ts(b, S)


def spread_over(ap, n):
    return ap.rearrange("p (a b) -> p a b", a=1).to_broadcast([ap.shape[0], n, ap.shape[1]])


def vit_tower(nc, a, out):
    with ExitStack() as ctx:
        def sb(name, shape, dt=F32):
            return ctx.enter_context(nc.sbuf_tensor(name, shape, dt))

        def sem(name):
            return ctx.enter_context(nc.semaphore(name))

        hT = sb("hT", [P, HC, B * S])
        ident = sb("ident", [P, P])
        means = sb("means", [P, P])
        eps = sb("eps", [P, 1])
        ps = ctx.enter_context(nc.psum_tensor("ps", [P, 8, 512], F32))
        with ExitStack() as one:
            mamba_and_experts(nc, one, a, hT, ident, means, eps, ps)
        with ExitStack() as two:
            attention(nc, two, a, hT, ident, means, eps, ps)
        with ExitStack() as three:
            modulated_ffn(nc, three, a, out, hT, means, eps, ps)


def mamba_and_experts(nc, ctx, a, hT, ident, means, eps, ps):
    def sb(name, shape, dt=F32):
        return ctx.enter_context(nc.sbuf_tensor(name, shape, dt))

    def sem(name):
        return ctx.enter_context(nc.semaphore(name))

    tok_w = sb("tok_w", [P, XC, H])
    w_in = sb("w_in", [P, HC, 2 * DI])
    w_out = sb("w_out", [P, DC, H])
    w_x = sb("w_x", [P, DC, 112])
    w_dt = sb("w_dt", [P, DI])
    up_w = sb("up_w", [P, HC, E * EI])
    down_w = sb("down_w", [P, E, H])
    sup_w = sb("sup_w", [P, HC, SC * P])
    sdown_w = sb("sdown_w", [P, SC, H])
    gate_w = sb("gate_w", [P, HC, E])
    taps = sb("taps", [P, DC, TAPS])
    tap_b = sb("tap_b", [P, DC])
    b_dt = sb("b_dt", [P, DC])
    d_skip = sb("d_skip", [P, DC])
    a_neg = sb("a_neg", [P, DC, NS])
    pick_state = sb("pick_state", [96, 2 * NS, P], BF16)
    pick_expert = sb("pick_expert", [48, E, P], BF16)
    identb = sb("identb", [P, P], BF16)
    lower = sb("lower", [P, E, E])

    x_in = sb("x_in", [P, XC, S])
    u = sb("u", [P, DC, S])
    zg = sb("zg", [P, DC, S])
    delta = sb("delta", [P, DC, S])
    du = sb("du", [P, DC, S])
    bc = sb("bc", [96, S], BF16)
    mx = sb("mx", [P, HC, S])
    comb_t = sb("comb_t", [48, S], BF16)
    m_th = sb("m_th", [P, 2, S])
    m_act = sb("m_act", [P, 2, S])
    sc = sb("sc", [P, 4 * E])
    comb = sb("comb", [P, 4, E])
    comb_p = sb("comb_p", [P, 4, P // E, E], BF16)

    R = sb("R", [P, 8192])

    def view(at, *shape):
        n = int(np.prod(shape))
        v = R[:, at:at + n]
        if len(shape) == 2:
            v = v.rearrange("p (a b) -> p a b", a=shape[0])
        if len(shape) == 3:
            v = v.rearrange("p (a b c) -> p a b c", a=shape[0], b=shape[1])
        return v

    xc = view(0, HC, S)
    sq = view(1024, HC, S)
    rstd = view(2560, S)
    xpad = view(3072, DC, S + TAPS - 1)
    th = view(5132, DC, S)
    r_bc = view(7180, S)
    dtl = view(7680, S)
    dA = view(0, 2, 2, S)
    dBu = view(2048, 2, S)
    hs = view(3072, 2, S)
    hC = view(4096, 2, 2, S)
    y = view(6144, DC, S)
    c_gt = view(3072, 4, E * E)
    c_eq = view(4096, 4, E * E)
    pairs = view(5120, 6, 4 * NG)
    gsum = view(5300, 4 * NG)
    g_gt = view(5400, 4, NG * NG)
    g_eq = view(5500, 4, NG * NG)
    grank = view(5600, 4 * NG)
    masked = view(5700, 4 * E)
    rank = view(5800, 4 * E)
    wsum = view(5900, 4)
    wres = view(6000, 4 * E)
    den = view(6100, 4 * E)

    ws_t = view(0, HC, H)
    v_rep = view(512, TOKD, H)

    loaded, x_loaded = sem("loaded"), sem("x_loaded")

    setup_vector = Steps(sem("setup_vector"), [f"tok{k}" for k in range(XC)] + ["tap", "tapb", "cap", "aneg"]
                    + ["ib", "ps", "pe", "mh"])
    setup_scalar = Steps(sem("setup_scalar"), ["aexp"])
    front_tensor = Steps(sem("front_tensor"), ["tok", "mean", "var", "x_in", "z", "bcdt", "dt"])
    front_scalar = Steps(sem("front_scalar"), ["h", "sq", "std", "xpad", "thz", "thu", "dtl", "v", "abs", "exp", "ln"])
    front_vector = Steps(sem("front_vector"), ["pad", "xc", "rstd", "xn"] + [f"conv{j}" for j in range(TAPS)] + ["zg", "u"]
               + ["bc1", "r1", "bc2", "r2", "bc3"] + ["delta", "du"])
    scan_tensor = Steps(sem("scan_tensor"), scan_tensor_order() + ["proj"])
    scan_scalar = Steps(sem("scan_scalar"), [f"dA{k}" for k in range(KSTEP)])
    scan_vector = Steps(sem("scan_vector"), scan_vector_order() + ["res"])
    expert_tensor = Steps(sem("expert_tensor"), [n for j in range(MOE + 1) for n in
                                      ([f"up{j}"] + ([f"cb{j}"] if j < E else []) if j < MOE else [])
                                      + ([f"dn{j - 1}"] if j else [])])
    expert_scalar = Steps(sem("expert_scalar"), [f"th{j}" for j in range(MOE)])
    expert_vector = Steps(sem("expert_vector"), [n for j in range(MOE) for n in ([f"a{j}"] + ([f"c{j}"] if j < E else []))] + ["res"])
    route_tensor = Steps(sem("route_tensor"), ["mean", "var", "gate", "turn"])
    route_scalar = Steps(sem("route_scalar"), ["sq", "std", "e", "comb_t"])
    route_vector = Steps(sem("route_vector"), ["xc", "rstd", "xn", "s1", "s", "p0", "p1", "p2", "p3", "p4", "p5", "gs", "ggt", "geq",
                                     "geql", "gsumr", "gr", "gm", "msk", "cgt", "ceq", "ceql", "csum", "cr", "w", "ws",
                                     "wr", "rcp", "comb", "k1", "q1", "k2", "q2", "k3"])

    LOADS = 16 * 21

    with nc.Block() as block:
        @block.sync
        def _(sp):
            for dst, src in (
                (ident[:], a["ident"]), (means[:], a["means"]), (eps[:], a["eps"]),
                (ws_t, a["ws_t"].rearrange("(c p) o -> p c o", p=P)),
                (v_rep, a["tok_v"].rearrange("(n d) o -> n d o", n=1).to_broadcast([P, TOKD, H])),
                (w_in[:], a["w_in"].rearrange("(c p) o -> p c o", p=P)),
                (w_out[:], a["w_out"].rearrange("(c p) o -> p c o", p=P)),
                (w_x[:], a["w_x"].rearrange("(c p) o -> p c o", p=P)),
                (w_dt[96:112, :], a["w_dt"]),
                (up_w[:], a["up"].rearrange("(c p) o -> p c o", p=P)),
                (down_w[:], a["down"].rearrange("e p o -> p e o")),
                (sup_w[:], a["sup"].rearrange("(c p) o -> p c o", p=P)),
                (sdown_w[:], a["sdown"].rearrange("(c p) o -> p c o", p=P)),
                (gate_w[:], a["gate"].rearrange("(c p) o -> p c o", p=P)),
                (taps[:], a["taps"]), (tap_b[:], a["tap_b"]), (b_dt[:], a["b_dt"]), (d_skip[:], a["d_skip"]),
                (a_neg[:], a["a_log"]), (lower[:], a["lower"]), (x_in[:, :, :], a["x"][0]),
            ):
                sp.dma_start(dst, src).then_inc(loaded, 16)
            sp.dma_start(hT[0:96, :, :].rearrange("p a b -> p (a b)")[:, 0:2 * NS * P], a["pick_state"]).then_inc(x_loaded, 16)
            sp.dma_start(u[0:48, :, :].rearrange("p a b -> p (a b)"), a["pick_expert"]).then_inc(x_loaded, 16)
            for b in range(1, B):
                sp.wait_ge(front_tensor.sem, front_tensor.at(b - 1, "tok"))
                sp.dma_start(x_in[:, :, :], a["x"][b]).then_inc(x_loaded, 16)

        @block.scalar
        def _(act):
            def front(b):
                act.wait_ge(front_tensor.sem, front_tensor.at(b, "tok"))
                nc.scalar.activation(hT[:, :, tok_cols(b)], ps[:, 0:2, :], ACT.Copy).then_inc(front_scalar.sem, 1)
                act.wait_ge(front_vector.sem, front_vector.at(b, "xc"))
                nc.scalar.activation(sq, xc, ACT.Square).then_inc(front_scalar.sem, 1)
                act.wait_ge(front_tensor.sem, front_tensor.at(b, "var"))
                nc.scalar.activation(rstd, ps[:, 3, :], ACT.Sqrt, bias=eps[:, 0:1]).then_inc(front_scalar.sem, 1)
                act.wait_ge(front_tensor.sem, front_tensor.at(b, "x_in"))
                act.wait_ge(front_vector.sem, front_vector.at(b, "pad"))
                nc.scalar.activation(xpad[:, :, TAPS - 1:], ps[:, 4:8, :], ACT.Copy).then_inc(front_scalar.sem, 1)
                act.wait_ge(front_tensor.sem, front_tensor.at(b, "z"))
                nc.scalar.activation(th, ps[:, 0:4, :], ACT.Tanh, scale=0.5).then_inc(front_scalar.sem, 1)
                act.wait_ge(front_vector.sem, front_vector.at(b, "zg"))
                nc.scalar.activation(th, u[:], ACT.Tanh).then_inc(front_scalar.sem, 1)
                act.wait_ge(front_tensor.sem, front_tensor.at(b, "bcdt"))
                nc.scalar.activation(dtl[96:112, :], ps[96:112, 4, :], ACT.Copy).then_inc(front_scalar.sem, 1)
                act.wait_ge(front_tensor.sem, front_tensor.at(b, "dt"))
                act.wait_ge(front_vector.sem, front_vector.at(b, "u"))
                for c in range(DC):
                    last = nc.scalar.activation(delta[:, c, :], ps[:, c, :], ACT.Identity, bias=b_dt[:, c:c + 1])
                last.then_inc(front_scalar.sem, 1)
                act.wait_ge(front_scalar.sem, front_scalar.at(b, "v"))
                nc.scalar.activation(th, delta[:], ACT.Abs).then_inc(front_scalar.sem, 1)
                act.wait_ge(front_scalar.sem, front_scalar.at(b, "abs"))
                nc.scalar.activation(th, th, ACT.Exp, scale=-1.0).then_inc(front_scalar.sem, 1)
                act.wait_ge(front_scalar.sem, front_scalar.at(b, "exp"))
                nc.scalar.activation(th, th, ACT.Ln, bias=1.0).then_inc(front_scalar.sem, 1)

            def scan_step(b, k):
                half, n = divmod(k, NS)
                if k == 0:
                    act.wait_ge(front_vector.sem, front_vector.at(b, "du"))
                if k >= 2:
                    act.wait_ge(scan_vector.sem, scan_vector.at(b, f"scan{k - 2}"))
                for i in range(2):
                    c = 2 * half + i
                    last = nc.scalar.activation(dA[:, k % 2, i, :], delta[:, c, :], ACT.Exp, scale=a_neg[:, c, n:n + 1])
                last.then_inc(scan_scalar.sem, 1)

            def expert_step(m, j):
                act.wait_ge(expert_tensor.sem, expert_tensor.at(m, f"up{j}"))
                if j >= 2:
                    act.wait_ge(expert_vector.sem, expert_vector.at(m, f"a{j - 2}"))
                nc.scalar.activation(m_th[:, j % 2, :], ps[:, 4, :], ACT.Tanh, scale=0.5).then_inc(expert_scalar.sem, 1)

            def route(b):
                act.wait_ge(route_vector.sem, route_vector.at(b, "xc"))
                nc.scalar.activation(sq, mx[:], ACT.Square).then_inc(route_scalar.sem, 1)
                act.wait_ge(route_tensor.sem, route_tensor.at(b, "var"))
                nc.scalar.activation(rstd, ps[:, 5, :], ACT.Sqrt, bias=eps[:, 0:1]).then_inc(route_scalar.sem, 1)
                act.wait_ge(route_tensor.sem, route_tensor.at(b, "gate"))
                nc.scalar.activation(sc[:], ps[:, 4, 0:4 * E], ACT.Exp, scale=-1.0).then_inc(route_scalar.sem, 1)
                act.wait_ge(route_tensor.sem, route_tensor.at(b, "turn"))
                nc.scalar.activation(comb_t[:], ps[0:48, 5, :], ACT.Copy).then_inc(route_scalar.sem, 1)

            def rnd(b, experts):
                front(b)
                for k in range(KSTEP):
                    scan_step(b, k)
                    for j in range(MOE):
                        if experts and expert_at(j) == k:
                            expert_step(b - 1, j)
                route(b)

            act.wait_ge(loaded, LOADS)
            act.wait_ge(setup_vector.sem, setup_vector.at(0, "cap"))
            nc.scalar.activation(a_neg[:], a_neg[:], ACT.Exp).then_inc(setup_scalar.sem, 1)
            act.wait_ge(setup_vector.sem, setup_vector.at(0, "mh"))
            rnd(0, False)
            with act.Fori(1, B) as b:
                rnd(b, True)
            for j in range(MOE):
                expert_step(B - 1, j)

        @block.tensor
        def _(pe):
            def mm(o, w, x, first, last):
                return nc.tensor.matmul(o, w, x, start=first, stop=last)

            def front(b):
                if isinstance(b, int):
                    pe.wait_ge(setup_vector.sem, setup_vector.at(0, "mh"))
                else:
                    pe.wait_ge(scan_vector.sem, scan_vector.at(b - 1, "res"))
                    pe.wait_ge(route_scalar.sem, route_scalar.at(b - 1, "comb_t"))
                if not isinstance(b, int):
                    pe.wait_ge(x_loaded, b * 16 + 32)
                for o in range(HC):
                    for k in range(XC):
                        last = mm(ps[:, o, :], tok_w[:, k, o * P:(o + 1) * P], x_in[:, k, :], k == 0, k == XC - 1)
                last.then_inc(front_tensor.sem, 1)
                pe.wait_ge(front_scalar.sem, front_scalar.at(b, "h"))
                for c in range(HC):
                    last = mm(ps[:, 2, :], means[:], hT[:, c, tok_cols(b)], c == 0, c == HC - 1)
                last.then_inc(front_tensor.sem, 1)
                pe.wait_ge(front_scalar.sem, front_scalar.at(b, "sq"))
                for c in range(HC):
                    last = mm(ps[:, 3, :], means[:], sq[:, c, :], c == 0, c == HC - 1)
                last.then_inc(front_tensor.sem, 1)
                pe.wait_ge(front_vector.sem, front_vector.at(b, "xn"))
                for o in range(2 * DC):
                    bank = 4 + o if o < DC else o - DC
                    for c in range(HC):
                        last = mm(ps[:, bank, :], w_in[:, c, o * P:(o + 1) * P], xc[:, c, :], c == 0, c == HC - 1)
                    if o % DC == DC - 1:
                        last.then_inc(front_tensor.sem, 1)
                pe.wait_ge(front_vector.sem, front_vector.at(b, "u"))
                for c in range(DC):
                    last = mm(ps[0:112, 4, :], w_x[:, c, :], u[:, c, :], c == 0, c == DC - 1)
                last.then_inc(front_tensor.sem, 1)
                pe.wait_ge(front_scalar.sem, front_scalar.at(b, "dtl"))
                for c in range(DC):
                    last = mm(ps[:, c, :], w_dt[96:112, c * P:(c + 1) * P], dtl[96:112, :], True, True)
                last.then_inc(front_tensor.sem, 1)

            def spread(bank, row):
                return mm(ps[:, bank, :], pick_state[:, row, :], bc[:], True, True)

            def scan_step(b, name, k):
                n = k % NS
                if name == "B":
                    if k == 0:
                        pe.wait_ge(front_vector.sem, front_vector.at(b, "bc3"))
                        pe.wait_ge(front_scalar.sem, front_scalar.at(b, "ln"))
                    else:
                        pe.wait_ge(scan_vector.sem, scan_vector.at(b, f"dBu{k - 1}"))
                    spread(2, n).then_inc(scan_tensor.sem, 1)
                if name == "C":
                    if k:
                        pe.wait_ge(scan_vector.sem, scan_vector.at(b, f"hC{k - 1}"))
                    spread(3, NS + n).then_inc(scan_tensor.sem, 1)
                if name == "Y":
                    pe.wait_ge(scan_vector.sem, scan_vector.at(b, f"hC{k}"))
                    if k == NS:
                        pe.wait_ge(scan_vector.sem, scan_vector.at(b, "skip0"))
                    for i in range(2):
                        last = mm(ps[:, i, :], ident[:], hC[:, k % 2, i, :], n == 0, n == NS - 1)
                    last.then_inc(scan_tensor.sem, 1)

            def expert_up(m, j):
                if j:
                    pe.wait_ge(expert_vector.sem, expert_vector.at(m, f"a{j - 1}"))
                else:
                    pe.wait_ge(route_scalar.sem, route_scalar.at(m, "comb_t"))
                w = up_w if j < E else sup_w
                at = (j if j < E else j - E) * P
                for c in range(HC):
                    last = mm(ps[:, 4, :], w[:, c, at:at + P], mx[:, c, :], c == 0, c == HC - 1)
                last.then_inc(expert_tensor.sem, 1)
                if j < E:
                    if j:
                        pe.wait_ge(expert_vector.sem, expert_vector.at(m, f"c{j - 1}"))
                    mm(ps[:, 5, :], pick_expert[:, j, :], comb_t[:], True, True).then_inc(expert_tensor.sem, 1)

            def expert_down(m, j):
                pe.wait_ge(expert_vector.sem, expert_vector.at(m, f"c{j}" if j < E else f"a{j}"))
                for o in range(HC):
                    w = down_w[:, j, o * P:(o + 1) * P] if j < E else sdown_w[:, j - E, o * P:(o + 1) * P]
                    last = mm(ps[:, 6 + o, :], w, m_act[:, j % 2, :], j == 0, j == MOE - 1)
                last.then_inc(expert_tensor.sem, 1)

            def route(b):
                pe.wait_ge(scan_vector.sem, scan_vector.at(b, "res"))
                for c in range(HC):
                    last = mm(ps[:, 4, :], means[:], hT[:, c, tok_cols(b)], c == 0, c == HC - 1)
                last.then_inc(route_tensor.sem, 1)
                pe.wait_ge(route_scalar.sem, route_scalar.at(b, "sq"))
                for c in range(HC):
                    last = mm(ps[:, 5, :], means[:], sq[:, c, :], c == 0, c == HC - 1)
                last.then_inc(route_tensor.sem, 1)
                pe.wait_ge(route_vector.sem, route_vector.at(b, "xn"))
                for t in range(4):
                    for c in range(HC):
                        last = mm(ps[:, 4, t * E:(t + 1) * E], mx[:, c, t * P:(t + 1) * P], gate_w[:, c, :],
                                  c == 0, c == HC - 1)
                last.then_inc(route_tensor.sem, 1)
                pe.wait_ge(route_vector.sem, route_vector.at(b, "k3"))
                for t in range(4):
                    last = mm(ps[:, 5, t * P:(t + 1) * P], comb_p[:, t, :, :].rearrange("p a b -> p (a b)"), identb[:],
                              True, True)
                last.then_inc(route_tensor.sem, 1)

            def rnd(b, experts):
                front(b)
                for k in range(-1, KSTEP + 1):
                    for name, at in step_parts(k):
                        scan_step(b, name, at)
                    for j in range(MOE + 1):
                        if experts and expert_at(j) == k:
                            if j < MOE:
                                expert_up(b - 1, j)
                            if j:
                                expert_down(b - 1, j - 1)
                pe.wait_ge(scan_vector.sem, scan_vector.at(b, "gated1"))
                for o in range(HC):
                    for c in range(DC):
                        last = mm(ps[:, 2 + o, :], w_out[:, c, o * P:(o + 1) * P], y[:, c, :], c == 0, c == DC - 1)
                last.then_inc(scan_tensor.sem, 1)
                if experts:
                    pe.wait_ge(expert_vector.sem, expert_vector.at(b - 1, "res"))
                route(b)

            pe.wait_ge(loaded, LOADS)
            rnd(0, False)
            with pe.Fori(1, B) as b:
                rnd(b, True)
            for j in range(MOE + 1):
                if j < MOE:
                    expert_up(B - 1, j)
                if j:
                    expert_down(B - 1, j - 1)

        @block.vector
        def _(dve):
            V = nc.vector

            def front(b):
                if not isinstance(b, int):
                    dve.wait_ge(route_tensor.sem, route_tensor.at(b - 1, "turn"))
                dve.wait_ge(front_tensor.sem, front_tensor.at(b, "mean"))
                V.memset(xpad[:, :, 0:TAPS - 1], 0.0).then_inc(front_vector.sem, 1)
                V.tensor_tensor(xc, hT[:, :, tok_cols(b)], ps[:, 2:3, :].to_broadcast([P, HC, S]), ALU.subtract).then_inc(front_vector.sem, 1)
                dve.wait_ge(front_scalar.sem, front_scalar.at(b, "std"))
                V.reciprocal(rstd, rstd).then_inc(front_vector.sem, 1)
                dve.wait_ge(front_vector.sem, front_vector.at(b, "rstd"))
                V.tensor_tensor(xc, xc, rstd.rearrange("p (a b) -> p a b", a=1).to_broadcast([P, HC, S]), ALU.mult).then_inc(front_vector.sem, 1)
                dve.wait_ge(front_scalar.sem, front_scalar.at(b, "xpad"))
                for j in range(TAPS):
                    tap = TAPS - 1 - j
                    if j:
                        dve.wait_ge(front_vector.sem, front_vector.at(b, f"conv{j - 1}"))
                    for c in range(DC):
                        x = xpad[:, c, tap:tap + S]
                        w = taps[:, c, tap:tap + 1]
                        if j == 0:
                            last = V.tensor_scalar(u[:, c, :], x, w, tap_b[:, c:c + 1], ALU.mult, ALU.add)
                        else:
                            last = V.scalar_tensor_tensor(u[:, c, :], x, w, u[:, c, :], ALU.mult, ALU.add)
                    last.then_inc(front_vector.sem, 1)
                dve.wait_ge(front_scalar.sem, front_scalar.at(b, "thz"))
                V.scalar_tensor_tensor(zg[:], th, 1.0, ps[:, 0:4, :], ALU.add, ALU.mult).then_inc(front_vector.sem, 1)
                dve.wait_ge(front_scalar.sem, front_scalar.at(b, "thu"))
                V.scalar_tensor_tensor(u[:], th, 1.0, u[:], ALU.add, ALU.mult).then_inc(front_vector.sem, 1)
                dve.wait_ge(front_tensor.sem, front_tensor.at(b, "bcdt"))
                V.tensor_copy(bc[:], ps[0:96, 4, :]).then_inc(front_vector.sem, 1)
                dve.wait_ge(front_vector.sem, front_vector.at(b, "bc1"))
                V.tensor_tensor(r_bc[0:96, :], ps[0:96, 4, :], bc[:], ALU.subtract).then_inc(front_vector.sem, 1)
                dve.wait_ge(front_vector.sem, front_vector.at(b, "r1"))
                V.tensor_copy(bc[32:64, :], r_bc[32:64, :])
                V.tensor_copy(bc[64:96, :], r_bc[64:96, :]).then_inc(front_vector.sem, 1)
                dve.wait_ge(front_vector.sem, front_vector.at(b, "bc2"))
                V.tensor_tensor(r_bc[64:96, :], r_bc[64:96, :], bc[64:96, :], ALU.subtract).then_inc(front_vector.sem, 1)
                dve.wait_ge(front_vector.sem, front_vector.at(b, "r2"))
                V.tensor_copy(bc[64:96, :], r_bc[64:96, :]).then_inc(front_vector.sem, 1)
                dve.wait_ge(front_scalar.sem, front_scalar.at(b, "ln"))
                V.scalar_tensor_tensor(delta[:], delta[:], 0.0, th, ALU.max, ALU.add).then_inc(front_vector.sem, 1)
                dve.wait_ge(front_vector.sem, front_vector.at(b, "delta"))
                V.tensor_tensor(du[:], delta[:], u[:], ALU.mult).then_inc(front_vector.sem, 1)

            def scan_first(b, k):
                half = k // NS
                dve.wait_ge(scan_tensor.sem, scan_tensor.at(b, f"B{k}"))
                if k == 0:
                    dve.wait_ge(front_vector.sem, front_vector.at(b, "du"))
                V.tensor_tensor(dBu, du[:, 2 * half:2 * half + 2, :], ps[:, 2:3, :].to_broadcast([P, 2, S]), ALU.mult)\
                    .then_inc(scan_vector.sem, 1)
                dve.wait_ge(scan_scalar.sem, scan_scalar.at(b, f"dA{k}"))
                dve.wait_ge(scan_vector.sem, scan_vector.at(b, f"dBu{k}"))
                for i in range(2):
                    last = V.tensor_tensor_scan(hs[:, i, :], dA[:, k % 2, i, :], dBu[:, i, :], 0.0, ALU.mult, ALU.add)
                last.then_inc(scan_vector.sem, 1)

            def scan_second(b, k):
                dve.wait_ge(scan_tensor.sem, scan_tensor.at(b, f"C{k}"))
                dve.wait_ge(scan_vector.sem, scan_vector.at(b, f"scan{k}"))
                if k >= 2:
                    dve.wait_ge(scan_tensor.sem, scan_tensor.at(b, f"Y{k - 2}"))
                V.tensor_tensor(hC[:, k % 2], hs, ps[:, 3:4, :].to_broadcast([P, 2, S]), ALU.mult).then_inc(scan_vector.sem, 1)

            def scan_end(b, half):
                dve.wait_ge(scan_tensor.sem, scan_tensor.at(b, f"Y{NS * half + NS - 1}"))
                for i in range(2):
                    c = 2 * half + i
                    last = V.scalar_tensor_tensor(y[:, c, :], u[:, c, :], d_skip[:, c:c + 1], ps[:, i, :], ALU.mult, ALU.add)
                last.then_inc(scan_vector.sem, 1)
                dve.wait_ge(scan_vector.sem, scan_vector.at(b, f"skip{half}"))
                pair = slice(2 * half, 2 * half + 2)
                V.tensor_tensor(y[:, pair, :], y[:, pair, :], zg[:, pair, :], ALU.mult).then_inc(scan_vector.sem, 1)

            def expert_step(m, j):
                dve.wait_ge(expert_scalar.sem, expert_scalar.at(m, f"th{j}"))
                if j >= 2:
                    dve.wait_ge(expert_tensor.sem, expert_tensor.at(m, f"dn{j - 2}"))
                V.scalar_tensor_tensor(m_act[:, j % 2, :], m_th[:, j % 2, :], 1.0, ps[:, 4, :], ALU.add, ALU.mult)\
                    .then_inc(expert_vector.sem, 1)
                if j < E:
                    dve.wait_ge(expert_tensor.sem, expert_tensor.at(m, f"cb{j}"))
                    dve.wait_ge(expert_vector.sem, expert_vector.at(m, f"a{j}"))
                    V.tensor_tensor(m_act[:, j % 2, :], m_act[:, j % 2, :], ps[:, 5, :], ALU.mult).then_inc(expert_vector.sem, 1)

            def expert_end(m):
                dve.wait_ge(expert_tensor.sem, expert_tensor.at(m, f"dn{MOE - 1}"))
                V.scalar_tensor_tensor(hT[:, :, tok_cols(m)], ps[:, 6:8, :], 0.5, hT[:, :, tok_cols(m)], ALU.mult, ALU.add)\
                    .then_inc(expert_vector.sem, 1)

            def route(b):
                def step(ins, name):
                    ins.then_inc(route_vector.sem, 1)
                    dve.wait_ge(route_vector.sem, route_vector.at(b, name))

                dve.wait_ge(route_tensor.sem, route_tensor.at(b, "mean"))
                V.tensor_tensor(mx[:], hT[:, :, tok_cols(b)], ps[:, 4:5, :].to_broadcast([P, HC, S]), ALU.subtract).then_inc(route_vector.sem, 1)
                dve.wait_ge(route_scalar.sem, route_scalar.at(b, "std"))
                V.reciprocal(rstd, rstd).then_inc(route_vector.sem, 1)
                dve.wait_ge(route_vector.sem, route_vector.at(b, "rstd"))
                V.tensor_tensor(mx[:], mx[:], rstd.rearrange("p (a b) -> p a b", a=1).to_broadcast([P, HC, S]), ALU.mult).then_inc(route_vector.sem, 1)
                dve.wait_ge(route_scalar.sem, route_scalar.at(b, "e"))
                step(V.tensor_scalar(sc[:], sc[:], 1.0, None, ALU.add), "s1")
                step(V.reciprocal(sc[:], sc[:]), "s")
                s4 = sc[:].rearrange("p (g e) -> p g e", e=E // NG)
                w = 0
                for i in range(4):
                    for j in range(i + 1, 4):
                        V.tensor_tensor(pairs[:, w, :], s4[:, :, i], s4[:, :, j], ALU.add).then_inc(route_vector.sem, 1)
                        w += 1
                dve.wait_ge(route_vector.sem, route_vector.at(b, "p5"))
                step(V.tensor_reduce(gsum, pairs.rearrange("p w g -> p g w"), AX.X, ALU.max), "gs")
                gt = gsum.rearrange("p (t g) -> p t g", t=4)
                gg, ge = (v.rearrange("p t (i j) -> p t i j", i=NG) for v in (g_gt, g_eq))
                mine = gsum.rearrange("p (q o) -> p q o", o=1).to_broadcast([P, 4 * NG, NG])
                for t in range(4):
                    own = gt[:, t, :].rearrange("p (i o) -> p i o", o=1).to_broadcast([P, NG, NG])
                    other = gt[:, t, :].rearrange("p (o j) -> p o j", o=1).to_broadcast([P, NG, NG])
                    last = V.tensor_tensor(gg[:, t], other, own, ALU.is_gt)
                last.then_inc(route_vector.sem, 1)
                for t in range(4):
                    own = gt[:, t, :].rearrange("p (i o) -> p i o", o=1).to_broadcast([P, NG, NG])
                    other = gt[:, t, :].rearrange("p (o j) -> p o j", o=1).to_broadcast([P, NG, NG])
                    last = V.tensor_tensor(ge[:, t], other, own, ALU.is_equal)
                step(last, "geq")
                for t in range(4):
                    last = V.tensor_tensor(ge[:, t], ge[:, t], lower[:, 0:NG, 0:NG], ALU.mult)
                step(last, "geql")
                step(V.tensor_tensor(g_gt, g_gt, g_eq, ALU.add), "gsumr")
                step(V.tensor_reduce(grank, g_gt.rearrange("p t (i j) -> p (t i) j", j=NG), AX.X, ALU.add), "gr")
                step(V.tensor_scalar(grank, grank, 1.5, None, ALU.is_lt), "gm")
                step(V.tensor_tensor(masked.rearrange("p (g e) -> p g e", e=E // NG), s4,
                                     grank.rearrange("p (g o) -> p g o", o=1).to_broadcast([P, 4 * NG, E // NG]), ALU.mult), "msk")
                mt = masked.rearrange("p (t e) -> p t e", t=4)
                cg, ce = (v.rearrange("p t (i j) -> p t i j", i=E) for v in (c_gt, c_eq))
                for t in range(4):
                    own = mt[:, t, :].rearrange("p (i o) -> p i o", o=1).to_broadcast([P, E, E])
                    other = mt[:, t, :].rearrange("p (o j) -> p o j", o=1).to_broadcast([P, E, E])
                    last = V.tensor_tensor(cg[:, t], other, own, ALU.is_gt)
                last.then_inc(route_vector.sem, 1)
                for t in range(4):
                    own = mt[:, t, :].rearrange("p (i o) -> p i o", o=1).to_broadcast([P, E, E])
                    other = mt[:, t, :].rearrange("p (o j) -> p o j", o=1).to_broadcast([P, E, E])
                    last = V.tensor_tensor(ce[:, t], other, own, ALU.is_equal)
                step(last, "ceq")
                for t in range(4):
                    last = V.tensor_tensor(ce[:, t], ce[:, t], lower[:], ALU.mult)
                step(last, "ceql")
                step(V.tensor_tensor(c_gt, c_gt, c_eq, ALU.add), "csum")
                step(V.tensor_reduce(rank, c_gt.rearrange("p t (i j) -> p (t i) j", j=E), AX.X, ALU.add), "cr")
                step(V.scalar_tensor_tensor(masked, rank, TOPK - 0.5, sc[:], ALU.is_lt, ALU.mult), "w")
                step(V.tensor_reduce(wsum, mt, AX.X, ALU.add), "ws")
                step(V.tensor_scalar(wsum, wsum, 1e-20, None, ALU.add), "wr")
                step(V.reciprocal(wsum, wsum), "rcp")
                step(V.scalar_tensor_tensor(comb[:], mt, 2.5, wsum.rearrange("p (t o) -> p t o", o=1).to_broadcast([P, 4, E]),
                                            ALU.mult, ALU.mult), "comb")
                left = wres.rearrange("p (t e) -> p t e", t=4)
                step(V.tensor_copy(comb_p[:, :, 0, :], comb[:]), "k1")
                step(V.tensor_tensor(left, comb[:], comb_p[:, :, 0, :], ALU.subtract), "q1")
                step(V.tensor_copy(comb_p[:, :, 1, :], left), "k2")
                step(V.tensor_tensor(left, left, comb_p[:, :, 1, :], ALU.subtract), "q2")
                V.tensor_copy(comb_p[:, :, 2, :], left).then_inc(route_vector.sem, 1)

            def rnd(b, experts):
                front(b)
                for k in range(KSTEP):
                    scan_first(b, k)
                    for j in range(MOE):
                        if experts and expert_at(j) == k:
                            expert_step(b - 1, j)
                    scan_second(b, k)
                    if k % NS == NS - 1:
                        scan_end(b, k // NS)
                if experts:
                    expert_end(b - 1)
                dve.wait_ge(scan_tensor.sem, scan_tensor.at(b, "proj"))
                V.scalar_tensor_tensor(hT[:, :, tok_cols(b)], ps[:, 2:4, :], 0.5, hT[:, :, tok_cols(b)], ALU.mult, ALU.add)\
                    .then_inc(scan_vector.sem, 1)
                route(b)

            dve.wait_ge(loaded, LOADS)
            for d in range(TOKD):
                for c in range(HC):
                    V.tensor_tensor(tok_w[:, d * HC + c, :], ws_t[:, c, :], v_rep[:, d, :], ALU.mult).then_inc(setup_vector.sem, 1)
            V.tensor_scalar(taps[:], taps[:], 0.5, None, ALU.mult).then_inc(setup_vector.sem, 1)
            V.tensor_scalar(tap_b[:], tap_b[:], 0.5, None, ALU.mult).then_inc(setup_vector.sem, 1)
            V.tensor_scalar(a_neg[:], a_neg[:], 80.0, None, ALU.min).then_inc(setup_vector.sem, 1)
            dve.wait_ge(setup_scalar.sem, setup_scalar.at(0, "aexp"))
            V.tensor_scalar(a_neg[:], a_neg[:], -1.0, None, ALU.mult).then_inc(setup_vector.sem, 1)
            V.tensor_copy(identb[:], ident[:]).then_inc(setup_vector.sem, 1)
            dve.wait_ge(x_loaded, 32)
            V.tensor_copy(pick_state[:].rearrange("p a b -> p (a b)"),
                          hT[0:96, :, :].rearrange("p a b -> p (a b)")[:, 0:2 * NS * P]).then_inc(setup_vector.sem, 1)
            V.tensor_copy(pick_expert[:].rearrange("p a b -> p (a b)"), u[0:48, :, :].rearrange("p a b -> p (a b)"))\
                .then_inc(setup_vector.sem, 1)
            V.memset(comb_p[:], 0.0).then_inc(setup_vector.sem, 1)
            dve.wait_ge(setup_vector.sem, setup_vector.at(0, "mh"))
            rnd(0, False)
            with dve.Fori(1, B) as b:
                rnd(b, True)
            for j in range(MOE):
                expert_step(B - 1, j)
            expert_end(B - 1)


def expert_at(j):
    return (j * 3) // 2


def step_parts(k):
    parts = []
    if 0 <= k < KSTEP:
        parts.append(("C", k))
    if 1 <= k <= KSTEP:
        parts.append(("Y", k - 1))
    if -1 <= k < KSTEP - 1:
        parts.append(("B", k + 1))
    return parts


def scan_tensor_order():
    return [f"{name}{at}" for k in range(-1, KSTEP + 1) for name, at in step_parts(k)]


def scan_vector_order():
    names = []
    for k in range(KSTEP):
        names += [f"dBu{k}", f"scan{k}", f"hC{k}"]
        if k % NS == NS - 1:
            names += [f"skip{k // NS}", f"gated{k // NS}"]
    return names


def attention(nc, ctx, a, hT, ident, means, eps, ps):
    T, NH, D = B, 16, H // 16
    ROWS = 2 * T - 1
    PAIRS = T * HC

    def sb(name, shape, dt=F32):
        return ctx.enter_context(nc.sbuf_tensor(name, shape, dt))

    def sem(name):
        return ctx.enter_context(nc.semaphore(name))

    qkv_w = sb("qkv_w", [P, HC, 3 * H])
    pos_w = sb("pos_w", [P, HC, H])
    o_w = sb("o_w", [P, HC, H])
    pos_t = sb("pos_t", [P, HC, ROWS])
    qkv_b = sb("qkv_b", [P, 3 * HC])
    pos_b = sb("pos_b", [P, HC])
    o_b = sb("o_b", [P, HC])
    r_w = sb("r_w", [P, HC])
    r_r = sb("r_r", [P, HC])
    heads = sb("heads", [P, PAIRS, P])
    unheads = sb("unheads", [P, PAIRS, P])
    qkv = sb("qkv", [P, 3 * HC, B * S])
    p_row = sb("p_row", [P, HC, ROWS])
    p_gap = sb("p_gap", [P, HC, ROWS])
    gap = sb("gap", [P, T])
    p_t = sb("p_t", [P, HC, T])
    xc = sb("xc_a", [P, HC, S])
    sq = sb("sq_a", [P, HC, S])
    rstd = sb("rstd_a", [P, S])
    prod = sb("prod", [P, 3, S])
    s_row = sb("s_row", [P, S])
    s_tok = sb("s_tok", [P, 4, P])
    peak = sb("peak", [P, 4, NH])
    total = sb("total", [P, 4, NH])
    w_row = sb("w_row", [P, S])
    part = sb("part", [P, 2, S])
    mix = sb("mix", [P, HC, S])
    SCALE = float(D) ** -0.5

    loaded = sem("loaded_a")
    pos_tensor = Steps(sem("pos_tensor"), ["p", "gap"])
    pos_scalar = Steps(sem("pos_scalar"), ["p"])
    pos_vector = Steps(sem("pos_vector"), ["bq", "gap_w", "p_gap", "gap"])
    qkv_tensor = Steps(sem("qkv_tensor"), ["mean", "var", "qkv"])
    qkv_scalar = Steps(sem("qkv_scalar"), ["sq", "std", "qkv"])
    qkv_vector = Steps(sem("qkv_vector"), ["xc", "rstd", "xn"])
    score_tensor = Steps(sem("score_tensor"), [f"s{i}" for i in range(PAIRS)] + ["turn", "back"])
    score_scalar = Steps(sem("score_scalar"), ["s", "exp", "w"])
    score_vector = Steps(sem("score_vector"), ["rows"] + [f"prod{i}" for i in range(PAIRS)] + ["max", "sub", "sum", "rcp", "w"])
    mix_tensor = Steps(sem("mix_tensor"), [f"w{i}" for i in range(PAIRS)] + ["out"])
    mix_vector = Steps(sem("mix_vector"), [n for i in range(PAIRS) for n in ([f"m{i}"] + ([f"a{i}"] if i >= HC else []))] + ["res"])
    LOADS = 16 * 11

    with nc.Block() as block:
        @block.sync
        def _(sp):
            for dst, src in (
                (qkv_w[:], a["qkv_w"].rearrange("(c p) o -> p c o", p=P)),
                (pos_w[:], a["pos_w"].rearrange("(c p) o -> p c o", p=P)),
                (o_w[:], a["o_w"].rearrange("(c p) o -> p c o", p=P)),
                (pos_t[:], a["pos_t"].rearrange("(c p) o -> p c o", p=P)),
                (qkv_b[:], a["qkv_b"]), (pos_b[:], a["pos_b"]), (o_b[:], a["o_b"]), (r_w[:], a["r_w"]), (r_r[:], a["r_r"]),
                (heads[:], a["heads"]), (unheads[:], a["unheads"]),
            ):
                sp.dma_start(dst, src).then_inc(loaded, 16)

        @block.tensor
        def _(pe):
            def mm(o, w, x, first, last):
                return nc.tensor.matmul(o, w, x, start=first, stop=last)

            def scores(t):
                for i in range(PAIRS):
                    pe.wait_ge(score_vector.sem, score_vector.at(t, f"prod{i}"))
                    mm(ps[:, 0, :], heads[:, i, :], prod[:, i % 3, :], i == 0, i == PAIRS - 1).then_inc(score_tensor.sem, 1)

            def softmax(t):
                pe.wait_ge(score_scalar.sem, score_scalar.at(t, "s"))
                for n in range(4):
                    last = nc.tensor.transpose(ps[:, 1, n * P:(n + 1) * P], s_row[:, n * P:(n + 1) * P], ident[:])
                last.then_inc(score_tensor.sem, 1)
                pe.wait_ge(score_vector.sem, score_vector.at(t, "w"))
                for n in range(4):
                    last = nc.tensor.transpose(ps[:, 2, n * P:(n + 1) * P], s_tok[:, n, :], ident[:])
                last.then_inc(score_tensor.sem, 1)

            def mixing(t):
                pe.wait_ge(score_scalar.sem, score_scalar.at(t, "w"))
                for i in range(PAIRS):
                    if i >= 3:
                        pe.wait_ge(mix_vector.sem, mix_vector.at(t, f"m{i - 3}"))
                    mm(ps[:, 3 + i % 3, :], unheads[:, i, :], w_row[:], True, True).then_inc(mix_tensor.sem, 1)
                pe.wait_ge(mix_vector.sem, mix_vector.at(t, f"a{PAIRS - 1}"))
                for o in range(HC):
                    for c in range(HC):
                        last = mm(ps[:, 6 + o, :], o_w[:, c, o * P:(o + 1) * P], mix[:, c, :], c == 0, c == HC - 1)
                last.then_inc(mix_tensor.sem, 1)

            pe.wait_ge(loaded, LOADS)
            for o in range(HC):
                for c in range(HC):
                    last = mm(ps[:, o, 0:ROWS], pos_w[:, c, o * P:(o + 1) * P], pos_t[:, c, :], c == 0, c == HC - 1)
            last.then_inc(pos_tensor.sem, 1)
            pe.wait_ge(pos_vector.sem, pos_vector.at(0, "p_gap"))
            for i in range(PAIRS):
                s, c = divmod(i, HC)
                last = mm(ps[:, 2, 0:T], heads[:, i, :], p_gap[:, c, s:s + T], i == 0, i == PAIRS - 1)
            last.then_inc(pos_tensor.sem, 1)

            def project(t):
                for c in range(HC):
                    last = mm(ps[:, 0, :], means[:], hT[:, c, tok_cols(t)], c == 0, c == HC - 1)
                last.then_inc(qkv_tensor.sem, 1)
                pe.wait_ge(qkv_scalar.sem, qkv_scalar.at(t, "sq"))
                for c in range(HC):
                    last = mm(ps[:, 1, :], means[:], sq[:, c, :], c == 0, c == HC - 1)
                last.then_inc(qkv_tensor.sem, 1)
                pe.wait_ge(qkv_vector.sem, qkv_vector.at(t, "xn"))
                if not isinstance(t, int):
                    pe.wait_ge(qkv_scalar.sem, qkv_scalar.at(t - 1, "qkv"))
                for o in range(3 * HC):
                    for c in range(HC):
                        last = mm(ps[:, 2 + o, :], qkv_w[:, c, o * P:(o + 1) * P], xc[:, c, :], c == 0, c == HC - 1)
                last.then_inc(qkv_tensor.sem, 1)

            pe.wait_ge(pos_vector.sem, pos_vector.at(0, "gap"))
            project(0)
            with pe.Fori(1, T) as t:
                project(t)
            pe.wait_ge(qkv_scalar.sem, qkv_scalar.at(T - 1, "qkv"))
            scores(0)
            softmax(0)
            with pe.Fori(1, T) as t:
                scores(t)
                mixing(t - 1)
                softmax(t)
            mixing(T - 1)

        @block.scalar
        def _(act):
            act.wait_ge(loaded, LOADS)
            act.wait_ge(pos_tensor.sem, pos_tensor.at(0, "p"))
            for o in range(HC):
                last = nc.scalar.activation(p_row[:, o, :], ps[:, o, 0:ROWS], ACT.Identity, bias=pos_b[:, o:o + 1])
            last.then_inc(pos_scalar.sem, 1)
            act.wait_ge(pos_vector.sem, pos_vector.at(0, "bq"))
            with act.Fori(0, T) as t:
                act.wait_ge(qkv_vector.sem, qkv_vector.at(t, "xc"))
                nc.scalar.activation(sq[:], xc[:], ACT.Square).then_inc(qkv_scalar.sem, 1)
                act.wait_ge(qkv_tensor.sem, qkv_tensor.at(t, "var"))
                nc.scalar.activation(rstd[:], ps[:, 1, :], ACT.Sqrt, bias=eps[:, 0:1]).then_inc(qkv_scalar.sem, 1)
                act.wait_ge(qkv_tensor.sem, qkv_tensor.at(t, "qkv"))
                for o in range(3 * HC):
                    last = nc.scalar.activation(qkv[:, o, tok_cols(t)], ps[:, 2 + o, :], ACT.Identity, bias=qkv_b[:, o:o + 1])
                last.then_inc(qkv_scalar.sem, 1)
            act.wait_ge(pos_vector.sem, pos_vector.at(0, "gap"))
            with act.Fori(0, T) as t:
                act.wait_ge(score_tensor.sem, score_tensor.at(t, f"s{PAIRS - 1}"))
                nc.scalar.activation(s_row[:], ps[:, 0, :], ACT.Identity, scale=SCALE,
                                     bias=gap[:, bass.ds(T - 1 - t, 1)]).then_inc(score_scalar.sem, 1)
                act.wait_ge(score_vector.sem, score_vector.at(t, "sub"))
                nc.scalar.activation(s_tok[:], s_tok[:], ACT.Exp).then_inc(score_scalar.sem, 1)
                act.wait_ge(score_tensor.sem, score_tensor.at(t, "back"))
                nc.scalar.activation(w_row[:], ps[:, 2, :], ACT.Copy).then_inc(score_scalar.sem, 1)

        @block.vector
        def _(dve):
            V = nc.vector
            dve.wait_ge(loaded, LOADS)
            V.tensor_tensor(qkv_b[:, 0:HC], qkv_b[:, 0:HC], r_w[:], ALU.add).then_inc(pos_vector.sem, 1)
            V.tensor_tensor(r_r[:], r_r[:], r_w[:], ALU.subtract).then_inc(pos_vector.sem, 1)
            dve.wait_ge(pos_vector.sem, pos_vector.at(0, "gap_w"))
            dve.wait_ge(pos_scalar.sem, pos_scalar.at(0, "p"))
            for c in range(HC):
                last = V.tensor_scalar(p_gap[:, c, :], p_row[:, c, :], r_r[:, c:c + 1], None, ALU.mult)
            last.then_inc(pos_vector.sem, 1)
            dve.wait_ge(pos_tensor.sem, pos_tensor.at(0, "gap"))
            V.tensor_scalar(gap[:], ps[:, 2, 0:T], SCALE, None, ALU.mult).then_inc(pos_vector.sem, 1)
            with dve.Fori(0, T) as t:
                dve.wait_ge(qkv_tensor.sem, qkv_tensor.at(t, "mean"))
                V.tensor_tensor(xc[:], hT[:, :, tok_cols(t)], spread_over(ps[:, 0, :], HC), ALU.subtract).then_inc(qkv_vector.sem, 1)
                dve.wait_ge(qkv_scalar.sem, qkv_scalar.at(t, "std"))
                V.reciprocal(rstd[:], rstd[:]).then_inc(qkv_vector.sem, 1)
                dve.wait_ge(qkv_vector.sem, qkv_vector.at(t, "rstd"))
                V.tensor_tensor(xc[:], xc[:], spread_over(rstd[:], HC), ALU.mult).then_inc(qkv_vector.sem, 1)

            def scores(t):
                V.tensor_copy(p_t[:], p_row[:, :, bass.ds(T - 1 - t, T)]).then_inc(score_vector.sem, 1)
                dve.wait_ge(score_vector.sem, score_vector.at(t, "rows"))
                for i in range(PAIRS):
                    s, c = divmod(i, HC)
                    if i >= 3:
                        dve.wait_ge(score_tensor.sem, score_tensor.at(t, f"s{i - 3}"))
                    V.scalar_tensor_tensor(prod[:, i % 3, :], qkv[:, HC + c, tok_cols(s)], p_t[:, c, s:s + 1],
                                           qkv[:, c, tok_cols(t)], ALU.add, ALU.mult).then_inc(score_vector.sem, 1)

            def softmax(t):
                dve.wait_ge(score_tensor.sem, score_tensor.at(t, "turn"))
                by_head = ps[:, 1, :].rearrange("p (n s h) -> p n h s", n=4, s=T)
                V.tensor_reduce(peak[:], by_head, AX.X, ALU.max).then_inc(score_vector.sem, 1)
                dve.wait_ge(score_vector.sem, score_vector.at(t, "max"))
                for n in range(4):
                    last = V.tensor_tensor(s_tok[:, n, :].rearrange("p (s h) -> p s h", s=T),
                                           ps[:, 1, n * P:(n + 1) * P].rearrange("p (s h) -> p s h", s=T),
                                           peak[:, n:n + 1, :].to_broadcast([P, T, NH]), ALU.subtract)
                last.then_inc(score_vector.sem, 1)
                dve.wait_ge(score_scalar.sem, score_scalar.at(t, "exp"))
                V.tensor_reduce(total[:], s_tok[:].rearrange("p n (s h) -> p n h s", s=T), AX.X, ALU.add).then_inc(score_vector.sem, 1)
                dve.wait_ge(score_vector.sem, score_vector.at(t, "sum"))
                V.reciprocal(total[:], total[:]).then_inc(score_vector.sem, 1)
                dve.wait_ge(score_vector.sem, score_vector.at(t, "rcp"))
                for n in range(4):
                    v = s_tok[:, n, :].rearrange("p (s h) -> p s h", s=T)
                    last = V.tensor_tensor(v, v, total[:, n:n + 1, :].to_broadcast([P, T, NH]), ALU.mult)
                last.then_inc(score_vector.sem, 1)

            def mixing(t):
                for i in range(PAIRS):
                    s, c = divmod(i, HC)
                    dve.wait_ge(mix_tensor.sem, mix_tensor.at(t, f"w{i}"))
                    dst = mix[:, c, :] if s == 0 else part[:, i % 2, :]
                    V.tensor_tensor(dst, qkv[:, 2 * HC + c, tok_cols(s)], ps[:, 3 + i % 3, :], ALU.mult).then_inc(mix_vector.sem, 1)
                    if s:
                        dve.wait_ge(mix_vector.sem, mix_vector.at(t, f"m{i}"))
                        V.tensor_tensor(mix[:, c, :], mix[:, c, :], part[:, i % 2, :], ALU.add).then_inc(mix_vector.sem, 1)
                dve.wait_ge(mix_tensor.sem, mix_tensor.at(t, "out"))
                for c in range(HC):
                    last = V.scalar_tensor_tensor(hT[:, c, tok_cols(t)], ps[:, 6 + c, :], o_b[:, c:c + 1],
                                                  hT[:, c, tok_cols(t)], ALU.add, ALU.add)
                last.then_inc(mix_vector.sem, 1)

            dve.wait_ge(qkv_scalar.sem, qkv_scalar.at(T - 1, "qkv"))
            scores(0)
            softmax(0)
            with dve.Fori(1, T) as t:
                scores(t)
                mixing(t - 1)
                softmax(t)
            mixing(T - 1)


def modulated_ffn(nc, ctx, a, out, hT, means, eps, ps):
    E, F, J = 8, 1024, 16
    FC = F // P
    COLS = H * F // J
    PIECE = 4 * 512
    NP = COLS // PIECE
    PIECES = 2 * NP

    def sb(name, shape, dt=F32):
        return ctx.enter_context(nc.sbuf_tensor(name, shape, dt))

    def sem(name):
        return ctx.enter_context(nc.semaphore(name))

    g1_w = sb("g1_w", [P, HC, H])
    g1_b = sb("g1_b", [P, HC])
    g2_rep = sb("g2_rep", [P, HC, P])
    g2_rep_b = sb("g2_rep_b", [P, 1])
    g2_w = sb("g2_w", [P, HC, E])
    g2_b = sb("g2_b", [E, 1])
    same = sb("same", [P, B, J])
    base = sb("base", [J, P])
    tb1 = sb("tb1", [E, F])
    tb2 = sb("tb2", [E, H])
    b1 = sb("b1", [P, FC])
    b2 = sb("b2", [P, HC])
    msum = sb("msum", [P, HC, B])
    g_rep = sb("g_rep", [P, B])
    g_e = sb("g_e", [E, B])
    kron = sb("kron", [P, B, J])
    mb = sb("mb", [P, FC + HC, B])
    xn = sb("xn_f", [P, HC, B * S])
    sq = sb("sq_f", [P, HC, S])
    rstd = sb("rstd_f", [P, S])
    tw = sb("tw", [P, 2, PIECE])
    w_base = sb("w_base", [J, 2, PIECE])
    mixed = sb("mixed", [P, 2, PIECE])
    w1 = sb("w1", [P, 2, HC, F])
    w2 = sb("w2", [P, 2, FC, H])
    hid = sb("hid", [P, FC, S])
    res = sb("res", [P, 2, HC, S])
    own_w = [nc.dram_tensor(f"own_w{n}", [P, COLS], F32, kind="Internal").ap() for n in (1, 2)]

    loaded = sem("loaded_f")
    tw_loaded, own_stored, own_loaded, stored = (
        [sem(f"{name}{i}") for i in range(2)] for name in ("tw_loaded", "own_stored", "own_loaded", "stored"))
    norm_tensor = Steps(sem("norm_tensor"), ["mean", "var", "gate"])
    norm_scalar = Steps(sem("norm_scalar"), ["sq", "std", "sum"])
    norm_vector = Steps(sem("norm_vector"), ["xc", "rstd", "xn"])
    gate_tensor = Steps(sem("gate_tensor"), ["g", "b"])
    gate_scalar = Steps(sem("gate_scalar"), ["g"])
    gate_vector = Steps(sem("gate_vector"), ["kron", "mb1", "mb2"])
    weight_tensor = Steps(sem("weight_tensor"), ["w"])
    weight_copied = Steps(sem("weight_copied"), ["w"])
    ffn_tensor = Steps(sem("ffn_tensor"), [n for f in range(FC) for n in [f"up{f}"]] + ["down"])
    ffn_scalar = Steps(sem("ffn_scalar"), [f"gelu{f}" for f in range(FC)])
    ffn_vector = Steps(sem("ffn_vector"), ["res"])
    LOADS = 16 * 12

    with nc.Block() as block:
        @block.sync
        def _(sp):
            for dst, src in (
                (g1_w[:], a["g1_w"].rearrange("(c p) o -> p c o", p=P)), (g1_b[:], a["g1_b"]),
                (g2_rep[:], a["g2_rep"].rearrange("(c p) o -> p c o", p=P)), (g2_rep_b[:], a["g2_rep_b"]),
                (g2_w[:], a["g2_w"].rearrange("(c p) o -> p c o", p=P)), (g2_b[:], a["g2_b"]),
                (same[:], a["same"]), (base[:], a["same"][0:J].rearrange("p b j -> p (b j)")),
                (tb1[:], a["tb1"]), (tb2[:], a["tb2"]), (b1[:], a["b1"]), (b2[:], a["b2"]),
            ):
                sp.dma_start(dst, src).then_inc(loaded, 16)
            for n in range(PIECES):
                if n >= 2:
                    sp.wait_ge(weight_tensor.sem, weight_tensor.at(n - 2, "w"))
                cols = slice(n % NP * PIECE, (n % NP + 1) * PIECE)
                sp.dma_start(tw[:, n % 2, :], a["tw1" if n < NP else "tw2"][:, cols]).then_inc(tw_loaded[n % 2], 16)
                sp.dma_start(w_base[:, n % 2, :], a["fw1" if n < NP else "fw2"][:, cols]).then_inc(tw_loaded[n % 2], 16)
            for i in range(2):
                sp.wait_ge(own_stored[i], 16 * PIECES // 2)
            for b in range(B):
                if b >= 2:
                    sp.wait_ge(ffn_tensor.sem, ffn_tensor.at(b - 2, "down"))
                mine = slice(b * J, (b + 1) * J)
                sp.dma_start(w1[:, b % 2], own_w[0][mine, :].rearrange("j (i f) -> (j i) f", f=F)
                             .rearrange("(c p) f -> p c f", p=P)).then_inc(own_loaded[b % 2], 16)
                sp.dma_start(w2[:, b % 2], own_w[1][mine, :].rearrange("j (i h) -> (j i) h", h=H)
                             .rearrange("(c p) h -> p c h", p=P)).then_inc(own_loaded[b % 2], 16)

        @block.gpsimd
        def _(pool):
            for n in range(PIECES):
                cols = slice(n % NP * PIECE, (n % NP + 1) * PIECE)
                pool.wait_ge(weight_copied.sem, weight_copied.at(n, "w"))
                pool.dma_start(own_w[n // NP][:, cols], mixed[:, n % 2, :]).then_inc(own_stored[n % 2], 16)
            for b in range(B):
                pool.wait_ge(ffn_vector.sem, ffn_vector.at(b, "res"))
                pool.dma_start(out[:, :, b * S:(b + 1) * S].rearrange("c p s -> p c s"), res[:, b % 2]).then_inc(stored[b % 2], 16)
            for i in range(2):
                pool.wait_ge(stored[i], 16 * B // 2)

        @block.tensor
        def _(pe):
            def mm(o, w, x, first, last):
                return nc.tensor.matmul(o, w, x, start=first, stop=last)

            pe.wait_ge(loaded, LOADS)

            def norm(b):
                if not isinstance(b, int):
                    pe.wait_ge(norm_vector.sem, norm_vector.at(b - 1, "xc"))
                for c in range(HC):
                    last = mm(ps[:, 0, :], means[:], hT[:, c, tok_cols(b)], c == 0, c == HC - 1)
                last.then_inc(norm_tensor.sem, 1)
                pe.wait_ge(norm_scalar.sem, norm_scalar.at(b, "sq"))
                for c in range(HC):
                    last = mm(ps[:, 1, :], means[:], sq[:, c, :], c == 0, c == HC - 1)
                last.then_inc(norm_tensor.sem, 1)
                pe.wait_ge(norm_vector.sem, norm_vector.at(b, "xn"))
                if not isinstance(b, int):
                    pe.wait_ge(norm_scalar.sem, norm_scalar.at(b - 1, "sum"))
                for o in range(HC):
                    for c in range(HC):
                        last = mm(ps[:, 2 + o, :], g1_w[:, c, o * P:(o + 1) * P], xn[:, c, tok_cols(b)], c == 0, c == HC - 1)
                last.then_inc(norm_tensor.sem, 1)

            norm(0)
            with pe.Fori(1, B) as b:
                norm(b)
            pe.wait_ge(norm_scalar.sem, norm_scalar.at(B - 1, "sum"))
            for c in range(HC):
                mm(ps[:, 0, 0:B], g2_rep[:, c, :], msum[:, c, :], c == 0, c == HC - 1)
            for c in range(HC):
                last = mm(ps[0:E, 1, 0:B], g2_w[:, c, :], msum[:, c, :], c == 0, c == HC - 1)
            last.then_inc(gate_tensor.sem, 1)
            pe.wait_ge(gate_scalar.sem, gate_scalar.at(0, "g"))
            for f in range(FC):
                mm(ps[:, 2, f * B:(f + 1) * B], tb1[:, f * P:(f + 1) * P], g_e[:], True, True)
            for c in range(HC):
                last = mm(ps[:, 3, c * B:(c + 1) * B], tb2[:, c * P:(c + 1) * P], g_e[:], True, True)
            last.then_inc(gate_tensor.sem, 1)
            pe.wait_ge(gate_vector.sem, gate_vector.at(0, "mb2"))
            for n in range(PIECES):
                pe.wait_ge(tw_loaded[n % 2], 32 * (n // 2 + 1))
                if n >= 2:
                    pe.wait_ge(weight_copied.sem, weight_copied.at(n - 2, "w"))
                for i in range(4):
                    cols = slice(i * 512, (i + 1) * 512)
                    bank = 4 * (n % 2) + i
                    mm(ps[:, bank, :], kron[:].rearrange("p b j -> p (b j)"), tw[:, n % 2, cols], True, False)
                    last = mm(ps[:, bank, :], base[:], w_base[:, n % 2, cols], False, True)
                last.then_inc(weight_tensor.sem, 1)
            pe.wait_ge(weight_copied.sem, weight_copied.at(PIECES - 1, "w"))
            for b in range(B):
                pe.wait_ge(own_loaded[b % 2], 32 * (b // 2 + 1))
                for f in range(FC):
                    if f >= 4:
                        pe.wait_ge(ffn_scalar.sem, ffn_scalar.at(b, f"gelu{f - 4}"))
                    elif b:
                        pe.wait_ge(ffn_scalar.sem, ffn_scalar.at(b - 1, f"gelu{f + 4}"))
                    for c in range(HC):
                        last = mm(ps[:, f % 4, :], w1[:, b % 2, c, f * P:(f + 1) * P], xn[:, c, tok_cols(b)], c == 0, c == HC - 1)
                    last.then_inc(ffn_tensor.sem, 1)
                if b >= 2:
                    pe.wait_ge(ffn_vector.sem, ffn_vector.at(b - 2, "res"))
                for f in range(FC):
                    pe.wait_ge(ffn_scalar.sem, ffn_scalar.at(b, f"gelu{f}"))
                    for o in range(HC):
                        last = mm(ps[:, 4 + 2 * (b % 2) + o, :], w2[:, b % 2, f, o * P:(o + 1) * P], hid[:, f, :], f == 0, f == FC - 1)
                last.then_inc(ffn_tensor.sem, 1)

        @block.scalar
        def _(act):
            act.wait_ge(loaded, LOADS)
            with act.Fori(0, B) as b:
                act.wait_ge(norm_vector.sem, norm_vector.at(b, "xc"))
                nc.scalar.activation(sq[:], xn[:, :, tok_cols(b)], ACT.Square).then_inc(norm_scalar.sem, 1)
                act.wait_ge(norm_tensor.sem, norm_tensor.at(b, "var"))
                nc.scalar.activation(rstd[:], ps[:, 1, :], ACT.Sqrt, bias=eps[:, 0:1]).then_inc(norm_scalar.sem, 1)
                act.wait_ge(norm_tensor.sem, norm_tensor.at(b, "gate"))
                act.wait_ge(norm_scalar.sem, norm_scalar.at(b, "std"))
                for o in range(HC):
                    last = nc.scalar.activation(hid[:, o, :], ps[:, 2 + o, :], ACT.Relu, bias=g1_b[:, o:o + 1],
                                                accum_out=msum[:, o, bass.ds(b, 1)])
                last.then_inc(norm_scalar.sem, 1)
            act.wait_ge(gate_tensor.sem, gate_tensor.at(0, "g"))
            nc.scalar.activation(g_rep[:], ps[:, 0, 0:B], ACT.Identity, scale=1.0 / S, bias=g2_rep_b[:, 0:1])
            nc.scalar.activation(g_e[:], ps[0:E, 1, 0:B], ACT.Identity, scale=1.0 / S, bias=g2_b[:, 0:1]).then_inc(gate_scalar.sem, 1)
            for b in range(B):
                if b == 0:
                    act.wait_ge(gate_vector.sem, gate_vector.at(0, "mb2"))
                for f in range(FC):
                    act.wait_ge(ffn_tensor.sem, ffn_tensor.at(b, f"up{f}"))
                    if f == 0 and b:
                        act.wait_ge(ffn_tensor.sem, ffn_tensor.at(b - 1, "down"))
                    nc.scalar.activation(hid[:, f, :], ps[:, f % 4, :], ACT.Gelu_apprx_tanh, bias=mb[:, f, b:b + 1]).then_inc(ffn_scalar.sem, 1)

        @block.vector
        def _(dve):
            V = nc.vector
            dve.wait_ge(loaded, LOADS)
            with dve.Fori(0, B) as b:
                dve.wait_ge(norm_tensor.sem, norm_tensor.at(b, "mean"))
                V.tensor_tensor(xn[:, :, tok_cols(b)], hT[:, :, tok_cols(b)], spread_over(ps[:, 0, :], HC), ALU.subtract).then_inc(norm_vector.sem, 1)
                dve.wait_ge(norm_scalar.sem, norm_scalar.at(b, "std"))
                V.reciprocal(rstd[:], rstd[:]).then_inc(norm_vector.sem, 1)
                dve.wait_ge(norm_vector.sem, norm_vector.at(b, "rstd"))
                V.tensor_tensor(xn[:, :, tok_cols(b)], xn[:, :, tok_cols(b)], spread_over(rstd[:], HC), ALU.mult).then_inc(norm_vector.sem, 1)
            dve.wait_ge(gate_scalar.sem, gate_scalar.at(0, "g"))
            V.tensor_tensor(kron[:], same[:], g_rep[:].rearrange("p (b o) -> p b o", o=1).to_broadcast([P, B, J]), ALU.mult).then_inc(gate_vector.sem, 1)
            dve.wait_ge(gate_tensor.sem, gate_tensor.at(0, "b"))
            V.tensor_tensor(mb[:, 0:FC, :], ps[:, 2, 0:FC * B].rearrange("p (f b) -> p f b", b=B),
                            b1[:].rearrange("p (f o) -> p f o", o=1).to_broadcast([P, FC, B]), ALU.add).then_inc(gate_vector.sem, 1)
            V.tensor_tensor(mb[:, FC:, :], ps[:, 3, 0:HC * B].rearrange("p (f b) -> p f b", b=B),
                            b2[:].rearrange("p (f o) -> p f o", o=1).to_broadcast([P, HC, B]), ALU.add).then_inc(gate_vector.sem, 1)
            for n in range(PIECES):
                dve.wait_ge(weight_tensor.sem, weight_tensor.at(n, "w"))
                if n >= 2:
                    dve.wait_ge(own_stored[n % 2], 16 * (n // 2))
                half = 4 * (n % 2)
                V.tensor_copy(mixed[:, n % 2, :], ps[:, half:half + 4, :].rearrange("p a b -> p (a b)")).then_inc(weight_copied.sem, 1)
            dve.wait_ge(gate_vector.sem, gate_vector.at(0, "mb2"))
            for b in range(B):
                dve.wait_ge(ffn_tensor.sem, ffn_tensor.at(b, "down"))
                if b >= 2:
                    dve.wait_ge(stored[b % 2], 16 * (b // 2))
                for c in range(HC):
                    last = V.scalar_tensor_tensor(res[:, b % 2, c, :], ps[:, 4 + 2 * (b % 2) + c, :], mb[:, FC + c, b:b + 1],
                                                  hT[:, c, tok_cols(b)], ALU.add, ALU.add)
                last.then_inc(ffn_vector.sem, 1)


def lay_out(i):
    f = lambda n: np.asarray(i[n])
    a = {}
    B,S,H,D = f('x').shape
    x = f('x').transpose(0,3,2,1).reshape(B, D*H//P, P, S).transpose(0,2,1,3)
    a['x'] = np.ascontiguousarray(x)
    a['ident'] = np.eye(P, dtype=np.float32)
    a['means'] = np.full((P,P), 1/H, np.float32)
    a['eps'] = np.full((P,1), 1e-5, np.float32)
    a['ws_t'] = f('L0_tok_weighted_sum').T
    a['tok_v'] = f('L0_tok_weight').T
    a['w_in'] = f('L0_attn_W_in'); a['w_out'] = f('L0_attn_W_out')
    wx = f('L0_attn_W_xproj'); bcw = wx[:, 16:]
    a['w_x'] = np.concatenate([bcw, bcw, bcw, wx[:, :16]], 1)
    a['w_dt'] = f('L0_attn_W_dt')
    a['up'] = f('L0_ffn_expert_up').transpose(1,0,2).reshape(H, -1)
    a['down'] = f('L0_ffn_expert_down')
    a['sup'] = f('L0_ffn_shared_up'); a['sdown'] = f('L0_ffn_shared_down')
    a['gate'] = f('L0_ffn_gate_weight').T
    ch = lambda v: np.moveaxis(v.reshape((-1, P) + v.shape[1:]), 0, 1)
    a['taps'] = ch(f('L0_attn_conv_w')[:,0,:]); a['tap_b'] = ch(f('L0_attn_conv_b')); a['b_dt'] = ch(f('L0_attn_b_dt'))
    a['d_skip'] = ch(f('L0_attn_D_skip')); a['a_log'] = ch(f('L0_attn_A_log'))
    E=16
    a['lower'] = np.broadcast_to(np.tril(np.ones((E,E),np.float32), -1), (P,E,E))
    ps = np.zeros((3,32,32,P),np.float32)
    for j in range(32): ps[:,j,j]=1
    a['pick_state'] = ps.reshape(96, 32*P)
    pe = np.zeros((3,16,16,P),np.float32)
    for j in range(16): pe[:,j,j]=1
    a['pick_expert'] = pe.reshape(48,16*P)
    fl = lambda v: ch(np.asarray(v).reshape(-1))
    a['qkv_w'] = f('L1_attn_in_proj_weight').T; a['qkv_b'] = fl(f('L1_attn_in_proj_bias'))
    a['pos_w'] = f('L1_attn_pos_proj_weight').T; a['pos_b'] = fl(f('L1_attn_pos_proj_bias'))
    a['o_w'] = f('L1_attn_out_proj_weight').T; a['o_b'] = fl(f('L1_attn_out_proj_bias'))
    a['pos_t'] = f('L1_attn_pos')[:15, 0].T
    a['r_w'] = fl(f('L1_attn_r_w_bias')); a['r_r'] = fl(f('L1_attn_r_r_bias'))
    hd = np.zeros((P, 8, 2, 8, 16), np.float32)
    for s in range(8):
        for c in range(2):
            for p in range(P): hd[p, s, c, s, c*8 + p//16] = 1
    hd = hd.reshape(P, 16, P)
    a['heads'] = hd; a['unheads'] = hd.transpose(2,1,0)
    a['g1_w'] = f('L1_ffn_gate_w1').T; a['g1_b'] = fl(f('L1_ffn_gate_b1'))
    g2 = f('L1_ffn_gate_w2')
    a['g2_rep'] = np.repeat(g2.T, 16, 1); a['g2_rep_b'] = np.repeat(f('L1_ffn_gate_b2'), 16)[:,None]
    a['g2_w'] = g2.T; a['g2_b'] = f('L1_ffn_gate_b2')[:,None]
    a['same'] = np.broadcast_to(np.tile(np.eye(16, dtype=np.float32), (8,1))[:,None,:], (P,8,16))
    a['tb1'] = f('L1_ffn_Tb1'); a['tb2'] = f('L1_ffn_Tb2')
    a['b1'] = fl(f('L1_ffn_b1')); a['b2'] = fl(f('L1_ffn_b2'))
    a['tw1'] = f('L1_ffn_TW1').transpose(0,2,1).reshape(P, -1); a['fw1'] = f('L1_ffn_W1').T.reshape(16, -1)
    a['tw2'] = f('L1_ffn_TW2').transpose(0,2,1).reshape(P, -1); a['fw2'] = f('L1_ffn_W2').T.reshape(16, -1)
    return {k: np.ascontiguousarray(v) for k,v in a.items()}


def kernel(**inputs):
    import concourse.bacc as _bacc
    from concourse.bass_utils import run_bass_kernel_spmd as _run

    nc = _bacc.Bacc("TRN2", target_bir_lowering=False, num_devices=1)
    arrays, aps = {}, {}
    for name, a in lay_out(inputs).items():
        arrays[f"in_{name}_dram"] = a
        aps[name] = nc.dram_tensor(f"in_{name}_dram", a.shape, mybir.dt.from_np(a.dtype), kind="ExternalInput").ap()
    out = nc.dram_tensor("out_0_dram", (HC, P, B * S), F32, kind="ExternalOutput").ap()
    vit_tower(nc, aps, out)
    r = _run(nc, [arrays], core_ids=[0])
    got = r.results[0]["out_0_dram"]
    return np.ascontiguousarray(got.reshape(H, B, S).transpose(1, 2, 0))
```

```python
from contextlib import ExitStack

import numpy as np
import concourse.bass as bass
from concourse import mybir

F32 = mybir.dt.float32
BF16 = mybir.dt.bfloat16
ALU = mybir.AluOpType
ACT = mybir.ActivationFunctionType
AX = mybir.AxisListType

P = 128
B, S, H = 8, 512, 256
HC = H // P
TOKD = 4
XC = H * TOKD // P
DI = 2 * H
DC = DI // P
NS = 16
TAPS = 4
E = 16
EI = 128
SC = 4
NG = 4
TOPK = 4
KSTEP = 2 * NS
MOE = E + SC
EPS = 1e-5


class Steps:

    def __init__(self, sem, names):
        self.sem = sem
        self.names = list(names)
        self.index = {n: k + 1 for k, n in enumerate(self.names)}
        assert len(self.index) == len(self.names)

    def at(self, rnd, name):
        return rnd * len(self.names) + self.index[name]


def tok_cols(b):
    return slice(b * S, (b + 1) * S) if isinstance(b, int) else bass.ts(b, S)


def spread_over(ap, n):
    return ap.rearrange("p (a b) -> p a b", a=1).to_broadcast([ap.shape[0], n, ap.shape[1]])


def vit_tower(nc, a, out):
    with ExitStack() as ctx:
        def sb(name, shape, dt=F32):
            return ctx.enter_context(nc.sbuf_tensor(name, shape, dt))

        def sem(name):
            return ctx.enter_context(nc.semaphore(name))

        hT = sb("hT", [P, HC, B * S])
        ident = sb("ident", [P, P])
        means = sb("means", [P, P])
        eps = sb("eps", [P, 1])
        ps = ctx.enter_context(nc.psum_tensor("ps", [P, 8, 512], F32))
        with ExitStack() as one:
            mamba_and_experts(nc, one, a, hT, ident, means, eps, ps)
        with ExitStack() as two:
            attention(nc, two, a, hT, ident, means, eps, ps)
        with ExitStack() as three:
            modulated_ffn(nc, three, a, out, hT, means, eps, ps)


def tensor_scan_parts(k):
    parts = []
    if 0 <= k < KSTEP:
        parts.append(("C", k))
    if 1 <= k <= KSTEP:
        parts.append(("Y", k - 1))
    if -1 <= k < KSTEP - 1:
        parts.append(("B", k + 1))
    return parts


def mamba_and_experts(nc, ctx, a, hT, ident, means, eps, ps):
    def sb(name, shape, dt=F32):
        return ctx.enter_context(nc.sbuf_tensor(name, shape, dt))

    def sem(name):
        return ctx.enter_context(nc.semaphore(name))

    tok_w = sb("tok_w", [P, XC, H])
    w_in = sb("w_in", [P, HC, 2 * DI])
    w_out = sb("w_out", [P, DC, H])
    w_x = sb("w_x", [P, DC, 112])
    w_dt = sb("w_dt", [P, DI])
    up_w = sb("up_w", [P, HC, E * EI])
    down_w = sb("down_w", [P, E, H])
    sup_w = sb("sup_w", [P, HC, SC * P])
    sdown_w = sb("sdown_w", [P, SC, H])
    gate_w = sb("gate_w", [P, HC, E])
    taps = sb("taps", [P, DC, TAPS])
    tap_b = sb("tap_b", [P, DC])
    b_dt = sb("b_dt", [P, DC])
    d_skip = sb("d_skip", [P, DC])
    a_neg = sb("a_neg", [P, DC, NS])
    pick_state = sb("pick_state", [96, 2 * NS], BF16)
    pick_expert = sb("pick_expert", [P, E], BF16)
    picks_f = sb("picks_f", [P, 2 * NS + E])
    identb = sb("identb", [P, P], BF16)
    lower = sb("lower", [P, E, E])

    x_in = sb("x_in", [P, XC // 2, S])
    u_raw = sb("u_raw", [P, DC, S])
    z_raw = sb("z_raw", [P, DC, S])
    u = sb("u", [P, DC, S])
    zg = sb("zg", [P, DC, S])
    delta = sb("delta", [P, DC, S])
    du = sb("du", [P, DC, S])
    bc = sb("bc", [96, S], BF16)
    mx = sb("mx", [P, HC, S])
    comb_t = sb("comb_t", [P, S], BF16)
    m_act = sb("m_act", [P, 2, S])
    sc = sb("sc", [P, 4 * E])
    comb = sb("comb", [P, 4, E])
    comb_p = sb("comb_p", [P, 4, P // E, E], BF16)

    def viewer(region):
        def view(at, *shape):
            n = int(np.prod(shape))
            v = region[:, at:at + n]
            if len(shape) == 2:
                v = v.rearrange("p (a b) -> p a b", a=shape[0])
            if len(shape) == 3:
                v = v.rearrange("p (a b c) -> p a b c", a=shape[0], b=shape[1])
            return v
        return view

    view = viewer(sb("scan_region", [P, 5120]))
    dA = view(0, 2, 2, S)
    hs = view(2048, 2, S)
    hC = view(3072, 2, 2, S)
    th = view(0, DC, S)
    thz = view(2048, DC, S)
    r_bc = view(4096, S)
    dtl = view(4608, S)
    view = viewer(sb("front_region", [P, 4 * S + 2 * (S + TAPS - 1)]))
    xc = view(0, HC, S)
    sq = view(2 * S, HC, S)
    xpad = view(4 * S, 2, S + TAPS - 1)
    view = viewer(sb("route_region", [P, 1616]))
    r_sq = view(0, HC, S)
    c_gt = view(0, 2, E * E)
    c_eq = view(512, 2, E * E)
    pairs = view(1024, 6, 4 * NG)
    gsum = view(1120, 4 * NG)
    g_gt = view(1136, 4, NG * NG)
    g_eq = view(1200, 4, NG * NG)
    grank = view(1264, 4 * NG)
    masked = view(1280, 4 * E)
    rank = view(1344, 4 * E)
    wsum = view(1408, 4)
    wres = view(1412, 4 * E)
    inv = sb("inv", [P, 2, 4])

    ws_t = u_raw[:, 0:1, :].rearrange("p a (c o) -> p (a c) o", c=HC)
    v_rep = u_raw[:, 1:3, :].rearrange("p a (c o) -> p (a c) o", c=2)

    loaded, x_loaded, down_loaded = sem("loaded"), sem("x_loaded"), sem("down_loaded")
    setup_vector = Steps(sem("setup_vector"), [f"tok{k}" for k in range(XC)]
                         + ["tap", "tapb", "cap", "aneg", "identb", "pick_state", "pick_expert", "pad"])
    setup_scalar = Steps(sem("setup_scalar"), ["aexp"])
    front_tensor = Steps(sem("front_tensor"), ["tok_lo", "tok", "mean", "var", "inv", "x0", "z0", "x1", "z1"])
    front_scalar = Steps(sem("front_scalar"), ["h", "sq", "std", "x0", "z0", "x1", "z1"])
    front_vector = Steps(sem("front_vector"), ["pad", "xc", "inv", "xn"] + [f"conv{p}{j}" for p in range(2) for j in range(TAPS)])
    entry_tensor = Steps(sem("entry_tensor"), ["bcdt", "dt"])
    entry_scalar = Steps(sem("entry_scalar"), ["thu", "thz", "dtl", "v", "abs", "exp", "ln"])
    entry_vector = Steps(sem("entry_vector"), ["u", "bc1", "r1", "bc2", "r2", "bc3", "zg", "delta0", "du0", "delta1", "du1"])
    scan_tensor = Steps(sem("scan_tensor"), [f"{name}{at}" for k in range(-1, KSTEP + 1) for name, at in tensor_scan_parts(k)]
                        + ["proj"])
    scan_scalar = Steps(sem("scan_scalar"), [f"dA{k}" for k in range(KSTEP)])
    scan_vector = Steps(sem("scan_vector"), [n for k in range(KSTEP) for n in
                                             [f"dBu{k}", f"scan{k}", f"hC{k}"]
                                             + ([f"skip{k // NS}", f"gated{k // NS}"] if k % NS == NS - 1 else [])] + ["res"])
    route_tensor = Steps(sem("route_tensor"), ["mean", "var", "inv", "gate", "turn"])
    route_scalar = Steps(sem("route_scalar"), ["sq", "std", "e", "comb_t"])
    route_vector = Steps(sem("route_vector"), ["xc", "inv", "xn", "s1", "s", "p0", "p1", "p2", "p3", "p4", "p5", "gs", "ggt", "geq",
                                               "geql", "gsumr", "gr", "gm", "msk", "cgt0", "ceq0", "ceql0", "csum0", "cr0",
                                               "cgt1", "ceq1", "ceql1", "csum1", "cr1", "w", "ws",
                                               "wr", "rcp", "comb", "k1", "q1", "k2", "q2", "k3"])
    expert_tensor = Steps(sem("expert_tensor"), [n for j in range(MOE + 2) for n in
                                                 ([f"dn{j - 2}"] if j >= 2 else [])
                                                 + (([f"up{j}"] + ([f"cb{j}"] if j < E else [])) if j < MOE else [])])
    expert_scalar = Steps(sem("expert_scalar"), [f"th{j}" for j in range(MOE)])
    expert_vector = Steps(sem("expert_vector"), [n for j in range(MOE) for n in ([f"a{j}"] + ([f"c{j}"] if j < E else []))] + ["res"])

    LOADS = 16 * 20
    MOE_AT = KSTEP - MOE

    with nc.Block() as block:
        @block.sync
        def _(sp):
            for dst, src in (
                (ident[:], a["ident"]), (means[:], a["means"]), (eps[:], a["eps"]),
                (ws_t, a["ws_t"].rearrange("(c p) o -> p c o", p=P)),
                (v_rep, a["tok_v"].rearrange("(n d) o -> n d o", n=1).to_broadcast([P, TOKD, H])),
                (taps[:], a["taps"]), (tap_b[:], a["tap_b"]), (b_dt[:], a["b_dt"]), (d_skip[:], a["d_skip"]),
                (a_neg[:], a["a_log"]), (lower[:], a["lower"]), (picks_f[:], a["picks"]),
                (w_in[:], a["w_in"].rearrange("(c p) o -> p c o", p=P)),
                (w_x[:], a["w_x"].rearrange("(c p) o -> p c o", p=P)),
                (w_dt[96:112, :], a["w_dt"]),
                (w_out[:], a["w_out"].rearrange("(c p) o -> p c o", p=P)),
                (gate_w[:], a["gate"].rearrange("(c p) o -> p c o", p=P)),
                (sup_w[:], a["sup"].rearrange("(c p) o -> p c o", p=P)),
                (sdown_w[:], a["sdown"].rearrange("(c p) o -> p c o", p=P)),
                (up_w[:], a["up"].rearrange("(c p) o -> p c o", p=P)),
            ):
                sp.dma_start(dst, src).then_inc(loaded, 16)
            half = XC // 2
            for b in range(B):
                if b:
                    sp.wait_ge(front_tensor.sem, front_tensor.at(b - 1, "tok"))
                sp.dma_start(x_in[:], a["x"][b][:, 0:half, :]).then_inc(x_loaded, 16)
                sp.wait_ge(front_tensor.sem, front_tensor.at(b, "tok_lo"))
                sp.dma_start(x_in[:], a["x"][b][:, half:, :]).then_inc(x_loaded, 16)

        @block.gpsimd
        def _(pool):
            pool.dma_start(down_w[:], a["down"].rearrange("e p o -> p e o")).then_inc(down_loaded, 16)

        @block.scalar
        def _(act):
            A = nc.scalar

            def front(n, at):
                if at == 4:
                    act.wait_ge(front_tensor.sem, front_tensor.at(n, "tok"))
                    A.activation(hT[:, :, tok_cols(n)], ps[:, 6:8, :], ACT.Copy).then_inc(front_scalar.sem, 1)
                if at == 6:
                    act.wait_ge(front_vector.sem, front_vector.at(n, "xc"))
                    A.activation(sq, xc, ACT.Square).then_inc(front_scalar.sem, 1)
                if at == 7:
                    act.wait_ge(front_tensor.sem, front_tensor.at(n, "var"))
                    A.activation(inv[:, 0, :], ps[:, 7, 0:4], ACT.Sqrt, bias=eps[:, 0:1]).then_inc(front_scalar.sem, 1)
                if at == 9:
                    act.wait_ge(front_tensor.sem, front_tensor.at(n, "x0"))
                    act.wait_ge(front_vector.sem, front_vector.at(n, "pad"))
                    A.activation(xpad[:, :, TAPS - 1:], ps[:, 6:8, :], ACT.Copy).then_inc(front_scalar.sem, 1)
                if at == 10:
                    act.wait_ge(front_tensor.sem, front_tensor.at(n, "z0"))
                    A.activation(z_raw[:, 0:2, :], ps[:, 6:8, :], ACT.Copy).then_inc(front_scalar.sem, 1)
                if at == 12:
                    act.wait_ge(front_tensor.sem, front_tensor.at(n, "x1"))
                    act.wait_ge(front_vector.sem, front_vector.at(n, f"conv0{TAPS - 1}"))
                    A.activation(xpad[:, :, TAPS - 1:], ps[:, 6:8, :], ACT.Copy).then_inc(front_scalar.sem, 1)
                if at == 13:
                    act.wait_ge(front_tensor.sem, front_tensor.at(n, "z1"))
                    A.activation(z_raw[:, 2:4, :], ps[:, 6:8, :], ACT.Copy).then_inc(front_scalar.sem, 1)

            def entry(b):
                act.wait_ge(front_vector.sem, front_vector.at(b, f"conv1{TAPS - 1}"))
                if not (isinstance(b, int) and b == 0):
                    act.wait_ge(scan_tensor.sem, scan_tensor.at(b - 1, f"Y{KSTEP - 1}"))
                A.activation(th, u_raw[:], ACT.Tanh).then_inc(entry_scalar.sem, 1)
                act.wait_ge(front_scalar.sem, front_scalar.at(b, "z1"))
                A.activation(thz, z_raw[:], ACT.Tanh, scale=0.5).then_inc(entry_scalar.sem, 1)
                act.wait_ge(entry_tensor.sem, entry_tensor.at(b, "bcdt"))
                A.activation(dtl[96:112, :], ps[96:112, 2, :], ACT.Copy).then_inc(entry_scalar.sem, 1)
                act.wait_ge(entry_tensor.sem, entry_tensor.at(b, "dt"))
                for c in range(DC):
                    last = A.activation(delta[:, c, :], ps[:, 4 + c, :], ACT.Identity, bias=b_dt[:, c:c + 1])
                last.then_inc(entry_scalar.sem, 1)
                act.wait_ge(entry_scalar.sem, entry_scalar.at(b, "v"))
                A.activation(th, delta[:], ACT.Abs).then_inc(entry_scalar.sem, 1)
                act.wait_ge(entry_scalar.sem, entry_scalar.at(b, "abs"))
                A.activation(th, th, ACT.Exp, scale=-1.0).then_inc(entry_scalar.sem, 1)
                act.wait_ge(entry_scalar.sem, entry_scalar.at(b, "exp"))
                A.activation(th, th, ACT.Ln, bias=1.0).then_inc(entry_scalar.sem, 1)

            def scan_step(b, k):
                half, n = divmod(k, NS)
                if k == 0:
                    act.wait_ge(entry_vector.sem, entry_vector.at(b, "delta1"))
                if k >= 2:
                    act.wait_ge(scan_vector.sem, scan_vector.at(b, f"scan{k - 2}"))
                for i in range(2):
                    c = 2 * half + i
                    last = A.activation(dA[:, k % 2, i, :], delta[:, c, :], ACT.Exp, scale=a_neg[:, c, n:n + 1])
                last.then_inc(scan_scalar.sem, 1)

            def route(m, at):
                if at == 1:
                    act.wait_ge(route_vector.sem, route_vector.at(m, "xc"))
                    A.activation(r_sq, mx[:], ACT.Square).then_inc(route_scalar.sem, 1)
                if at == 3:
                    act.wait_ge(route_tensor.sem, route_tensor.at(m, "var"))
                    A.activation(inv[:, 1, :], ps[:, 5, 0:4], ACT.Sqrt, bias=eps[:, 0:1]).then_inc(route_scalar.sem, 1)
                if at == 6:
                    act.wait_ge(route_tensor.sem, route_tensor.at(m, "gate"))
                    A.activation(sc[:], ps[:, 5, 0:4 * E], ACT.Exp, scale=-1.0).then_inc(route_scalar.sem, 1)
                if at == 12:
                    act.wait_ge(route_tensor.sem, route_tensor.at(m, "turn"))
                    A.activation(comb_t[:], ps[:, 5, :], ACT.Copy).then_inc(route_scalar.sem, 1)

            def expert_step(m, j):
                act.wait_ge(expert_tensor.sem, expert_tensor.at(m, f"up{j}"))
                if j >= 2:
                    act.wait_ge(expert_tensor.sem, expert_tensor.at(m, f"dn{j - 2}"))
                A.activation(m_act[:, j % 2, :], ps[:, 4, :], ACT.Tanh, scale=0.5).then_inc(expert_scalar.sem, 1)

            def rnd(b, before, after):
                entry(b)
                for k in range(KSTEP + 1):
                    if k < KSTEP:
                        scan_step(b, k)
                    if before:
                        route(b - 1, k)
                        if 0 <= k - 1 - MOE_AT < MOE:
                            expert_step(b - 1, k - 1 - MOE_AT)
                    if after:
                        front(b + 1, k)

            act.wait_ge(loaded, LOADS)
            act.wait_ge(setup_vector.sem, setup_vector.at(0, "cap"))
            A.activation(a_neg[:], a_neg[:], ACT.Exp).then_inc(setup_scalar.sem, 1)
            act.wait_ge(setup_vector.sem, setup_vector.at(0, "pad"))
            for k in range(KSTEP):
                front(0, k)
            rnd(0, False, True)
            with act.Fori(1, B - 1) as b:
                rnd(b, True, True)
            rnd(B - 1, True, False)
            for k in range(KSTEP):
                route(B - 1, k)
            for j in range(MOE):
                expert_step(B - 1, j)

        @block.tensor
        def _(pe):
            def mm(o, w, x, first, last):
                return nc.tensor.matmul(o, w, x, start=first, stop=last)

            def token_sums(o, x):
                for t in range(4):
                    for c in range(HC):
                        last = mm(o[:, t:t + 1], x[:, c, t * P:(t + 1) * P], means[:, 0:1], c == 0, c == HC - 1)
                return last

            def spread_tokens(bank, v):
                for t in range(4):
                    last = mm(ps[:, bank, t * P:(t + 1) * P], v[:, t:t + 1].to_broadcast([P, P]), ident[:], True, True)
                return last

            def front(n, at):
                half = XC // 2
                if at in (1, 3):
                    hi = at == 3
                    pe.wait_ge(x_loaded, n * 32 + (32 if hi else 16))
                    for k in range(half):
                        for o in range(HC):
                            last = mm(ps[:, 6 + o, :], tok_w[:, hi * half + k, o * P:(o + 1) * P], x_in[:, k, :],
                                      not hi and k == 0, hi and k == half - 1)
                    last.then_inc(front_tensor.sem, 1)
                if at == 5:
                    pe.wait_ge(front_scalar.sem, front_scalar.at(n, "h"))
                    for c in range(HC):
                        last = mm(ps[:, 6, :], means[:], hT[:, c, tok_cols(n)], c == 0, c == HC - 1)
                    last.then_inc(front_tensor.sem, 1)
                if at == 6:
                    pe.wait_ge(front_scalar.sem, front_scalar.at(n, "sq"))
                    token_sums(ps[:, 7, :], sq).then_inc(front_tensor.sem, 1)
                if at == 8:
                    pe.wait_ge(front_vector.sem, front_vector.at(n, "inv"))
                    spread_tokens(6, inv[:, 0, :]).then_inc(front_tensor.sem, 1)
                for i, (name, step, o) in enumerate((("x0", 9, 0), ("z0", 10, DC), ("x1", 11, 2), ("z1", 12, DC + 2))):
                    if at == step:
                        if i == 0:
                            pe.wait_ge(front_vector.sem, front_vector.at(n, "xn"))
                        else:
                            pe.wait_ge(front_scalar.sem, front_scalar.at(n, ("x0", "z0", "x1")[i - 1]))
                        for q in range(2):
                            for c in range(HC):
                                last = mm(ps[:, 6 + q, :], w_in[:, c, (o + q) * P:(o + q + 1) * P], xc[:, c, :], c == 0, c == HC - 1)
                        last.then_inc(front_tensor.sem, 1)

            def entry(b):
                pe.wait_ge(entry_vector.sem, entry_vector.at(b, "u"))
                for c in range(DC):
                    last = mm(ps[0:112, 2, :], w_x[:, c, :], u[:, c, :], c == 0, c == DC - 1)
                last.then_inc(entry_tensor.sem, 1)
                pe.wait_ge(entry_scalar.sem, entry_scalar.at(b, "dtl"))
                if not (isinstance(b, int) and b == 0):
                    pe.wait_ge(scan_vector.sem, scan_vector.at(b - 1, "res"))
                for c in range(DC):
                    last = mm(ps[:, 4 + c, :], w_dt[96:112, c * P:(c + 1) * P], dtl[96:112, :], True, True)
                last.then_inc(entry_tensor.sem, 1)

            def spread(bank, row):
                return mm(ps[:, bank, :], pick_state[:, row:row + 1].to_broadcast([96, P]), bc[:], True, True)

            def scan_part(b, name, k):
                n = k % NS
                if name == "B":
                    if k == 0:
                        pe.wait_ge(entry_vector.sem, entry_vector.at(b, "bc3"))
                        pe.wait_ge(entry_scalar.sem, entry_scalar.at(b, "dtl"))
                    else:
                        pe.wait_ge(scan_vector.sem, scan_vector.at(b, f"dBu{k - 1}"))
                    spread(2, n).then_inc(scan_tensor.sem, 1)
                if name == "C":
                    if k:
                        pe.wait_ge(scan_vector.sem, scan_vector.at(b, f"hC{k - 1}"))
                    spread(3, NS + n).then_inc(scan_tensor.sem, 1)
                if name == "Y":
                    pe.wait_ge(scan_vector.sem, scan_vector.at(b, f"hC{k}"))
                    if k == NS:
                        pe.wait_ge(scan_vector.sem, scan_vector.at(b, "skip0"))
                    for i in range(2):
                        last = mm(ps[:, i, :], ident[:], hC[:, k % 2, i, :], n == 0, n == NS - 1)
                    last.then_inc(scan_tensor.sem, 1)

            def project(b):
                pe.wait_ge(scan_vector.sem, scan_vector.at(b, "gated1"))
                for o in range(HC):
                    for c in range(DC):
                        last = mm(ps[:, o, :], w_out[:, c, o * P:(o + 1) * P], zg[:, c, :], c == 0, c == DC - 1)
                last.then_inc(scan_tensor.sem, 1)

            def expert_up(m, j):
                if j:
                    pe.wait_ge(expert_vector.sem, expert_vector.at(m, f"a{j - 1}"))
                else:
                    pe.wait_ge(route_scalar.sem, route_scalar.at(m, "comb_t"))
                w = up_w if j < E else sup_w
                at = (j if j < E else j - E) * P
                for c in range(HC):
                    last = mm(ps[:, 4, :], w[:, c, at:at + P], mx[:, c, :], c == 0, c == HC - 1)
                last.then_inc(expert_tensor.sem, 1)
                if j < E:
                    if j:
                        pe.wait_ge(expert_vector.sem, expert_vector.at(m, f"c{j - 1}"))
                    mm(ps[:, 5, :], pick_expert[:, j:j + 1].to_broadcast([P, P]), comb_t[:], True, True)\
                        .then_inc(expert_tensor.sem, 1)

            def expert_down(m, j):
                pe.wait_ge(expert_vector.sem, expert_vector.at(m, f"c{j}" if j < E else f"a{j}"))
                for o in range(HC):
                    w = down_w[:, j, o * P:(o + 1) * P] if j < E else sdown_w[:, j - E, o * P:(o + 1) * P]
                    last = mm(ps[:, 6 + o, :], w, m_act[:, j % 2, :], j == 0, j == MOE - 1)
                last.then_inc(expert_tensor.sem, 1)

            def expert_step(m, j):
                if 2 <= j:
                    expert_down(m, j - 2)
                if j < MOE:
                    expert_up(m, j)

            def route(m, at):
                if at == 0:
                    pe.wait_ge(scan_vector.sem, scan_vector.at(m, "res"))
                    for c in range(HC):
                        last = mm(ps[:, 4, :], means[:], hT[:, c, tok_cols(m)], c == 0, c == HC - 1)
                    last.then_inc(route_tensor.sem, 1)
                if at == 2:
                    pe.wait_ge(route_scalar.sem, route_scalar.at(m, "sq"))
                    token_sums(ps[:, 5, :], r_sq).then_inc(route_tensor.sem, 1)
                if at == 4:
                    pe.wait_ge(route_vector.sem, route_vector.at(m, "inv"))
                    spread_tokens(4, inv[:, 1, :]).then_inc(route_tensor.sem, 1)
                if at == 5:
                    pe.wait_ge(route_vector.sem, route_vector.at(m, "xn"))
                    for t in range(4):
                        for c in range(HC):
                            last = mm(ps[:, 5, t * E:(t + 1) * E], mx[:, c, t * P:(t + 1) * P], gate_w[:, c, :],
                                      c == 0, c == HC - 1)
                    last.then_inc(route_tensor.sem, 1)
                if at == 12:
                    pe.wait_ge(route_vector.sem, route_vector.at(m, "k3"))
                    for t in range(4):
                        last = mm(ps[:, 5, t * P:(t + 1) * P], comb_p[:, t, :, :].rearrange("p a b -> p (a b)"), identb[:],
                                  True, True)
                    last.then_inc(route_tensor.sem, 1)

            def rnd(b, before, after):
                entry(b)
                for k in range(-1, KSTEP + 1):
                    for name, at in tensor_scan_parts(k):
                        scan_part(b, name, at)
                    if k == 0:
                        pe.wait_ge(entry_scalar.sem, entry_scalar.at(b, "v"))
                    if before:
                        route(b - 1, k)
                        if after and k - MOE_AT == 2:
                            pe.wait_ge(front_scalar.sem, front_scalar.at(b + 1, "z1"))
                        if 0 <= k - MOE_AT < MOE + 1:
                            expert_step(b - 1, k - MOE_AT)
                    if after:
                        front(b + 1, k)
                if before:
                    expert_step(b - 1, MOE + 1)
                project(b)

            pe.wait_ge(loaded, LOADS)
            pe.wait_ge(setup_vector.sem, setup_vector.at(0, "pad"))
            for k in range(KSTEP):
                front(0, k)
            pe.wait_ge(front_scalar.sem, front_scalar.at(0, "z1"))
            rnd(0, False, True)
            pe.wait_ge(down_loaded, 16)
            with pe.Fori(1, B - 1) as b:
                rnd(b, True, True)
            rnd(B - 1, True, False)
            pe.wait_ge(expert_vector.sem, expert_vector.at(B - 2, "res"))
            for k in range(KSTEP):
                route(B - 1, k)
            for j in range(MOE + 2):
                expert_step(B - 1, j)

        @block.vector
        def _(dve):
            V = nc.vector

            def front(n, at):
                if at == 4:
                    V.memset(xpad[:, :, 0:TAPS - 1], 0.0).then_inc(front_vector.sem, 1)
                if at == 5:
                    dve.wait_ge(front_tensor.sem, front_tensor.at(n, "mean"))
                    V.tensor_tensor(xc, hT[:, :, tok_cols(n)], spread_over(ps[:, 6, :], HC), ALU.subtract).then_inc(front_vector.sem, 1)
                if at == 7:
                    dve.wait_ge(front_scalar.sem, front_scalar.at(n, "std"))
                    V.reciprocal(inv[:, 0, :], inv[:, 0, :]).then_inc(front_vector.sem, 1)
                if at == 8:
                    dve.wait_ge(front_tensor.sem, front_tensor.at(n, "inv"))
                    V.tensor_tensor(xc, xc, spread_over(ps[:, 6, :], HC), ALU.mult).then_inc(front_vector.sem, 1)
                for pair, steps in ((0, (10, 10, 11, 11)), (1, (14, 16, 18, 20))):
                    for j in range(TAPS):
                        if at == steps[j]:
                            conv(n, pair, j)

            def conv(n, pair, j):
                tap = TAPS - 1 - j
                if j:
                    dve.wait_ge(front_vector.sem, front_vector.at(n, f"conv{pair}{j - 1}"))
                else:
                    dve.wait_ge(front_scalar.sem, front_scalar.at(n, f"x{pair}"))
                for i in range(2):
                    c = 2 * pair + i
                    x = xpad[:, i, tap:tap + S]
                    w = taps[:, c, tap:tap + 1]
                    if j == 0:
                        last = V.tensor_scalar(u_raw[:, c, :], x, w, tap_b[:, c:c + 1], ALU.mult, ALU.add)
                    else:
                        last = V.scalar_tensor_tensor(u_raw[:, c, :], x, w, u_raw[:, c, :], ALU.mult, ALU.add)
                last.then_inc(front_vector.sem, 1)

            def entry_u(b):
                if not (isinstance(b, int) and b == 0):
                    dve.wait_ge(scan_vector.sem, scan_vector.at(b - 1, "gated1"))
                dve.wait_ge(entry_scalar.sem, entry_scalar.at(b, "thu"))
                V.scalar_tensor_tensor(u[:], th, 1.0, u_raw[:], ALU.add, ALU.mult).then_inc(entry_vector.sem, 1)

            def entry(b):
                dve.wait_ge(entry_tensor.sem, entry_tensor.at(b, "bcdt"))
                dve.wait_ge(entry_scalar.sem, entry_scalar.at(b, "dtl"))
                V.tensor_copy(bc[:], ps[0:96, 2, :]).then_inc(entry_vector.sem, 1)
                dve.wait_ge(entry_vector.sem, entry_vector.at(b, "bc1"))
                V.tensor_tensor(r_bc[0:96, :], ps[0:96, 2, :], bc[:], ALU.subtract).then_inc(entry_vector.sem, 1)
                dve.wait_ge(entry_vector.sem, entry_vector.at(b, "r1"))
                V.tensor_copy(bc[32:64, :], r_bc[32:64, :])
                V.tensor_copy(bc[64:96, :], r_bc[64:96, :]).then_inc(entry_vector.sem, 1)
                dve.wait_ge(entry_vector.sem, entry_vector.at(b, "bc2"))
                V.tensor_tensor(r_bc[64:96, :], r_bc[64:96, :], bc[64:96, :], ALU.subtract).then_inc(entry_vector.sem, 1)
                dve.wait_ge(entry_vector.sem, entry_vector.at(b, "r2"))
                V.tensor_copy(bc[64:96, :], r_bc[64:96, :]).then_inc(entry_vector.sem, 1)
                dve.wait_ge(entry_scalar.sem, entry_scalar.at(b, "thz"))
                V.scalar_tensor_tensor(zg[:], thz, 1.0, z_raw[:], ALU.add, ALU.mult).then_inc(entry_vector.sem, 1)
                dve.wait_ge(entry_scalar.sem, entry_scalar.at(b, "ln"))
                for half in range(2):
                    pair = slice(2 * half, 2 * half + 2)
                    V.scalar_tensor_tensor(delta[:, pair, :], delta[:, pair, :], 0.0, th[:, pair, :], ALU.max, ALU.add)\
                        .then_inc(entry_vector.sem, 1)
                    dve.wait_ge(entry_vector.sem, entry_vector.at(b, f"delta{half}"))
                    V.tensor_tensor(du[:, pair, :], delta[:, pair, :], u[:, pair, :], ALU.mult).then_inc(entry_vector.sem, 1)

            def scan_first(b, k):
                half = k // NS
                dve.wait_ge(scan_tensor.sem, scan_tensor.at(b, f"B{k}"))
                if k == 0:
                    dve.wait_ge(entry_vector.sem, entry_vector.at(b, "du1"))
                else:
                    dve.wait_ge(scan_vector.sem, scan_vector.at(b, f"hC{k - 1}"))
                V.tensor_tensor(hs, du[:, 2 * half:2 * half + 2, :], spread_over(ps[:, 2, :], 2), ALU.mult)\
                    .then_inc(scan_vector.sem, 1)
                dve.wait_ge(scan_scalar.sem, scan_scalar.at(b, f"dA{k}"))
                dve.wait_ge(scan_vector.sem, scan_vector.at(b, f"dBu{k}"))
                for i in range(2):
                    last = V.tensor_tensor_scan(hs[:, i, :], dA[:, k % 2, i, :], hs[:, i, :], 0.0, ALU.mult, ALU.add)
                last.then_inc(scan_vector.sem, 1)

            def scan_second(b, k):
                dve.wait_ge(scan_tensor.sem, scan_tensor.at(b, f"C{k}"))
                dve.wait_ge(scan_vector.sem, scan_vector.at(b, f"scan{k}"))
                if k >= 2:
                    dve.wait_ge(scan_tensor.sem, scan_tensor.at(b, f"Y{k - 2}"))
                V.tensor_tensor(hC[:, k % 2], hs, spread_over(ps[:, 3, :], 2), ALU.mult).then_inc(scan_vector.sem, 1)

            def scan_end(b, half):
                dve.wait_ge(scan_tensor.sem, scan_tensor.at(b, f"Y{NS * half + NS - 1}"))
                pair = slice(2 * half, 2 * half + 2)
                for i in range(2):
                    c = 2 * half + i
                    last = V.scalar_tensor_tensor(u[:, c, :], u[:, c, :], d_skip[:, c:c + 1], ps[:, i, :], ALU.mult, ALU.add)
                last.then_inc(scan_vector.sem, 1)
                dve.wait_ge(scan_vector.sem, scan_vector.at(b, f"skip{half}"))
                V.tensor_tensor(zg[:, pair, :], u[:, pair, :], zg[:, pair, :], ALU.mult).then_inc(scan_vector.sem, 1)

            def scan_residual(b):
                dve.wait_ge(scan_tensor.sem, scan_tensor.at(b, "proj"))
                V.scalar_tensor_tensor(hT[:, :, tok_cols(b)], ps[:, 0:2, :], 0.5, hT[:, :, tok_cols(b)], ALU.mult, ALU.add)\
                    .then_inc(scan_vector.sem, 1)

            def expert_step(m, j):
                dve.wait_ge(expert_scalar.sem, expert_scalar.at(m, f"th{j}"))
                V.scalar_tensor_tensor(m_act[:, j % 2, :], m_act[:, j % 2, :], 1.0, ps[:, 4, :], ALU.add, ALU.mult)\
                    .then_inc(expert_vector.sem, 1)
                if j < E:
                    dve.wait_ge(expert_tensor.sem, expert_tensor.at(m, f"cb{j}"))
                    dve.wait_ge(expert_vector.sem, expert_vector.at(m, f"a{j}"))
                    V.tensor_tensor(m_act[:, j % 2, :], m_act[:, j % 2, :], ps[:, 5, :], ALU.mult).then_inc(expert_vector.sem, 1)

            def expert_end(m):
                dve.wait_ge(expert_tensor.sem, expert_tensor.at(m, f"dn{MOE - 1}"))
                V.scalar_tensor_tensor(hT[:, :, tok_cols(m)], ps[:, 6:8, :], 0.5, hT[:, :, tok_cols(m)], ALU.mult, ALU.add)\
                    .then_inc(expert_vector.sem, 1)

            def route(m, at):
                def step(ins, name):
                    ins.then_inc(route_vector.sem, 1)
                    dve.wait_ge(route_vector.sem, route_vector.at(m, name))

                def ranked(v, n):
                    return (v.rearrange("p (i o) -> p i o", o=1).to_broadcast([P, n, n]),
                            v.rearrange("p (o j) -> p o j", o=1).to_broadcast([P, n, n]))

                s4 = sc[:].rearrange("p (g e) -> p g e", e=E // NG)
                gt = gsum.rearrange("p (t g) -> p t g", t=4)
                gg, ge = (v.rearrange("p t (i j) -> p t i j", i=NG) for v in (g_gt, g_eq))
                mt = masked.rearrange("p (t e) -> p t e", t=4)
                cg, ce = (v.rearrange("p t (i j) -> p t i j", i=E) for v in (c_gt, c_eq))
                if at == 0:
                    dve.wait_ge(route_tensor.sem, route_tensor.at(m, "mean"))
                    V.tensor_tensor(mx[:], hT[:, :, tok_cols(m)], spread_over(ps[:, 4, :], HC), ALU.subtract).then_inc(route_vector.sem, 1)
                if at == 3:
                    dve.wait_ge(route_scalar.sem, route_scalar.at(m, "std"))
                    V.reciprocal(inv[:, 1, :], inv[:, 1, :]).then_inc(route_vector.sem, 1)
                if at == 4:
                    dve.wait_ge(route_tensor.sem, route_tensor.at(m, "inv"))
                    V.tensor_tensor(mx[:], mx[:], spread_over(ps[:, 4, :], HC), ALU.mult).then_inc(route_vector.sem, 1)
                if at == 6:
                    dve.wait_ge(route_scalar.sem, route_scalar.at(m, "e"))
                    step(V.tensor_scalar(sc[:], sc[:], 1.0, None, ALU.add), "s1")
                    step(V.reciprocal(sc[:], sc[:]), "s")
                    w = 0
                    for i in range(4):
                        for j in range(i + 1, 4):
                            V.tensor_tensor(pairs[:, w, :], s4[:, :, i], s4[:, :, j], ALU.add).then_inc(route_vector.sem, 1)
                            w += 1
                if at == 7:
                    dve.wait_ge(route_vector.sem, route_vector.at(m, "p5"))
                    step(V.tensor_reduce(gsum, pairs.rearrange("p w g -> p g w"), AX.X, ALU.max), "gs")
                    for t in range(4):
                        own, other = ranked(gt[:, t, :], NG)
                        last = V.tensor_tensor(gg[:, t], other, own, ALU.is_gt)
                    last.then_inc(route_vector.sem, 1)
                    for t in range(4):
                        own, other = ranked(gt[:, t, :], NG)
                        last = V.tensor_tensor(ge[:, t], other, own, ALU.is_equal)
                    step(last, "geq")
                if at == 8:
                    for t in range(4):
                        last = V.tensor_tensor(ge[:, t], ge[:, t], lower[:, 0:NG, 0:NG], ALU.mult)
                    step(last, "geql")
                    step(V.tensor_tensor(g_gt, g_gt, g_eq, ALU.add), "gsumr")
                    step(V.tensor_reduce(grank, g_gt.rearrange("p t (i j) -> p (t i) j", j=NG), AX.X, ALU.add), "gr")
                    step(V.tensor_scalar(grank, grank, 1.5, None, ALU.is_lt), "gm")
                    step(V.tensor_tensor(masked.rearrange("p (g e) -> p g e", e=E // NG), s4,
                                         grank.rearrange("p (g o) -> p g o", o=1).to_broadcast([P, 4 * NG, E // NG]), ALU.mult), "msk")
                for h in range(2):
                    if at == 9 + h:
                        for t in range(2):
                            own, other = ranked(mt[:, 2 * h + t, :], E)
                            last = V.tensor_tensor(cg[:, t], other, own, ALU.is_gt)
                        last.then_inc(route_vector.sem, 1)
                        for t in range(2):
                            own, other = ranked(mt[:, 2 * h + t, :], E)
                            last = V.tensor_tensor(ce[:, t], other, own, ALU.is_equal)
                        step(last, f"ceq{h}")
                        for t in range(2):
                            last = V.tensor_tensor(ce[:, t], ce[:, t], lower[:], ALU.mult)
                        step(last, f"ceql{h}")
                        step(V.tensor_tensor(c_gt, c_gt, c_eq, ALU.add), f"csum{h}")
                        step(V.tensor_reduce(rank[:, 2 * h * E:2 * (h + 1) * E], c_gt.rearrange("p t (i j) -> p (t i) j", j=E),
                                             AX.X, ALU.add), f"cr{h}")
                if at == 11:
                    step(V.scalar_tensor_tensor(masked, rank, TOPK - 0.5, sc[:], ALU.is_lt, ALU.mult), "w")
                    step(V.tensor_reduce(wsum, mt, AX.X, ALU.add), "ws")
                    step(V.tensor_scalar(wsum, wsum, 1e-20, None, ALU.add), "wr")
                    step(V.reciprocal(wsum, wsum), "rcp")
                    step(V.scalar_tensor_tensor(comb[:], mt, 2.5, wsum.rearrange("p (t o) -> p t o", o=1).to_broadcast([P, 4, E]),
                                                ALU.mult, ALU.mult), "comb")
                    left = wres.rearrange("p (t e) -> p t e", t=4)
                    step(V.tensor_copy(comb_p[:, :, 0, :], comb[:]), "k1")
                    step(V.tensor_tensor(left, comb[:], comb_p[:, :, 0, :], ALU.subtract), "q1")
                    step(V.tensor_copy(comb_p[:, :, 1, :], left), "k2")
                    step(V.tensor_tensor(left, left, comb_p[:, :, 1, :], ALU.subtract), "q2")
                    V.tensor_copy(comb_p[:, :, 2, :], left).then_inc(route_vector.sem, 1)

            def rnd(b, before, after):
                entry(b)
                for k in range(KSTEP):
                    scan_first(b, k)
                    if before:
                        route(b - 1, k)
                        if 0 <= k - 1 - MOE_AT < MOE:
                            expert_step(b - 1, k - 1 - MOE_AT)
                    if after:
                        front(b + 1, k)
                    scan_second(b, k)
                    if k == NS - 1:
                        scan_end(b, 0)
                if before:
                    expert_step(b - 1, MOE - 1)
                scan_end(b, 1)
                if after:
                    entry_u(b + 1)
                if before:
                    expert_end(b - 1)
                scan_residual(b)

            dve.wait_ge(loaded, LOADS)
            for d in range(TOKD):
                for c in range(HC):
                    V.tensor_tensor(tok_w[:, d * HC + c, :], ws_t[:, c, :], v_rep[:, d, :], ALU.mult).then_inc(setup_vector.sem, 1)
            V.tensor_scalar(taps[:], taps[:], 0.5, None, ALU.mult).then_inc(setup_vector.sem, 1)
            V.tensor_scalar(tap_b[:], tap_b[:], 0.5, None, ALU.mult).then_inc(setup_vector.sem, 1)
            V.tensor_scalar(a_neg[:], a_neg[:], 80.0, None, ALU.min).then_inc(setup_vector.sem, 1)
            dve.wait_ge(setup_scalar.sem, setup_scalar.at(0, "aexp"))
            V.tensor_scalar(a_neg[:], a_neg[:], -1.0, None, ALU.mult).then_inc(setup_vector.sem, 1)
            V.tensor_copy(identb[:], ident[:]).then_inc(setup_vector.sem, 1)
            V.tensor_copy(pick_state[:], picks_f[0:96, 0:2 * NS]).then_inc(setup_vector.sem, 1)
            V.tensor_copy(pick_expert[:], picks_f[:, 2 * NS:]).then_inc(setup_vector.sem, 1)
            V.memset(comb_p[:], 0.0).then_inc(setup_vector.sem, 1)
            dve.wait_ge(setup_vector.sem, setup_vector.at(0, "pad"))
            for k in range(KSTEP):
                front(0, k)
            entry_u(0)
            rnd(0, False, True)
            with dve.Fori(1, B - 1) as b:
                rnd(b, True, True)
            rnd(B - 1, True, False)
            for k in range(KSTEP):
                route(B - 1, k)
            for j in range(MOE):
                expert_step(B - 1, j)
            expert_end(B - 1)


def attention(nc, ctx, a, hT, ident, means, eps, ps):
    T, NH, D = B, 16, H // 16
    ROWS = 2 * T - 1
    PAIRS = T * HC

    def sb(name, shape, dt=F32):
        return ctx.enter_context(nc.sbuf_tensor(name, shape, dt))

    def sem(name):
        return ctx.enter_context(nc.semaphore(name))

    qkv_w = sb("qkv_w", [P, HC, 3 * H])
    pos_w = sb("pos_w", [P, HC, H])
    o_w = sb("o_w", [P, HC, H])
    pos_t = sb("pos_t", [P, HC, ROWS])
    qkv_b = sb("qkv_b", [P, 3 * HC])
    pos_b = sb("pos_b", [P, HC])
    o_b = sb("o_b", [P, HC])
    r_w = sb("r_w", [P, HC])
    r_r = sb("r_r", [P, HC])
    heads = sb("heads", [P, PAIRS, P])
    unheads = sb("unheads", [P, PAIRS, P])
    qkv = sb("qkv", [P, 3 * HC, B * S])
    p_row = sb("p_row", [P, HC, ROWS])
    p_gap = sb("p_gap", [P, HC, ROWS])
    gap = sb("gap", [P, T])
    p_t = sb("p_t", [P, HC, T])
    xc = sb("xc_a", [P, HC, S])
    sq = sb("sq_a", [P, HC, S])
    rstd = sb("rstd_a", [P, S])
    prod = sb("prod", [P, 3, S])
    s_row = sb("s_row", [P, S])
    s_tok = sb("s_tok", [P, 4, P])
    peak = sb("peak", [P, 4, NH])
    total = sb("total", [P, 4, NH])
    w_row = sb("w_row", [P, S])
    part = sb("part", [P, 2, S])
    mix = sb("mix", [P, HC, S])
    SCALE = float(D) ** -0.5

    loaded = sem("loaded_a")
    pos_tensor = Steps(sem("pos_tensor"), ["p", "gap"])
    pos_scalar = Steps(sem("pos_scalar"), ["p"])
    pos_vector = Steps(sem("pos_vector"), ["bq", "gap_w", "p_gap", "gap"])
    qkv_tensor = Steps(sem("qkv_tensor"), ["mean", "var", "qkv"])
    qkv_scalar = Steps(sem("qkv_scalar"), ["sq", "std", "qkv"])
    qkv_vector = Steps(sem("qkv_vector"), ["xc", "rstd", "xn"])
    score_tensor = Steps(sem("score_tensor"), [f"s{i}" for i in range(PAIRS)] + ["turn", "back"])
    score_scalar = Steps(sem("score_scalar"), ["s", "exp", "w"])
    score_vector = Steps(sem("score_vector"), ["rows"] + [f"prod{i}" for i in range(PAIRS)] + ["max", "sub", "sum", "rcp", "w"])
    mix_tensor = Steps(sem("mix_tensor"), [f"w{i}" for i in range(PAIRS)] + ["out"])
    mix_vector = Steps(sem("mix_vector"), [n for i in range(PAIRS) for n in ([f"m{i}"] + ([f"a{i}"] if i >= HC else []))] + ["res"])
    LOADS = 16 * 11

    with nc.Block() as block:
        @block.sync
        def _(sp):
            for dst, src in (
                (qkv_w[:], a["qkv_w"].rearrange("(c p) o -> p c o", p=P)),
                (pos_w[:], a["pos_w"].rearrange("(c p) o -> p c o", p=P)),
                (o_w[:], a["o_w"].rearrange("(c p) o -> p c o", p=P)),
                (pos_t[:], a["pos_t"].rearrange("(c p) o -> p c o", p=P)),
                (qkv_b[:], a["qkv_b"]), (pos_b[:], a["pos_b"]), (o_b[:], a["o_b"]), (r_w[:], a["r_w"]), (r_r[:], a["r_r"]),
                (heads[:], a["heads"]), (unheads[:], a["unheads"]),
            ):
                sp.dma_start(dst, src).then_inc(loaded, 16)

        @block.tensor
        def _(pe):
            def mm(o, w, x, first, last):
                return nc.tensor.matmul(o, w, x, start=first, stop=last)

            def scores(t):
                for i in range(PAIRS):
                    pe.wait_ge(score_vector.sem, score_vector.at(t, f"prod{i}"))
                    mm(ps[:, 0, :], heads[:, i, :], prod[:, i % 3, :], i == 0, i == PAIRS - 1).then_inc(score_tensor.sem, 1)

            def softmax(t):
                pe.wait_ge(score_scalar.sem, score_scalar.at(t, "s"))
                for n in range(4):
                    last = nc.tensor.transpose(ps[:, 1, n * P:(n + 1) * P], s_row[:, n * P:(n + 1) * P], ident[:])
                last.then_inc(score_tensor.sem, 1)
                pe.wait_ge(score_vector.sem, score_vector.at(t, "w"))
                for n in range(4):
                    last = nc.tensor.transpose(ps[:, 2, n * P:(n + 1) * P], s_tok[:, n, :], ident[:])
                last.then_inc(score_tensor.sem, 1)

            def mixing(t):
                pe.wait_ge(score_scalar.sem, score_scalar.at(t, "w"))
                for i in range(PAIRS):
                    if i >= 3:
                        pe.wait_ge(mix_vector.sem, mix_vector.at(t, f"m{i - 3}"))
                    mm(ps[:, 3 + i % 3, :], unheads[:, i, :], w_row[:], True, True).then_inc(mix_tensor.sem, 1)
                pe.wait_ge(mix_vector.sem, mix_vector.at(t, f"a{PAIRS - 1}"))
                for o in range(HC):
                    for c in range(HC):
                        last = mm(ps[:, 6 + o, :], o_w[:, c, o * P:(o + 1) * P], mix[:, c, :], c == 0, c == HC - 1)
                last.then_inc(mix_tensor.sem, 1)

            pe.wait_ge(loaded, LOADS)
            for o in range(HC):
                for c in range(HC):
                    last = mm(ps[:, o, 0:ROWS], pos_w[:, c, o * P:(o + 1) * P], pos_t[:, c, :], c == 0, c == HC - 1)
            last.then_inc(pos_tensor.sem, 1)
            pe.wait_ge(pos_vector.sem, pos_vector.at(0, "p_gap"))
            for i in range(PAIRS):
                s, c = divmod(i, HC)
                last = mm(ps[:, 2, 0:T], heads[:, i, :], p_gap[:, c, s:s + T], i == 0, i == PAIRS - 1)
            last.then_inc(pos_tensor.sem, 1)

            def project(t):
                for c in range(HC):
                    last = mm(ps[:, 0, :], means[:], hT[:, c, tok_cols(t)], c == 0, c == HC - 1)
                last.then_inc(qkv_tensor.sem, 1)
                pe.wait_ge(qkv_scalar.sem, qkv_scalar.at(t, "sq"))
                for c in range(HC):
                    last = mm(ps[:, 1, :], means[:], sq[:, c, :], c == 0, c == HC - 1)
                last.then_inc(qkv_tensor.sem, 1)
                pe.wait_ge(qkv_vector.sem, qkv_vector.at(t, "xn"))
                if not isinstance(t, int):
                    pe.wait_ge(qkv_scalar.sem, qkv_scalar.at(t - 1, "qkv"))
                for o in range(3 * HC):
                    for c in range(HC):
                        last = mm(ps[:, 2 + o, :], qkv_w[:, c, o * P:(o + 1) * P], xc[:, c, :], c == 0, c == HC - 1)
                last.then_inc(qkv_tensor.sem, 1)

            pe.wait_ge(pos_vector.sem, pos_vector.at(0, "gap"))
            project(0)
            with pe.Fori(1, T) as t:
                project(t)
            pe.wait_ge(qkv_scalar.sem, qkv_scalar.at(T - 1, "qkv"))
            scores(0)
            softmax(0)
            with pe.Fori(1, T) as t:
                scores(t)
                mixing(t - 1)
                softmax(t)
            mixing(T - 1)

        @block.scalar
        def _(act):
            act.wait_ge(loaded, LOADS)
            act.wait_ge(pos_tensor.sem, pos_tensor.at(0, "p"))
            for o in range(HC):
                last = nc.scalar.activation(p_row[:, o, :], ps[:, o, 0:ROWS], ACT.Identity, bias=pos_b[:, o:o + 1])
            last.then_inc(pos_scalar.sem, 1)
            act.wait_ge(pos_vector.sem, pos_vector.at(0, "bq"))
            with act.Fori(0, T) as t:
                act.wait_ge(qkv_vector.sem, qkv_vector.at(t, "xc"))
                nc.scalar.activation(sq[:], xc[:], ACT.Square).then_inc(qkv_scalar.sem, 1)
                act.wait_ge(qkv_tensor.sem, qkv_tensor.at(t, "var"))
                nc.scalar.activation(rstd[:], ps[:, 1, :], ACT.Sqrt, bias=eps[:, 0:1]).then_inc(qkv_scalar.sem, 1)
                act.wait_ge(qkv_tensor.sem, qkv_tensor.at(t, "qkv"))
                for o in range(3 * HC):
                    last = nc.scalar.activation(qkv[:, o, tok_cols(t)], ps[:, 2 + o, :], ACT.Identity, bias=qkv_b[:, o:o + 1])
                last.then_inc(qkv_scalar.sem, 1)
            act.wait_ge(pos_vector.sem, pos_vector.at(0, "gap"))
            with act.Fori(0, T) as t:
                act.wait_ge(score_tensor.sem, score_tensor.at(t, f"s{PAIRS - 1}"))
                nc.scalar.activation(s_row[:], ps[:, 0, :], ACT.Identity, scale=SCALE,
                                     bias=gap[:, bass.ds(T - 1 - t, 1)]).then_inc(score_scalar.sem, 1)
                act.wait_ge(score_vector.sem, score_vector.at(t, "sub"))
                nc.scalar.activation(s_tok[:], s_tok[:], ACT.Exp).then_inc(score_scalar.sem, 1)
                act.wait_ge(score_tensor.sem, score_tensor.at(t, "back"))
                nc.scalar.activation(w_row[:], ps[:, 2, :], ACT.Copy).then_inc(score_scalar.sem, 1)

        @block.vector
        def _(dve):
            V = nc.vector
            dve.wait_ge(loaded, LOADS)
            V.tensor_tensor(qkv_b[:, 0:HC], qkv_b[:, 0:HC], r_w[:], ALU.add).then_inc(pos_vector.sem, 1)
            V.tensor_tensor(r_r[:], r_r[:], r_w[:], ALU.subtract).then_inc(pos_vector.sem, 1)
            dve.wait_ge(pos_vector.sem, pos_vector.at(0, "gap_w"))
            dve.wait_ge(pos_scalar.sem, pos_scalar.at(0, "p"))
            for c in range(HC):
                last = V.tensor_scalar(p_gap[:, c, :], p_row[:, c, :], r_r[:, c:c + 1], None, ALU.mult)
            last.then_inc(pos_vector.sem, 1)
            dve.wait_ge(pos_tensor.sem, pos_tensor.at(0, "gap"))
            V.tensor_scalar(gap[:], ps[:, 2, 0:T], SCALE, None, ALU.mult).then_inc(pos_vector.sem, 1)
            with dve.Fori(0, T) as t:
                dve.wait_ge(qkv_tensor.sem, qkv_tensor.at(t, "mean"))
                V.tensor_tensor(xc[:], hT[:, :, tok_cols(t)], spread_over(ps[:, 0, :], HC), ALU.subtract).then_inc(qkv_vector.sem, 1)
                dve.wait_ge(qkv_scalar.sem, qkv_scalar.at(t, "std"))
                V.reciprocal(rstd[:], rstd[:]).then_inc(qkv_vector.sem, 1)
                dve.wait_ge(qkv_vector.sem, qkv_vector.at(t, "rstd"))
                V.tensor_tensor(xc[:], xc[:], spread_over(rstd[:], HC), ALU.mult).then_inc(qkv_vector.sem, 1)

            def scores(t):
                V.tensor_copy(p_t[:], p_row[:, :, bass.ds(T - 1 - t, T)]).then_inc(score_vector.sem, 1)
                dve.wait_ge(score_vector.sem, score_vector.at(t, "rows"))
                for i in range(PAIRS):
                    s, c = divmod(i, HC)
                    if i >= 3:
                        dve.wait_ge(score_tensor.sem, score_tensor.at(t, f"s{i - 3}"))
                    V.scalar_tensor_tensor(prod[:, i % 3, :], qkv[:, HC + c, tok_cols(s)], p_t[:, c, s:s + 1],
                                           qkv[:, c, tok_cols(t)], ALU.add, ALU.mult).then_inc(score_vector.sem, 1)

            def softmax(t):
                dve.wait_ge(score_tensor.sem, score_tensor.at(t, "turn"))
                by_head = ps[:, 1, :].rearrange("p (n s h) -> p n h s", n=4, s=T)
                V.tensor_reduce(peak[:], by_head, AX.X, ALU.max).then_inc(score_vector.sem, 1)
                dve.wait_ge(score_vector.sem, score_vector.at(t, "max"))
                for n in range(4):
                    last = V.tensor_tensor(s_tok[:, n, :].rearrange("p (s h) -> p s h", s=T),
                                           ps[:, 1, n * P:(n + 1) * P].rearrange("p (s h) -> p s h", s=T),
                                           peak[:, n:n + 1, :].to_broadcast([P, T, NH]), ALU.subtract)
                last.then_inc(score_vector.sem, 1)
                dve.wait_ge(score_scalar.sem, score_scalar.at(t, "exp"))
                V.tensor_reduce(total[:], s_tok[:].rearrange("p n (s h) -> p n h s", s=T), AX.X, ALU.add).then_inc(score_vector.sem, 1)
                dve.wait_ge(score_vector.sem, score_vector.at(t, "sum"))
                V.reciprocal(total[:], total[:]).then_inc(score_vector.sem, 1)
                dve.wait_ge(score_vector.sem, score_vector.at(t, "rcp"))
                for n in range(4):
                    v = s_tok[:, n, :].rearrange("p (s h) -> p s h", s=T)
                    last = V.tensor_tensor(v, v, total[:, n:n + 1, :].to_broadcast([P, T, NH]), ALU.mult)
                last.then_inc(score_vector.sem, 1)

            def mixing(t):
                for i in range(PAIRS):
                    s, c = divmod(i, HC)
                    dve.wait_ge(mix_tensor.sem, mix_tensor.at(t, f"w{i}"))
                    dst = mix[:, c, :] if s == 0 else part[:, i % 2, :]
                    V.tensor_tensor(dst, qkv[:, 2 * HC + c, tok_cols(s)], ps[:, 3 + i % 3, :], ALU.mult).then_inc(mix_vector.sem, 1)
                    if s:
                        dve.wait_ge(mix_vector.sem, mix_vector.at(t, f"m{i}"))
                        V.tensor_tensor(mix[:, c, :], mix[:, c, :], part[:, i % 2, :], ALU.add).then_inc(mix_vector.sem, 1)
                dve.wait_ge(mix_tensor.sem, mix_tensor.at(t, "out"))
                for c in range(HC):
                    last = V.scalar_tensor_tensor(hT[:, c, tok_cols(t)], ps[:, 6 + c, :], o_b[:, c:c + 1],
                                                  hT[:, c, tok_cols(t)], ALU.add, ALU.add)
                last.then_inc(mix_vector.sem, 1)

            dve.wait_ge(qkv_scalar.sem, qkv_scalar.at(T - 1, "qkv"))
            scores(0)
            softmax(0)
            with dve.Fori(1, T) as t:
                scores(t)
                mixing(t - 1)
                softmax(t)
            mixing(T - 1)


def modulated_ffn(nc, ctx, a, out, hT, means, eps, ps):
    E, F, J = 8, 1024, 16
    FC = F // P
    COLS = H * F // J
    PIECE = 4 * 512
    NP = COLS // PIECE
    PIECES = 2 * NP

    def sb(name, shape, dt=F32):
        return ctx.enter_context(nc.sbuf_tensor(name, shape, dt))

    def sem(name):
        return ctx.enter_context(nc.semaphore(name))

    g1_w = sb("g1_w", [P, HC, H])
    g1_b = sb("g1_b", [P, HC])
    g2_rep = sb("g2_rep", [P, HC, P])
    g2_rep_b = sb("g2_rep_b", [P, 1])
    g2_w = sb("g2_w", [P, HC, E])
    g2_b = sb("g2_b", [E, 1])
    same = sb("same", [P, B, J])
    base = sb("base", [P, P])
    tb1 = sb("tb1", [E, F])
    tb2 = sb("tb2", [E, H])
    b1 = sb("b1", [P, FC])
    b2 = sb("b2", [P, HC])
    msum = sb("msum", [P, HC, B])
    g_rep = sb("g_rep", [P, B])
    g_e = sb("g_e", [E, B])
    kron = sb("kron", [P, B, J])
    mb = sb("mb", [P, FC + HC, B])
    xn = sb("xn_f", [P, HC, B * S])
    sq = sb("sq_f", [P, HC, S])
    rstd = sb("rstd_f", [P, S])
    tw = sb("tw", [P, 2, PIECE])
    w_base = sb("w_base", [P, 2, PIECE])
    mixed = sb("mixed", [P, 2, PIECE])
    w1 = sb("w1", [P, 2, HC, F])
    w2 = sb("w2", [P, 2, FC, H])
    hid = sb("hid", [P, FC, S])
    res = sb("res", [P, 2, HC, S])
    own_w = [nc.dram_tensor(f"own_w{n}", [P, COLS], F32, kind="Internal").ap() for n in (1, 2)]

    loaded, base_zeroed, weight_zeroed = sem("loaded_f"), sem("base_zeroed"), sem("weight_zeroed")
    tw_loaded, own_stored, own_loaded, stored = (
        [sem(f"{name}{i}") for i in range(2)] for name in ("tw_loaded", "own_stored", "own_loaded", "stored"))
    norm_tensor = Steps(sem("norm_tensor"), ["mean", "var", "gate"])
    norm_scalar = Steps(sem("norm_scalar"), ["sq", "std", "sum"])
    norm_vector = Steps(sem("norm_vector"), ["xc", "rstd", "xn"])
    gate_tensor = Steps(sem("gate_tensor"), ["g", "b"])
    gate_scalar = Steps(sem("gate_scalar"), ["g"])
    gate_vector = Steps(sem("gate_vector"), ["kron", "mb1", "mb2"])
    weight_tensor = Steps(sem("weight_tensor"), ["w"])
    weight_copied = Steps(sem("weight_copied"), ["w"])
    ffn_tensor = Steps(sem("ffn_tensor"), [n for f in range(FC) for n in [f"up{f}"]] + ["down"])
    ffn_scalar = Steps(sem("ffn_scalar"), [f"gelu{f}" for f in range(FC)])
    ffn_vector = Steps(sem("ffn_vector"), ["res"])
    LOADS = 16 * 12

    with nc.Block() as block:
        @block.sync
        def _(sp):
            sp.wait_ge(base_zeroed, 1)
            for dst, src in (
                (g1_w[:], a["g1_w"].rearrange("(c p) o -> p c o", p=P)), (g1_b[:], a["g1_b"]),
                (g2_rep[:], a["g2_rep"].rearrange("(c p) o -> p c o", p=P)), (g2_rep_b[:], a["g2_rep_b"]),
                (g2_w[:], a["g2_w"].rearrange("(c p) o -> p c o", p=P)), (g2_b[:], a["g2_b"]),
                (same[:], a["same"]), (base[0:J, :], a["same"][0:J].rearrange("p b j -> p (b j)")),
                (tb1[:], a["tb1"]), (tb2[:], a["tb2"]), (b1[:], a["b1"]), (b2[:], a["b2"]),
            ):
                sp.dma_start(dst, src).then_inc(loaded, 16)
            sp.wait_ge(weight_zeroed, 1)
            for n in range(PIECES):
                if n >= 2:
                    sp.wait_ge(weight_tensor.sem, weight_tensor.at(n - 2, "w"))
                cols = slice(n % NP * PIECE, (n % NP + 1) * PIECE)
                sp.dma_start(tw[:, n % 2, :], a["tw1" if n < NP else "tw2"][:, cols]).then_inc(tw_loaded[n % 2], 16)
                sp.dma_start(w_base[0:J, n % 2, :], a["fw1" if n < NP else "fw2"][:, cols]).then_inc(tw_loaded[n % 2], 16)
            for i in range(2):
                sp.wait_ge(own_stored[i], 16 * PIECES // 2)
            for b in range(B):
                if b >= 2:
                    sp.wait_ge(ffn_tensor.sem, ffn_tensor.at(b - 2, "down"))
                mine = slice(b * J, (b + 1) * J)
                sp.dma_start(w1[:, b % 2], own_w[0][mine, :].rearrange("j (i f) -> (j i) f", f=F)
                             .rearrange("(c p) f -> p c f", p=P)).then_inc(own_loaded[b % 2], 16)
                sp.dma_start(w2[:, b % 2], own_w[1][mine, :].rearrange("j (i h) -> (j i) h", h=H)
                             .rearrange("(c p) h -> p c h", p=P)).then_inc(own_loaded[b % 2], 16)

        @block.gpsimd
        def _(pool):
            nc.gpsimd.memset(base[:], 0.0).then_inc(base_zeroed, 1)
            nc.gpsimd.memset(w_base[:], 0.0).then_inc(weight_zeroed, 1)
            for n in range(PIECES):
                cols = slice(n % NP * PIECE, (n % NP + 1) * PIECE)
                pool.wait_ge(weight_copied.sem, weight_copied.at(n, "w"))
                pool.dma_start(own_w[n // NP][:, cols], mixed[:, n % 2, :]).then_inc(own_stored[n % 2], 16)
            for b in range(B):
                pool.wait_ge(ffn_vector.sem, ffn_vector.at(b, "res"))
                pool.dma_start(out[:, :, b * S:(b + 1) * S].rearrange("c p s -> p c s"), res[:, b % 2]).then_inc(stored[b % 2], 16)
            for i in range(2):
                pool.wait_ge(stored[i], 16 * B // 2)

        @block.tensor
        def _(pe):
            def mm(o, w, x, first, last):
                return nc.tensor.matmul(o, w, x, start=first, stop=last)

            pe.wait_ge(loaded, LOADS)

            def norm(b):
                if not isinstance(b, int):
                    pe.wait_ge(norm_vector.sem, norm_vector.at(b - 1, "xc"))
                for c in range(HC):
                    last = mm(ps[:, 0, :], means[:], hT[:, c, tok_cols(b)], c == 0, c == HC - 1)
                last.then_inc(norm_tensor.sem, 1)
                pe.wait_ge(norm_scalar.sem, norm_scalar.at(b, "sq"))
                for c in range(HC):
                    last = mm(ps[:, 1, :], means[:], sq[:, c, :], c == 0, c == HC - 1)
                last.then_inc(norm_tensor.sem, 1)
                pe.wait_ge(norm_vector.sem, norm_vector.at(b, "xn"))
                if not isinstance(b, int):
                    pe.wait_ge(norm_scalar.sem, norm_scalar.at(b - 1, "sum"))
                for o in range(HC):
                    for c in range(HC):
                        last = mm(ps[:, 2 + o, :], g1_w[:, c, o * P:(o + 1) * P], xn[:, c, tok_cols(b)], c == 0, c == HC - 1)
                last.then_inc(norm_tensor.sem, 1)

            norm(0)
            with pe.Fori(1, B) as b:
                norm(b)
            pe.wait_ge(norm_scalar.sem, norm_scalar.at(B - 1, "sum"))
            for c in range(HC):
                mm(ps[:, 0, 0:B], g2_rep[:, c, :], msum[:, c, :], c == 0, c == HC - 1)
            for c in range(HC):
                last = mm(ps[0:E, 1, 0:B], g2_w[:, c, :], msum[:, c, :], c == 0, c == HC - 1)
            last.then_inc(gate_tensor.sem, 1)
            pe.wait_ge(gate_scalar.sem, gate_scalar.at(0, "g"))
            for f in range(FC):
                mm(ps[:, 2, f * B:(f + 1) * B], tb1[:, f * P:(f + 1) * P], g_e[:], True, True)
            for c in range(HC):
                last = mm(ps[:, 3, c * B:(c + 1) * B], tb2[:, c * P:(c + 1) * P], g_e[:], True, True)
            last.then_inc(gate_tensor.sem, 1)
            pe.wait_ge(gate_vector.sem, gate_vector.at(0, "mb2"))
            for n in range(PIECES):
                pe.wait_ge(tw_loaded[n % 2], 32 * (n // 2 + 1))
                if n >= 2:
                    pe.wait_ge(weight_copied.sem, weight_copied.at(n - 2, "w"))
                for i in range(4):
                    cols = slice(i * 512, (i + 1) * 512)
                    bank = 4 * (n % 2) + i
                    mm(ps[:, bank, :], kron[:].rearrange("p b j -> p (b j)"), tw[:, n % 2, cols], True, False)
                    last = mm(ps[:, bank, :], base[:], w_base[:, n % 2, cols], False, True)
                last.then_inc(weight_tensor.sem, 1)
            pe.wait_ge(weight_copied.sem, weight_copied.at(PIECES - 1, "w"))
            for b in range(B):
                pe.wait_ge(own_loaded[b % 2], 32 * (b // 2 + 1))
                for f in range(FC):
                    if f >= 4:
                        pe.wait_ge(ffn_scalar.sem, ffn_scalar.at(b, f"gelu{f - 4}"))
                    elif b:
                        pe.wait_ge(ffn_scalar.sem, ffn_scalar.at(b - 1, f"gelu{f + 4}"))
                    for c in range(HC):
                        last = mm(ps[:, f % 4, :], w1[:, b % 2, c, f * P:(f + 1) * P], xn[:, c, tok_cols(b)], c == 0, c == HC - 1)
                    last.then_inc(ffn_tensor.sem, 1)
                if b >= 2:
                    pe.wait_ge(ffn_vector.sem, ffn_vector.at(b - 2, "res"))
                for f in range(FC):
                    pe.wait_ge(ffn_scalar.sem, ffn_scalar.at(b, f"gelu{f}"))
                    for o in range(HC):
                        last = mm(ps[:, 4 + 2 * (b % 2) + o, :], w2[:, b % 2, f, o * P:(o + 1) * P], hid[:, f, :], f == 0, f == FC - 1)
                last.then_inc(ffn_tensor.sem, 1)

        @block.scalar
        def _(act):
            act.wait_ge(loaded, LOADS)
            with act.Fori(0, B) as b:
                act.wait_ge(norm_vector.sem, norm_vector.at(b, "xc"))
                nc.scalar.activation(sq[:], xn[:, :, tok_cols(b)], ACT.Square).then_inc(norm_scalar.sem, 1)
                act.wait_ge(norm_tensor.sem, norm_tensor.at(b, "var"))
                nc.scalar.activation(rstd[:], ps[:, 1, :], ACT.Sqrt, bias=eps[:, 0:1]).then_inc(norm_scalar.sem, 1)
                act.wait_ge(norm_tensor.sem, norm_tensor.at(b, "gate"))
                act.wait_ge(norm_scalar.sem, norm_scalar.at(b, "std"))
                for o in range(HC):
                    last = nc.scalar.activation(hid[:, o, :], ps[:, 2 + o, :], ACT.Relu, bias=g1_b[:, o:o + 1],
                                                accum_out=msum[:, o, bass.ds(b, 1)])
                last.then_inc(norm_scalar.sem, 1)
            act.wait_ge(gate_tensor.sem, gate_tensor.at(0, "g"))
            nc.scalar.activation(g_rep[:], ps[:, 0, 0:B], ACT.Identity, scale=1.0 / S, bias=g2_rep_b[:, 0:1])
            nc.scalar.activation(g_e[:], ps[0:E, 1, 0:B], ACT.Identity, scale=1.0 / S, bias=g2_b[:, 0:1]).then_inc(gate_scalar.sem, 1)
            for b in range(B):
                if b == 0:
                    act.wait_ge(gate_vector.sem, gate_vector.at(0, "mb2"))
                for f in range(FC):
                    act.wait_ge(ffn_tensor.sem, ffn_tensor.at(b, f"up{f}"))
                    if f == 0 and b:
                        act.wait_ge(ffn_tensor.sem, ffn_tensor.at(b - 1, "down"))
                    nc.scalar.activation(hid[:, f, :], ps[:, f % 4, :], ACT.Gelu_apprx_tanh, bias=mb[:, f, b:b + 1]).then_inc(ffn_scalar.sem, 1)

        @block.vector
        def _(dve):
            V = nc.vector
            dve.wait_ge(loaded, LOADS)
            with dve.Fori(0, B) as b:
                dve.wait_ge(norm_tensor.sem, norm_tensor.at(b, "mean"))
                V.tensor_tensor(xn[:, :, tok_cols(b)], hT[:, :, tok_cols(b)], spread_over(ps[:, 0, :], HC), ALU.subtract).then_inc(norm_vector.sem, 1)
                dve.wait_ge(norm_scalar.sem, norm_scalar.at(b, "std"))
                V.reciprocal(rstd[:], rstd[:]).then_inc(norm_vector.sem, 1)
                dve.wait_ge(norm_vector.sem, norm_vector.at(b, "rstd"))
                V.tensor_tensor(xn[:, :, tok_cols(b)], xn[:, :, tok_cols(b)], spread_over(rstd[:], HC), ALU.mult).then_inc(norm_vector.sem, 1)
            dve.wait_ge(gate_scalar.sem, gate_scalar.at(0, "g"))
            V.tensor_tensor(kron[:], same[:], g_rep[:].rearrange("p (b o) -> p b o", o=1).to_broadcast([P, B, J]), ALU.mult).then_inc(gate_vector.sem, 1)
            dve.wait_ge(gate_tensor.sem, gate_tensor.at(0, "b"))
            V.tensor_tensor(mb[:, 0:FC, :], ps[:, 2, 0:FC * B].rearrange("p (f b) -> p f b", b=B),
                            b1[:].rearrange("p (f o) -> p f o", o=1).to_broadcast([P, FC, B]), ALU.add).then_inc(gate_vector.sem, 1)
            V.tensor_tensor(mb[:, FC:, :], ps[:, 3, 0:HC * B].rearrange("p (f b) -> p f b", b=B),
                            b2[:].rearrange("p (f o) -> p f o", o=1).to_broadcast([P, HC, B]), ALU.add).then_inc(gate_vector.sem, 1)
            for n in range(PIECES):
                dve.wait_ge(weight_tensor.sem, weight_tensor.at(n, "w"))
                if n >= 2:
                    dve.wait_ge(own_stored[n % 2], 16 * (n // 2))
                half = 4 * (n % 2)
                V.tensor_copy(mixed[:, n % 2, :], ps[:, half:half + 4, :].rearrange("p a b -> p (a b)")).then_inc(weight_copied.sem, 1)
            dve.wait_ge(gate_vector.sem, gate_vector.at(0, "mb2"))
            for b in range(B):
                dve.wait_ge(ffn_tensor.sem, ffn_tensor.at(b, "down"))
                if b >= 2:
                    dve.wait_ge(stored[b % 2], 16 * (b // 2))
                for c in range(HC):
                    last = V.scalar_tensor_tensor(res[:, b % 2, c, :], ps[:, 4 + 2 * (b % 2) + c, :], mb[:, FC + c, b:b + 1],
                                                  hT[:, c, tok_cols(b)], ALU.add, ALU.add)
                last.then_inc(ffn_vector.sem, 1)


def lay_out(i):
    f = lambda n: np.asarray(i[n])
    a = {}
    B,S,H,D = f('x').shape
    x = f('x').transpose(0,3,2,1).reshape(B, D*H//P, P, S).transpose(0,2,1,3)
    a['x'] = np.ascontiguousarray(x)
    a['ident'] = np.eye(P, dtype=np.float32)
    a['means'] = np.full((P,P), 1/H, np.float32)
    a['eps'] = np.full((P,1), 1e-5, np.float32)
    a['ws_t'] = f('L0_tok_weighted_sum').T
    a['tok_v'] = f('L0_tok_weight').T
    a['w_in'] = f('L0_attn_W_in'); a['w_out'] = f('L0_attn_W_out')
    wx = f('L0_attn_W_xproj'); bcw = wx[:, 16:]
    a['w_x'] = np.concatenate([bcw, bcw, bcw, wx[:, :16]], 1)
    a['w_dt'] = f('L0_attn_W_dt')
    a['up'] = f('L0_ffn_expert_up').transpose(1,0,2).reshape(H, -1)
    a['down'] = f('L0_ffn_expert_down')
    a['sup'] = f('L0_ffn_shared_up'); a['sdown'] = f('L0_ffn_shared_down')
    a['gate'] = f('L0_ffn_gate_weight').T
    ch = lambda v: np.moveaxis(v.reshape((-1, P) + v.shape[1:]), 0, 1)
    a['taps'] = ch(f('L0_attn_conv_w')[:,0,:]); a['tap_b'] = ch(f('L0_attn_conv_b')); a['b_dt'] = ch(f('L0_attn_b_dt'))
    a['d_skip'] = ch(f('L0_attn_D_skip')); a['a_log'] = ch(f('L0_attn_A_log'))
    E=16
    a['lower'] = np.broadcast_to(np.tril(np.ones((E,E),np.float32), -1), (P,E,E))
    a['picks'] = np.zeros((P, 48), np.float32)
    for part in range(3):
        a['picks'][32 * part:32 * part + 32, 0:32] = np.eye(32)
        a['picks'][16 * part:16 * part + 16, 32:48] = np.eye(16)
    fl = lambda v: ch(np.asarray(v).reshape(-1))
    a['qkv_w'] = f('L1_attn_in_proj_weight').T; a['qkv_b'] = fl(f('L1_attn_in_proj_bias'))
    a['pos_w'] = f('L1_attn_pos_proj_weight').T; a['pos_b'] = fl(f('L1_attn_pos_proj_bias'))
    a['o_w'] = f('L1_attn_out_proj_weight').T; a['o_b'] = fl(f('L1_attn_out_proj_bias'))
    a['pos_t'] = f('L1_attn_pos')[:15, 0].T
    a['r_w'] = fl(f('L1_attn_r_w_bias')); a['r_r'] = fl(f('L1_attn_r_r_bias'))
    hd = np.zeros((P, 8, 2, 8, 16), np.float32)
    for s in range(8):
        for c in range(2):
            for p in range(P): hd[p, s, c, s, c*8 + p//16] = 1
    hd = hd.reshape(P, 16, P)
    a['heads'] = hd; a['unheads'] = hd.transpose(2,1,0)
    a['g1_w'] = f('L1_ffn_gate_w1').T; a['g1_b'] = fl(f('L1_ffn_gate_b1'))
    g2 = f('L1_ffn_gate_w2')
    a['g2_rep'] = np.repeat(g2.T, 16, 1); a['g2_rep_b'] = np.repeat(f('L1_ffn_gate_b2'), 16)[:,None]
    a['g2_w'] = g2.T; a['g2_b'] = f('L1_ffn_gate_b2')[:,None]
    a['same'] = np.broadcast_to(np.tile(np.eye(16, dtype=np.float32), (8,1))[:,None,:], (P,8,16))
    a['tb1'] = f('L1_ffn_Tb1'); a['tb2'] = f('L1_ffn_Tb2')
    a['b1'] = fl(f('L1_ffn_b1')); a['b2'] = fl(f('L1_ffn_b2'))
    a['tw1'] = f('L1_ffn_TW1').transpose(0,2,1).reshape(P, -1); a['fw1'] = f('L1_ffn_W1').T.reshape(16, -1)
    a['tw2'] = f('L1_ffn_TW2').transpose(0,2,1).reshape(P, -1); a['fw2'] = f('L1_ffn_W2').T.reshape(16, -1)
    return {k: np.ascontiguousarray(v) for k,v in a.items()}


def kernel(**inputs):
    import concourse.bacc as _bacc
    from concourse.bass_utils import run_bass_kernel_spmd as _run

    nc = _bacc.Bacc("TRN2", target_bir_lowering=False, num_devices=1)
    arrays, aps = {}, {}
    for name, a in lay_out(inputs).items():
        arrays[f"in_{name}_dram"] = a
        aps[name] = nc.dram_tensor(f"in_{name}_dram", a.shape, mybir.dt.from_np(a.dtype), kind="ExternalInput").ap()
    out = nc.dram_tensor("out_0_dram", (HC, P, B * S), F32, kind="ExternalOutput").ap()
    vit_tower(nc, aps, out)
    r = _run(nc, [arrays], core_ids=[0])
    got = r.results[0]["out_0_dram"]
    return np.ascontiguousarray(got.reshape(H, B, S).transpose(1, 2, 0))
```

```python
from contextlib import ExitStack

import numpy as np
import concourse.bass as bass
from concourse import mybir

F32 = mybir.dt.float32
BF16 = mybir.dt.bfloat16
ALU = mybir.AluOpType
ACT = mybir.ActivationFunctionType
AX = mybir.AxisListType

P = 128
B, S, H = 8, 512, 256
HC = H // P
TOKD = 4
XC = H * TOKD // P
DI = 2 * H
DC = DI // P
NS = 16
TAPS = 4
E = 16
EI = 128
SC = 4
NG = 4
TOPK = 4
KSTEP = 2 * NS
MOE = SC + E
EPS = 1e-5


class Steps:

    def __init__(self, sem, names):
        self.sem = sem
        self.names = list(names)
        self.index = {n: k + 1 for k, n in enumerate(self.names)}
        assert len(self.index) == len(self.names)

    def at(self, rnd, name):
        return rnd * len(self.names) + self.index[name]


def tok_cols(b):
    return slice(b * S, (b + 1) * S) if isinstance(b, int) else bass.ts(b, S)


def spread_over(ap, n):
    return ap.rearrange("p (a b) -> p a b", a=1).to_broadcast([ap.shape[0], n, ap.shape[1]])


def vit_tower(nc, a, out):
    with ExitStack() as ctx:
        def sb(name, shape, dt=F32):
            return ctx.enter_context(nc.sbuf_tensor(name, shape, dt))

        def sem(name):
            return ctx.enter_context(nc.semaphore(name))

        hT = sb("hT", [P, HC, B * S])
        ident = sb("ident", [P, P])
        means = sb("means", [P, P])
        eps = sb("eps", [P, 1])
        ps = ctx.enter_context(nc.psum_tensor("ps", [P, 8, 512], F32))
        x_in = sb("x_in", [P, XC // 2, S])
        x_flat = x_in[:].rearrange("p a b -> p (a b)")
        qkv_w = x_flat[:, 0:HC * 3 * H].rearrange("p (c o) -> p c o", c=HC)
        o_w = x_flat[:, HC * 3 * H:HC * 4 * H].rearrange("p (c o) -> p c o", c=HC)
        proj_loaded = sem("proj_loaded")
        with ExitStack() as one:
            mamba_and_experts(nc, one, a, hT, ident, means, eps, ps, x_in, qkv_w, o_w, proj_loaded)
        g1_w = sb("g1_w", [P, HC, H])
        g1_b = sb("g1_b", [P, HC])
        gate_loaded = sem("gate_loaded")
        with ExitStack() as two:
            attention(nc, two, a, hT, ident, means, eps, ps, qkv_w, o_w, proj_loaded, g1_w, g1_b, gate_loaded)
        with ExitStack() as three:
            modulated_ffn(nc, three, a, out, hT, means, eps, ps, x_in[:].rearrange("p (a c) s -> p a c s", c=HC), g1_w, g1_b, gate_loaded)


def tensor_scan_parts(k):
    parts = []
    if 0 <= k < KSTEP:
        parts.append(("C", k))
    if 1 <= k <= KSTEP:
        parts.append(("Y", k - 1))
    if -1 <= k < KSTEP - 1:
        parts.append(("B", k + 1))
    return parts


def mamba_and_experts(nc, ctx, a, hT, ident, means, eps, ps, x_in, qkv_w, o_w, proj_loaded):
    def sb(name, shape, dt=F32):
        return ctx.enter_context(nc.sbuf_tensor(name, shape, dt))

    def sem(name):
        return ctx.enter_context(nc.semaphore(name))

    tok_w = sb("tok_w", [P, XC, H])
    w_in = sb("w_in", [P, HC, 2 * DI])
    w_out = sb("w_out", [P, DC, H])
    w_x = sb("w_x", [P, DC, 112])
    w_dt = sb("w_dt", [P, DI])
    up_w = sb("up_w", [P, HC, E * EI])
    down_w = sb("down_w", [P, E, H])
    sup_w = sb("sup_w", [P, HC, SC * P])
    sdown_w = sb("sdown_w", [P, SC, H])
    gate_w = sb("gate_w", [P, HC, E])
    taps = sb("taps", [P, DC, TAPS])
    tap_b = sb("tap_b", [P, DC])
    b_dt = sb("b_dt", [P, DC])
    d_skip = sb("d_skip", [P, DC])
    a_neg = sb("a_neg", [P, DC, NS])
    pick_state = sb("pick_state", [96, 2 * NS], BF16)
    pick_expert = sb("pick_expert", [P, E], BF16)
    picks_f = sb("picks_f", [P, 2 * NS + E])
    identb = sb("identb", [P, P], BF16)
    lower = sb("lower", [P, E, E])

    u_raw = sb("u_raw", [P, DC, S])
    z_raw = sb("z_raw", [P, DC, S])
    u = sb("u", [P, DC, S])
    zg = sb("zg", [P, DC, S])
    delta = sb("delta", [P, DC, S])
    du = sb("du", [P, DC, S])
    bc = sb("bc", [96, S], BF16)
    mx = sb("mx", [P, HC, S])
    comb_t = sb("comb_t", [P, S], BF16)
    m_act = sb("m_act", [P, 2, S])
    sc = sb("sc", [P, 4 * E])
    comb = sb("comb", [P, 4, E])
    comb_p = sb("comb_p", [P, 4, P // E, E], BF16)

    def viewer(region):
        def view(at, *shape):
            n = int(np.prod(shape))
            v = region[:, at:at + n]
            if len(shape) == 2:
                v = v.rearrange("p (a b) -> p a b", a=shape[0])
            if len(shape) == 3:
                v = v.rearrange("p (a b c) -> p a b c", a=shape[0], b=shape[1])
            return v
        return view

    view = viewer(sb("scan_region", [P, 5120]))
    dA = view(0, 2, 2, S)
    hs = view(2048, 2, S)
    hC = view(3072, 2, 2, S)
    th = view(0, DC, S)
    x_first_hi = view(0, XC // 2, S)
    thz = view(2048, DC, S)
    r_bc = view(4096, S)
    dtl = view(4608, S)
    view = viewer(sb("front_region", [P, 2 * S + DC * (S + TAPS - 1)]))
    xc = view(0, HC, S)
    sq = view(2 * S, HC, S)
    xpad = view(2 * S, DC, S + TAPS - 1)
    view = viewer(sb("route_region", [P, 1616]))
    r_sq = view(0, HC, S)
    c_gt = view(0, 2, E * E)
    c_eq = view(512, 2, E * E)
    pairs = view(1024, 6, 4 * NG)
    gsum = view(1120, 4 * NG)
    g_gt = view(1136, 4, NG * NG)
    g_eq = view(1200, 4, NG * NG)
    grank = view(1264, 4 * NG)
    masked = view(1280, 4 * E)
    rank = view(1344, 4 * E)
    wsum = view(1408, 4)
    wres = view(1412, 4 * E)
    inv = sb("inv", [P, 2, 4])

    ws_t = u_raw[:, 0:1, :].rearrange("p a (c o) -> p (a c) o", c=HC)
    v_rep = u_raw[:, 1:3, :].rearrange("p a (c o) -> p (a c) o", c=2)

    tok_loaded, loaded, experts_loaded, down_loaded = (
        sem(n) for n in ("tok_loaded", "loaded", "experts_loaded", "down_loaded"))
    x_loaded = [sem(f"x_loaded_{n}") for n in ("lo", "hi")]
    setup_vector = Steps(sem("setup_vector"), [f"tok{k}" for k in range(XC)]
                         + ["tap", "tapb", "cap", "aneg", "identb", "pick_state", "pick_expert", "pad"])
    setup_scalar = Steps(sem("setup_scalar"), ["aexp"])
    front_tensor = Steps(sem("front_tensor"), ["tok_lo", "tok", "mean", "var", "inv", "x0", "x1", "z0", "z1"])
    front_scalar = Steps(sem("front_scalar"), ["h", "sq", "std", "x0", "conv00", "x1", "conv10", "z0", "z1"])
    front_vector = Steps(sem("front_vector"), ["xc", "inv", "pad", "xn"] + [f"conv{p}{j}" for p in range(2) for j in range(1, TAPS)])
    entry_tensor = Steps(sem("entry_tensor"), ["bcdt"] + [f"dt{c}" for c in range(DC)])
    entry_scalar = Steps(sem("entry_scalar"), ["thu", "thz", "dtl"] + [f"abs{c}" for c in range(DC)] + ["exp", "ln0", "ln1"])
    entry_vector = Steps(sem("entry_vector"), ["u", "bc1", "r1", "bc2", "r2", "bc3"] + [f"pos{c}" for c in range(DC)]
                         + ["zg", "delta0", "du0", "delta1", "du1"])
    scan_tensor = Steps(sem("scan_tensor"), [f"{name}{at}" for k in range(-1, KSTEP + 1) for name, at in tensor_scan_parts(k)]
                        + ["proj"])
    scan_scalar = Steps(sem("scan_scalar"), [f"dA{k}" for k in range(KSTEP)])
    scan_vector = Steps(sem("scan_vector"), [n for k in range(KSTEP) for n in
                                             [f"dBu{k}", f"scan{k}"] + (["skip0", "gated0"] if k == NS else []) + [f"hC{k}"]]
                        + ["skip1", "gated1", "res"])
    route_tensor = Steps(sem("route_tensor"), ["mean", "var", "inv", "gate", "turn"])
    route_scalar = Steps(sem("route_scalar"), ["sq", "std", "e", "comb_t"])
    route_vector = Steps(sem("route_vector"), ["xc", "inv", "xn", "s1", "s", "p0", "p1", "p2", "p3", "p4", "p5", "gs", "ggt", "geq",
                                               "geql", "gsumr", "gr", "gm", "msk", "cgt0", "ceq0", "ceql0", "csum0", "cr0",
                                               "cgt1", "ceq1", "ceql1", "csum1", "cr1", "w", "ws",
                                               "wr", "rcp", "comb", "k1", "q1", "k2", "q2", "k3"])
    expert_tensor = Steps(sem("expert_tensor"), [n for j in range(MOE + 2) for n in
                                                 ([f"dn{j - 2}"] if j >= 2 else [])
                                                 + (([f"up{j}"] + ([f"cb{j}"] if j >= SC else [])) if j < MOE else [])])
    expert_scalar = Steps(sem("expert_scalar"), [f"th{j}" for j in range(MOE)])
    expert_vector = Steps(sem("expert_vector"), [n for j in range(MOE) for n in ([f"a{j}"] + ([f"c{j}"] if j >= SC else []))] + ["res"])

    TOK_LOADS, LOADS, EXPERT_LOADS = 16 * 5, 16 * 11, 16 * 4
    MOE_AT = KSTEP - MOE
    DT_BANKS = (4, 5, 0, 1)
    TURN_AT = MOE_AT + SC - 1
    SHARED_BESIDE = (7, 8, 10, 12)

    def x_tile(b, hi):
        return x_first_hi if hi and isinstance(b, int) and b == 0 else x_in[:]

    with nc.Block() as block:
        @block.sync
        def _(sp):
            half = XC // 2

            def load_x(b, hi):
                if hi and b:
                    sp.wait_ge(front_tensor.sem, front_tensor.at(b, "tok_lo"))
                elif b:
                    sp.wait_ge(front_tensor.sem, front_tensor.at(b - 1, "tok"))
                sp.dma_start(x_tile(b, hi), a["x"][b][:, hi * half:(hi + 1) * half, :]).then_inc(x_loaded[hi], 16)

            for dst, src in (
                (ws_t, a["ws_t"].rearrange("(c p) o -> p c o", p=P)),
                (v_rep, a["tok_v"].rearrange("(n d) o -> n d o", n=1).to_broadcast([P, TOKD, H])),
                (ident[:], a["ident"]), (means[:], a["means"]), (eps[:], a["eps"]),
            ):
                sp.dma_start(dst, src).then_inc(tok_loaded, 16)
            load_x(0, 0)
            load_x(0, 1)
            for dst, src in (
                (w_in[:], a["w_in"].rearrange("(c p) o -> p c o", p=P)),
                (taps[:], a["taps"]), (tap_b[:], a["tap_b"]), (b_dt[:], a["b_dt"]), (d_skip[:], a["d_skip"]),
                (a_neg[:], a["a_log"]), (lower[:], a["lower"]), (picks_f[:], a["picks"]),
                (w_x[:], a["w_x"].rearrange("(c p) o -> p c o", p=P)),
                (w_dt[96:112, :], a["w_dt"]),
                (w_out[:], a["w_out"].rearrange("(c p) o -> p c o", p=P)),
            ):
                sp.dma_start(dst, src).then_inc(loaded, 16)
            for dst, src in (
                (gate_w[:], a["gate"].rearrange("(c p) o -> p c o", p=P)),
                (sup_w[:], a["sup"].rearrange("(c p) o -> p c o", p=P)),
                (sdown_w[:], a["sdown"].rearrange("(c p) o -> p c o", p=P)),
                (up_w[:], a["up"].rearrange("(c p) o -> p c o", p=P)),
            ):
                sp.dma_start(dst, src).then_inc(experts_loaded, 16)
            for b in range(1, B):
                load_x(b, 0)
                load_x(b, 1)
            sp.wait_ge(front_tensor.sem, front_tensor.at(B - 1, "tok"))
            for dst, name in ((qkv_w, "qkv_w"), (o_w, "o_w")):
                sp.dma_start(dst, a[name].rearrange("(c p) o -> p c o", p=P)).then_inc(proj_loaded, 16)

        @block.gpsimd
        def _(pool):
            pool.wait_ge(front_tensor.sem, front_tensor.at(0, "tok"))
            pool.dma_start(down_w[:], a["down"].rearrange("e p o -> p e o")).then_inc(down_loaded, 16)

        @block.scalar
        def _(act):
            A = nc.scalar

            def front(n, at):
                if at == 4:
                    act.wait_ge(front_tensor.sem, front_tensor.at(n, "tok"))
                    A.activation(hT[:, :, tok_cols(n)], ps[:, 6:8, :], ACT.Copy).then_inc(front_scalar.sem, 1)
                if at == 6:
                    act.wait_ge(front_vector.sem, front_vector.at(n, "xc"))
                    A.activation(sq, xc, ACT.Square).then_inc(front_scalar.sem, 1)
                if at == 7:
                    act.wait_ge(front_tensor.sem, front_tensor.at(n, "var"))
                    A.activation(inv[:, 0, :], ps[:, 7, 0:4], ACT.Sqrt, bias=eps[:, 0:1]).then_inc(front_scalar.sem, 1)
                if at == 9:
                    act.wait_ge(front_tensor.sem, front_tensor.at(n, "x0"))
                    act.wait_ge(front_vector.sem, front_vector.at(n, "pad"))
                    A.activation(xpad[:, 0:2, TAPS - 1:], ps[:, 6:8, :], ACT.Copy).then_inc(front_scalar.sem, 1)
                    first_tap(n, 0)
                if at == 10:
                    act.wait_ge(front_tensor.sem, front_tensor.at(n, "x1"))
                    A.activation(xpad[:, 2:4, TAPS - 1:], ps[:, 6:8, :], ACT.Copy).then_inc(front_scalar.sem, 1)
                    first_tap(n, 1)
                if at == 11:
                    act.wait_ge(front_tensor.sem, front_tensor.at(n, "z0"))
                    A.activation(z_raw[:, 0:2, :], ps[:, 6:8, :], ACT.Copy).then_inc(front_scalar.sem, 1)
                if at == 13:
                    act.wait_ge(front_tensor.sem, front_tensor.at(n, "z1"))
                    A.activation(z_raw[:, 2:4, :], ps[:, 6:8, :], ACT.Copy).then_inc(front_scalar.sem, 1)

            def first_tap(n, pair):
                act.wait_ge(front_scalar.sem, front_scalar.at(n, f"x{pair}"))
                for c in (2 * pair, 2 * pair + 1):
                    last = A.activation(u_raw[:, c, :], xpad[:, c, TAPS - 1:], ACT.Identity,
                                        scale=taps[:, c, TAPS - 1:TAPS], bias=tap_b[:, c:c + 1])
                last.then_inc(front_scalar.sem, 1)

            def entry(b):
                act.wait_ge(front_vector.sem, front_vector.at(b, f"conv1{TAPS - 1}"))
                if not (isinstance(b, int) and b == 0):
                    act.wait_ge(scan_tensor.sem, scan_tensor.at(b - 1, f"Y{KSTEP - 1}"))
                A.activation(th, u_raw[:], ACT.Tanh).then_inc(entry_scalar.sem, 1)
                act.wait_ge(front_scalar.sem, front_scalar.at(b, "z1"))
                A.activation(thz, z_raw[:], ACT.Tanh, scale=0.5).then_inc(entry_scalar.sem, 1)
                act.wait_ge(entry_tensor.sem, entry_tensor.at(b, "bcdt"))
                A.activation(dtl[96:112, :], ps[96:112, 2, :], ACT.Copy).then_inc(entry_scalar.sem, 1)
                for c in range(DC):
                    act.wait_ge(entry_tensor.sem, entry_tensor.at(b, f"dt{c}"))
                    A.activation(th[:, c, :], ps[:, DT_BANKS[c], :], ACT.Abs, bias=b_dt[:, c:c + 1]).then_inc(entry_scalar.sem, 1)
                act.wait_ge(entry_scalar.sem, entry_scalar.at(b, f"abs{DC - 1}"))
                A.activation(th, th, ACT.Exp, scale=-1.0).then_inc(entry_scalar.sem, 1)
                act.wait_ge(entry_scalar.sem, entry_scalar.at(b, "exp"))
                for pair in range(2):
                    v = th[:, 2 * pair:2 * pair + 2, :]
                    A.activation(v, v, ACT.Ln, bias=1.0).then_inc(entry_scalar.sem, 1)

            def scan_step(b, k):
                half, n = divmod(k, NS)
                if k <= 1:
                    act.wait_ge(entry_vector.sem, entry_vector.at(b, f"delta{k}"))
                if k >= 2:
                    act.wait_ge(scan_vector.sem, scan_vector.at(b, f"scan{k - 2}"))
                for i in range(2):
                    c = 2 * half + i
                    last = A.activation(dA[:, k % 2, i, :], delta[:, c, :], ACT.Exp, scale=a_neg[:, c, n:n + 1])
                last.then_inc(scan_scalar.sem, 1)

            def route(m, at):
                if at == 1:
                    act.wait_ge(route_vector.sem, route_vector.at(m, "xc"))
                    A.activation(r_sq, mx[:], ACT.Square).then_inc(route_scalar.sem, 1)
                if at == 3:
                    act.wait_ge(route_tensor.sem, route_tensor.at(m, "var"))
                    A.activation(inv[:, 1, :], ps[:, 5, 0:4], ACT.Sqrt, bias=eps[:, 0:1]).then_inc(route_scalar.sem, 1)
                if at == 6:
                    act.wait_ge(route_tensor.sem, route_tensor.at(m, "gate"))
                    A.activation(sc[:], ps[:, 5, 0:4 * E], ACT.Exp, scale=-1.0).then_inc(route_scalar.sem, 1)
                if at == TURN_AT:
                    act.wait_ge(route_tensor.sem, route_tensor.at(m, "turn"))
                    A.activation(comb_t[:], ps[:, 5, :], ACT.Copy).then_inc(route_scalar.sem, 1)

            def expert_step(m, j):
                act.wait_ge(expert_tensor.sem, expert_tensor.at(m, f"up{j}"))
                if j >= 2:
                    act.wait_ge(expert_tensor.sem, expert_tensor.at(m, f"dn{j - 2}"))
                A.activation(m_act[:, j % 2, :], ps[:, 4, :], ACT.Tanh, scale=0.5).then_inc(expert_scalar.sem, 1)

            def rnd(b, before, after):
                entry(b)
                scan_step(b, 0)
                for k in range(KSTEP + 1):
                    if k + 1 < KSTEP:
                        scan_step(b, k + 1)
                    if before:
                        route(b - 1, k)
                        if 0 <= k - 1 - MOE_AT < MOE:
                            expert_step(b - 1, k - 1 - MOE_AT)
                    if after:
                        front(b + 1, k)

            act.wait_ge(tok_loaded, TOK_LOADS)
            for k in range(8):
                front(0, k)
            act.wait_ge(loaded, LOADS)
            act.wait_ge(setup_vector.sem, setup_vector.at(0, "cap"))
            A.activation(a_neg[:], a_neg[:], ACT.Exp).then_inc(setup_scalar.sem, 1)
            act.wait_ge(setup_vector.sem, setup_vector.at(0, "pad"))
            for k in range(8, KSTEP):
                front(0, k)
            rnd(0, False, True)
            with act.Fori(1, B - 1) as b:
                rnd(b, True, True)
            rnd(B - 1, True, False)
            for k in range(MOE_AT):
                route(B - 1, k)
            for j in range(SC):
                expert_step(B - 1, j)
            route(B - 1, TURN_AT)
            for j in range(SC, MOE):
                expert_step(B - 1, j)

        @block.tensor
        def _(pe):
            def mm(o, w, x, first, last):
                return nc.tensor.matmul(o, w, x, start=first, stop=last)

            def token_sums(o, x):
                for t in range(4):
                    for c in range(HC):
                        last = mm(o[:, t:t + 1], x[:, c, t * P:(t + 1) * P], means[:, 0:1], c == 0, c == HC - 1)
                return last

            def spread_tokens(bank, v):
                for t in range(4):
                    last = mm(ps[:, bank, t * P:(t + 1) * P], v[:, t:t + 1].to_broadcast([P, P]), ident[:], True, True)
                return last

            def front(n, at):
                half = XC // 2
                if at <= 4:
                    hi = at > 0
                    first, end = (at - 1, at) if hi else (0, half)
                    if not first:
                        pe.wait_ge(x_loaded[hi], n * 16 + 16)
                    for k in range(first, end):
                        for o in range(HC):
                            last = mm(ps[:, 6 + o, :], tok_w[:, hi * half + k, o * P:(o + 1) * P], x_tile(n, hi)[:, k, :],
                                      not hi and k == 0, hi and k == half - 1)
                    if end == half:
                        last.then_inc(front_tensor.sem, 1)
                if at == 5:
                    pe.wait_ge(front_scalar.sem, front_scalar.at(n, "h"))
                    for c in range(HC):
                        last = mm(ps[:, 6, :], means[:], hT[:, c, tok_cols(n)], c == 0, c == HC - 1)
                    last.then_inc(front_tensor.sem, 1)
                if at == 6:
                    pe.wait_ge(front_scalar.sem, front_scalar.at(n, "sq"))
                    token_sums(ps[:, 7, :], sq).then_inc(front_tensor.sem, 1)
                if at == 8:
                    pe.wait_ge(front_vector.sem, front_vector.at(n, "inv"))
                    spread_tokens(6, inv[:, 0, :]).then_inc(front_tensor.sem, 1)
                for i, (name, step, o) in enumerate((("x0", 9, 0), ("x1", 10, 2), ("z0", 11, DC), ("z1", 12, DC + 2))):
                    if at == step:
                        if i == 0:
                            pe.wait_ge(front_vector.sem, front_vector.at(n, "xn"))
                        else:
                            pe.wait_ge(front_scalar.sem, front_scalar.at(n, ("x0", "x1", "z0")[i - 1]))
                        for q in range(2):
                            for c in range(HC):
                                last = mm(ps[:, 6 + q, :], w_in[:, c, (o + q) * P:(o + q + 1) * P], xc[:, c, :], c == 0, c == HC - 1)
                        last.then_inc(front_tensor.sem, 1)

            def entry(b):
                pe.wait_ge(entry_vector.sem, entry_vector.at(b, "u"))
                for c in range(DC):
                    last = mm(ps[0:112, 2, :], w_x[:, c, :], u[:, c, :], c == 0, c == DC - 1)
                last.then_inc(entry_tensor.sem, 1)
                pe.wait_ge(entry_scalar.sem, entry_scalar.at(b, "dtl"))
                if not (isinstance(b, int) and b == 0):
                    pe.wait_ge(scan_vector.sem, scan_vector.at(b - 1, "res"))
                for c in range(DC):
                    mm(ps[:, DT_BANKS[c], :], w_dt[96:112, c * P:(c + 1) * P], dtl[96:112, :], True, True).then_inc(entry_tensor.sem, 1)

            def spread(bank, row):
                return mm(ps[:, bank, :], pick_state[:, row:row + 1].to_broadcast([96, P]), bc[:], True, True)

            def scan_part(b, name, k):
                n = k % NS
                if name == "B":
                    if k == 0:
                        pe.wait_ge(entry_vector.sem, entry_vector.at(b, "bc3"))
                        pe.wait_ge(entry_scalar.sem, entry_scalar.at(b, "dtl"))
                    else:
                        pe.wait_ge(scan_vector.sem, scan_vector.at(b, f"dBu{k - 1}"))
                    spread(2, n).then_inc(scan_tensor.sem, 1)
                if name == "C":
                    if k:
                        pe.wait_ge(scan_vector.sem, scan_vector.at(b, f"hC{k - 1}"))
                    spread(3, NS + n).then_inc(scan_tensor.sem, 1)
                if name == "Y":
                    pe.wait_ge(scan_vector.sem, scan_vector.at(b, f"hC{k}"))
                    if k == NS:
                        pe.wait_ge(scan_vector.sem, scan_vector.at(b, "skip0"))
                    for i in range(2):
                        last = mm(ps[:, i, :], ident[:], hC[:, k % 2, i, :], n == 0, n == NS - 1)
                    last.then_inc(scan_tensor.sem, 1)

            def project(b):
                pe.wait_ge(scan_vector.sem, scan_vector.at(b, "skip1"))
                for c in range(DC):
                    if c == DC // 2:
                        pe.wait_ge(scan_vector.sem, scan_vector.at(b, "gated1"))
                    for o in range(HC):
                        last = mm(ps[:, o, :], w_out[:, c, o * P:(o + 1) * P], zg[:, c, :], c == 0, c == DC - 1)
                last.then_inc(scan_tensor.sem, 1)

            def expert_up(m, j):
                if j:
                    pe.wait_ge(expert_vector.sem, expert_vector.at(m, f"a{j - 1}"))
                else:
                    pe.wait_ge(route_vector.sem, route_vector.at(m, "xn"))
                w = up_w if j >= SC else sup_w
                at = (j - SC if j >= SC else j) * P
                for c in range(HC):
                    last = mm(ps[:, 4, :], w[:, c, at:at + P], mx[:, c, :], c == 0, c == HC - 1)
                last.then_inc(expert_tensor.sem, 1)
                if j >= SC:
                    if j > SC:
                        pe.wait_ge(expert_vector.sem, expert_vector.at(m, f"c{j - 1}"))
                    else:
                        pe.wait_ge(route_scalar.sem, route_scalar.at(m, "comb_t"))
                    mm(ps[:, 5, :], pick_expert[:, j - SC:j - SC + 1].to_broadcast([P, P]), comb_t[:], True, True)\
                        .then_inc(expert_tensor.sem, 1)

            def expert_down(m, j):
                pe.wait_ge(expert_vector.sem, expert_vector.at(m, f"c{j}" if j >= SC else f"a{j}"))
                for o in range(HC):
                    w = down_w[:, j - SC, o * P:(o + 1) * P] if j >= SC else sdown_w[:, j, o * P:(o + 1) * P]
                    last = mm(ps[:, 6 + o, :], w, m_act[:, j % 2, :], j == 0, j == MOE - 1)
                last.then_inc(expert_tensor.sem, 1)

            def expert_step(m, j):
                if 2 <= j:
                    expert_down(m, j - 2)
                if j < MOE:
                    expert_up(m, j)

            def route(m, at):
                if at == 0:
                    pe.wait_ge(scan_vector.sem, scan_vector.at(m, "res"))
                    for c in range(HC):
                        last = mm(ps[:, 4, :], means[:], hT[:, c, tok_cols(m)], c == 0, c == HC - 1)
                    last.then_inc(route_tensor.sem, 1)
                if at == 2:
                    pe.wait_ge(route_scalar.sem, route_scalar.at(m, "sq"))
                    token_sums(ps[:, 5, :], r_sq).then_inc(route_tensor.sem, 1)
                if at == 4:
                    pe.wait_ge(route_vector.sem, route_vector.at(m, "inv"))
                    spread_tokens(4, inv[:, 1, :]).then_inc(route_tensor.sem, 1)
                if at == 5:
                    pe.wait_ge(route_vector.sem, route_vector.at(m, "xn"))
                    for t in range(4):
                        for c in range(HC):
                            last = mm(ps[:, 5, t * E:(t + 1) * E], mx[:, c, t * P:(t + 1) * P], gate_w[:, c, :],
                                      c == 0, c == HC - 1)
                    last.then_inc(route_tensor.sem, 1)
                if at == TURN_AT:
                    pe.wait_ge(route_vector.sem, route_vector.at(m, "k3"))
                    for t in range(4):
                        last = mm(ps[:, 5, t * P:(t + 1) * P], comb_p[:, t, :, :].rearrange("p a b -> p (a b)"), identb[:],
                                  True, True)
                    last.then_inc(route_tensor.sem, 1)

            def rnd(b, before, after):
                entry(b)
                for k in range(-1, KSTEP + 1):
                    for name, at in tensor_scan_parts(k):
                        scan_part(b, name, at)
                    if k == 0:
                        pe.wait_ge(entry_vector.sem, entry_vector.at(b, f"pos{DC - 1}"))
                    if before:
                        route(b - 1, k)
                        if after and k - MOE_AT == 2:
                            pe.wait_ge(front_scalar.sem, front_scalar.at(b + 1, "z1"))
                        if 0 <= k - MOE_AT < MOE + 1:
                            expert_step(b - 1, k - MOE_AT)
                    if after and k:
                        front(b + 1, max(k, 0))
                if before:
                    expert_step(b - 1, MOE + 1)
                project(b)

            pe.wait_ge(tok_loaded, TOK_LOADS)
            pe.wait_ge(setup_vector.sem, setup_vector.at(0, f"tok{XC - 1}"))
            for k in range(9):
                front(0, k)
            pe.wait_ge(loaded, LOADS)
            pe.wait_ge(setup_vector.sem, setup_vector.at(0, "pad"))
            for k in range(9, KSTEP):
                front(0, k)
            pe.wait_ge(front_scalar.sem, front_scalar.at(0, "z1"))
            rnd(0, False, True)
            pe.wait_ge(experts_loaded, EXPERT_LOADS)
            pe.wait_ge(down_loaded, 16)
            with pe.Fori(1, B - 1) as b:
                rnd(b, True, True)
            rnd(B - 1, True, False)
            pe.wait_ge(expert_vector.sem, expert_vector.at(B - 2, "res"))
            for k in range(MOE_AT):
                route(B - 1, k)
            for j in range(SC):
                expert_step(B - 1, j)
            route(B - 1, TURN_AT)
            for j in range(SC, MOE + 2):
                expert_step(B - 1, j)

        @block.vector
        def _(dve):
            V = nc.vector

            def front(n, at):
                if at == 5:
                    dve.wait_ge(front_tensor.sem, front_tensor.at(n, "mean"))
                    V.tensor_tensor(xc, hT[:, :, tok_cols(n)], spread_over(ps[:, 6, :], HC), ALU.subtract).then_inc(front_vector.sem, 1)
                if at == 7:
                    dve.wait_ge(front_scalar.sem, front_scalar.at(n, "std"))
                    V.reciprocal(inv[:, 0, :], inv[:, 0, :]).then_inc(front_vector.sem, 1)
                    V.memset(xpad[:, :, 0:TAPS - 1], 0.0).then_inc(front_vector.sem, 1)
                if at == 8:
                    dve.wait_ge(front_tensor.sem, front_tensor.at(n, "inv"))
                    V.tensor_tensor(xc, xc, spread_over(ps[:, 6, :], HC), ALU.mult).then_inc(front_vector.sem, 1)
                for pair, steps in ((0, (17, 19, 21)), (1, (23, 25, 27))):
                    for j in range(1, TAPS):
                        if at == steps[j - 1]:
                            conv(n, pair, j)

            def conv(n, pair, j):
                tap = TAPS - 1 - j
                if j > 1:
                    dve.wait_ge(front_vector.sem, front_vector.at(n, f"conv{pair}{j - 1}"))
                else:
                    dve.wait_ge(front_scalar.sem, front_scalar.at(n, f"conv{pair}0"))
                for c in (2 * pair, 2 * pair + 1):
                    last = V.scalar_tensor_tensor(u_raw[:, c, :], xpad[:, c, tap:tap + S], taps[:, c, tap:tap + 1],
                                                  u_raw[:, c, :], ALU.mult, ALU.add)
                last.then_inc(front_vector.sem, 1)

            def entry_u(b):
                if not (isinstance(b, int) and b == 0):
                    dve.wait_ge(scan_vector.sem, scan_vector.at(b - 1, "gated1"))
                dve.wait_ge(entry_scalar.sem, entry_scalar.at(b, "thu"))
                V.scalar_tensor_tensor(u[:], th, 1.0, u_raw[:], ALU.add, ALU.mult).then_inc(entry_vector.sem, 1)

            def entry(b):
                dve.wait_ge(entry_tensor.sem, entry_tensor.at(b, "bcdt"))
                dve.wait_ge(entry_scalar.sem, entry_scalar.at(b, "dtl"))
                V.tensor_copy(bc[:], ps[0:96, 2, :]).then_inc(entry_vector.sem, 1)
                dve.wait_ge(entry_vector.sem, entry_vector.at(b, "bc1"))
                V.tensor_tensor(r_bc[0:96, :], ps[0:96, 2, :], bc[:], ALU.subtract).then_inc(entry_vector.sem, 1)
                dve.wait_ge(entry_vector.sem, entry_vector.at(b, "r1"))
                V.tensor_copy(bc[32:64, :], r_bc[32:64, :])
                V.tensor_copy(bc[64:96, :], r_bc[64:96, :]).then_inc(entry_vector.sem, 1)
                dve.wait_ge(entry_vector.sem, entry_vector.at(b, "bc2"))
                V.tensor_tensor(r_bc[64:96, :], r_bc[64:96, :], bc[64:96, :], ALU.subtract).then_inc(entry_vector.sem, 1)
                dve.wait_ge(entry_vector.sem, entry_vector.at(b, "r2"))
                V.tensor_copy(bc[64:96, :], r_bc[64:96, :]).then_inc(entry_vector.sem, 1)
                for c in range(DC):
                    dve.wait_ge(entry_scalar.sem, entry_scalar.at(b, f"abs{c}"))
                    V.tensor_scalar(delta[:, c, :], ps[:, DT_BANKS[c], :], b_dt[:, c:c + 1], 0.0, ALU.add, ALU.max).then_inc(entry_vector.sem, 1)
                V.scalar_tensor_tensor(zg[:], thz, 1.0, z_raw[:], ALU.add, ALU.mult).then_inc(entry_vector.sem, 1)
                dve.wait_ge(entry_vector.sem, entry_vector.at(b, f"pos{DC - 1}"))
                entry_delta(b, 0)
                entry_du(b, 0)
                entry_delta(b, 1)

            def entry_delta(b, half):
                pair = slice(2 * half, 2 * half + 2)
                dve.wait_ge(entry_scalar.sem, entry_scalar.at(b, f"ln{half}"))
                V.tensor_tensor(delta[:, pair, :], delta[:, pair, :], th[:, pair, :], ALU.add).then_inc(entry_vector.sem, 1)

            def entry_du(b, half):
                pair = slice(2 * half, 2 * half + 2)
                dve.wait_ge(entry_vector.sem, entry_vector.at(b, f"delta{half}"))
                V.tensor_tensor(du[:, pair, :], delta[:, pair, :], u[:, pair, :], ALU.mult).then_inc(entry_vector.sem, 1)

            def scan_first(b, k):
                half = k // NS
                dve.wait_ge(scan_tensor.sem, scan_tensor.at(b, f"B{k}"))
                if k == NS:
                    dve.wait_ge(entry_vector.sem, entry_vector.at(b, "du1"))
                if k == 0:
                    dve.wait_ge(entry_vector.sem, entry_vector.at(b, "du0"))
                else:
                    dve.wait_ge(scan_vector.sem, scan_vector.at(b, f"hC{k - 1}"))
                V.tensor_tensor(hs, du[:, 2 * half:2 * half + 2, :], spread_over(ps[:, 2, :], 2), ALU.mult)\
                    .then_inc(scan_vector.sem, 1)
                dve.wait_ge(scan_scalar.sem, scan_scalar.at(b, f"dA{k}"))
                dve.wait_ge(scan_vector.sem, scan_vector.at(b, f"dBu{k}"))
                for i in range(2):
                    last = V.tensor_tensor_scan(hs[:, i, :], dA[:, k % 2, i, :], hs[:, i, :], 0.0, ALU.mult, ALU.add)
                last.then_inc(scan_vector.sem, 1)

            def scan_second(b, k):
                dve.wait_ge(scan_tensor.sem, scan_tensor.at(b, f"C{k}"))
                dve.wait_ge(scan_vector.sem, scan_vector.at(b, f"scan{k}"))
                if k >= 2:
                    dve.wait_ge(scan_tensor.sem, scan_tensor.at(b, f"Y{k - 2}"))
                V.tensor_tensor(hC[:, k % 2], hs, spread_over(ps[:, 3, :], 2), ALU.mult).then_inc(scan_vector.sem, 1)

            def scan_end(b, half):
                dve.wait_ge(scan_tensor.sem, scan_tensor.at(b, f"Y{NS * half + NS - 1}"))
                pair = slice(2 * half, 2 * half + 2)
                for i in range(2):
                    c = 2 * half + i
                    last = V.scalar_tensor_tensor(u[:, c, :], u[:, c, :], d_skip[:, c:c + 1], ps[:, i, :], ALU.mult, ALU.add)
                last.then_inc(scan_vector.sem, 1)
                dve.wait_ge(scan_vector.sem, scan_vector.at(b, f"skip{half}"))
                V.tensor_tensor(zg[:, pair, :], u[:, pair, :], zg[:, pair, :], ALU.mult).then_inc(scan_vector.sem, 1)

            def scan_residual(b):
                dve.wait_ge(scan_tensor.sem, scan_tensor.at(b, "proj"))
                V.scalar_tensor_tensor(hT[:, :, tok_cols(b)], ps[:, 0:2, :], 0.5, hT[:, :, tok_cols(b)], ALU.mult, ALU.add)\
                    .then_inc(scan_vector.sem, 1)

            def expert_step(m, j):
                dve.wait_ge(expert_scalar.sem, expert_scalar.at(m, f"th{j}"))
                V.scalar_tensor_tensor(m_act[:, j % 2, :], m_act[:, j % 2, :], 1.0, ps[:, 4, :], ALU.add, ALU.mult)\
                    .then_inc(expert_vector.sem, 1)
                if j >= SC:
                    dve.wait_ge(expert_tensor.sem, expert_tensor.at(m, f"cb{j}"))
                    dve.wait_ge(expert_vector.sem, expert_vector.at(m, f"a{j}"))
                    V.tensor_tensor(m_act[:, j % 2, :], m_act[:, j % 2, :], ps[:, 5, :], ALU.mult).then_inc(expert_vector.sem, 1)

            def expert_end(m):
                dve.wait_ge(expert_tensor.sem, expert_tensor.at(m, f"dn{MOE - 1}"))
                V.scalar_tensor_tensor(hT[:, :, tok_cols(m)], ps[:, 6:8, :], 0.5, hT[:, :, tok_cols(m)], ALU.mult, ALU.add)\
                    .then_inc(expert_vector.sem, 1)

            def route(m, at):
                def step(ins, name):
                    ins.then_inc(route_vector.sem, 1)
                    dve.wait_ge(route_vector.sem, route_vector.at(m, name))

                def ranked(v, tiles, n):
                    return (v.rearrange("p t (i o) -> p t i o", o=1).to_broadcast([P, tiles, n, n]),
                            v.rearrange("p t (o j) -> p t o j", o=1).to_broadcast([P, tiles, n, n]),
                            lower[:, 0:n, 0:n].rearrange("p (t i) j -> p t i j", t=1).to_broadcast([P, tiles, n, n]))

                s4 = sc[:].rearrange("p (g e) -> p g e", e=E // NG)
                gt = gsum.rearrange("p (t g) -> p t g", t=4)
                gg, ge = (v.rearrange("p t (i j) -> p t i j", i=NG) for v in (g_gt, g_eq))
                mt = masked.rearrange("p (t e) -> p t e", t=4)
                cg, ce = (v.rearrange("p t (i j) -> p t i j", i=E) for v in (c_gt, c_eq))
                if at == 0:
                    dve.wait_ge(route_tensor.sem, route_tensor.at(m, "mean"))
                    V.tensor_tensor(mx[:], hT[:, :, tok_cols(m)], spread_over(ps[:, 4, :], HC), ALU.subtract).then_inc(route_vector.sem, 1)
                if at == 3:
                    dve.wait_ge(route_scalar.sem, route_scalar.at(m, "std"))
                    V.reciprocal(inv[:, 1, :], inv[:, 1, :]).then_inc(route_vector.sem, 1)
                if at == 4:
                    dve.wait_ge(route_tensor.sem, route_tensor.at(m, "inv"))
                    V.tensor_tensor(mx[:], mx[:], spread_over(ps[:, 4, :], HC), ALU.mult).then_inc(route_vector.sem, 1)
                if at == 6:
                    dve.wait_ge(route_scalar.sem, route_scalar.at(m, "e"))
                    step(V.tensor_scalar(sc[:], sc[:], 1.0, None, ALU.add), "s1")
                    step(V.reciprocal(sc[:], sc[:]), "s")
                    w = 0
                    for i in range(4):
                        for j in range(i + 1, 4):
                            V.tensor_tensor(pairs[:, w, :], s4[:, :, i], s4[:, :, j], ALU.add).then_inc(route_vector.sem, 1)
                            w += 1
                if at == 7:
                    dve.wait_ge(route_vector.sem, route_vector.at(m, "p5"))
                    step(V.tensor_reduce(gsum, pairs.rearrange("p w g -> p g w"), AX.X, ALU.max), "gs")
                    own, other, _ = ranked(gt, 4, NG)
                    V.tensor_tensor(gg, other, own, ALU.is_gt).then_inc(route_vector.sem, 1)
                    step(V.tensor_tensor(ge, other, own, ALU.is_equal), "geq")
                if at == 8:
                    step(V.tensor_tensor(ge, ge, ranked(gt, 4, NG)[2], ALU.mult), "geql")
                    step(V.tensor_tensor(g_gt, g_gt, g_eq, ALU.add), "gsumr")
                    step(V.tensor_reduce(grank, g_gt.rearrange("p t (i j) -> p (t i) j", j=NG), AX.X, ALU.add), "gr")
                    step(V.tensor_scalar(grank, grank, 1.5, None, ALU.is_lt), "gm")
                    step(V.tensor_tensor(masked.rearrange("p (g e) -> p g e", e=E // NG), s4,
                                         grank.rearrange("p (g o) -> p g o", o=1).to_broadcast([P, 4 * NG, E // NG]), ALU.mult), "msk")
                for h in range(2):
                    if at == (10, 12)[h]:
                        own, other, before = ranked(mt[:, 2 * h:2 * h + 2, :], 2, E)
                        V.tensor_tensor(cg, other, own, ALU.is_gt).then_inc(route_vector.sem, 1)
                        step(V.tensor_tensor(ce, other, own, ALU.is_equal), f"ceq{h}")
                        step(V.tensor_tensor(ce, ce, before, ALU.mult), f"ceql{h}")
                        step(V.tensor_tensor(c_gt, c_gt, c_eq, ALU.add), f"csum{h}")
                        step(V.tensor_reduce(rank[:, 2 * h * E:2 * (h + 1) * E], c_gt.rearrange("p t (i j) -> p (t i) j", j=E),
                                             AX.X, ALU.add), f"cr{h}")
                if at == 13:
                    step(V.scalar_tensor_tensor(masked, rank, TOPK - 0.5, sc[:], ALU.is_lt, ALU.mult), "w")
                    step(V.tensor_reduce(wsum, mt, AX.X, ALU.add), "ws")
                    step(V.tensor_scalar(wsum, wsum, 1e-20, None, ALU.add), "wr")
                    step(V.reciprocal(wsum, wsum), "rcp")
                    step(V.scalar_tensor_tensor(comb[:], mt, 2.5, wsum.rearrange("p (t o) -> p t o", o=1).to_broadcast([P, 4, E]),
                                                ALU.mult, ALU.mult), "comb")
                if at == 14:
                    left = wres.rearrange("p (t e) -> p t e", t=4)
                    step(V.tensor_copy(comb_p[:, :, 0, :], comb[:]), "k1")
                    step(V.tensor_tensor(left, comb[:], comb_p[:, :, 0, :], ALU.subtract), "q1")
                    step(V.tensor_copy(comb_p[:, :, 1, :], left), "k2")
                    step(V.tensor_tensor(left, left, comb_p[:, :, 1, :], ALU.subtract), "q2")
                    V.tensor_copy(comb_p[:, :, 2, :], left).then_inc(route_vector.sem, 1)

            def rnd(b, before, after):
                entry(b)
                for k in range(KSTEP):
                    scan_first(b, k)
                    if before:
                        route(b - 1, k)
                        if 0 <= k - 1 - MOE_AT < MOE:
                            expert_step(b - 1, k - 1 - MOE_AT)
                    if after:
                        front(b + 1, k - 1)
                    if k == NS:
                        scan_end(b, 0)
                    scan_second(b, k)
                    if k == 0:
                        entry_du(b, 1)
                if before:
                    expert_step(b - 1, MOE - 1)
                scan_end(b, 1)
                if after:
                    entry_u(b + 1)
                if before:
                    expert_end(b - 1)
                scan_residual(b)

            dve.wait_ge(tok_loaded, TOK_LOADS)
            for d in range(TOKD):
                for c in range(HC):
                    V.tensor_tensor(tok_w[:, d * HC + c, :], ws_t[:, c, :], v_rep[:, d, :], ALU.mult).then_inc(setup_vector.sem, 1)
            dve.wait_ge(setup_vector.sem, setup_vector.at(0, f"tok{XC - 1}"))
            for k in range(9):
                front(0, k)
            dve.wait_ge(loaded, LOADS)
            V.tensor_scalar(taps[:], taps[:], 0.5, None, ALU.mult).then_inc(setup_vector.sem, 1)
            V.tensor_scalar(tap_b[:], tap_b[:], 0.5, None, ALU.mult).then_inc(setup_vector.sem, 1)
            V.tensor_scalar(a_neg[:], a_neg[:], 80.0, None, ALU.min).then_inc(setup_vector.sem, 1)
            dve.wait_ge(setup_scalar.sem, setup_scalar.at(0, "aexp"))
            V.tensor_scalar(a_neg[:], a_neg[:], -1.0, None, ALU.mult).then_inc(setup_vector.sem, 1)
            V.tensor_copy(identb[:], ident[:]).then_inc(setup_vector.sem, 1)
            V.tensor_copy(pick_state[:], picks_f[0:96, 0:2 * NS]).then_inc(setup_vector.sem, 1)
            V.tensor_copy(pick_expert[:], picks_f[:, 2 * NS:]).then_inc(setup_vector.sem, 1)
            V.memset(comb_p[:], 0.0).then_inc(setup_vector.sem, 1)
            dve.wait_ge(setup_vector.sem, setup_vector.at(0, "pad"))
            for k in range(9, KSTEP):
                front(0, k)
            entry_u(0)
            rnd(0, False, True)
            with dve.Fori(1, B - 1) as b:
                rnd(b, True, True)
            rnd(B - 1, True, False)
            for k in range(KSTEP):
                route(B - 1, k)
                if k in SHARED_BESIDE:
                    expert_step(B - 1, SHARED_BESIDE.index(k))
            for j in range(SC, MOE):
                expert_step(B - 1, j)
            expert_end(B - 1)


def attention(nc, ctx, a, hT, ident, means, eps, ps, qkv_w, o_w, proj_loaded, g1_w, g1_b, gate_loaded):
    T, NH, D = B, 16, H // 16
    ROWS = 2 * T - 1
    PAIRS = T * HC
    AHEAD = 8

    def sb(name, shape, dt=F32):
        return ctx.enter_context(nc.sbuf_tensor(name, shape, dt))

    def sem(name):
        return ctx.enter_context(nc.semaphore(name))

    pos_w = sb("pos_w", [P, HC, H])
    pos_t = sb("pos_t", [P, HC, ROWS])
    qkv_b = sb("qkv_b", [P, 3 * HC])
    pos_b = sb("pos_b", [P, HC])
    o_b = sb("o_b", [P, HC])
    r_w = sb("r_w", [P, HC])
    r_r = sb("r_r", [P, HC])
    heads = sb("heads", [P, PAIRS, P])
    unheads = sb("unheads", [P, PAIRS, P])
    qkv = sb("qkv", [P, 3 * HC, B * S])
    p_row = sb("p_row", [P, HC, ROWS])
    p_gap = sb("p_gap", [P, HC, ROWS])
    gap = sb("gap", [P, T])
    p_at = sb("p_at", [P, HC, T, T])
    sq = sb("sq_a", [P, HC, S])
    rstd = sb("rstd_a", [P, S])
    prod = sb("prod", [P, AHEAD, S])
    s_row = sb("s_row", [P, S])
    s_tok = sb("s_tok", [P, 4, P])
    peak = sb("peak", [P, 4, NH])
    total = sb("total", [P, 4, NH])
    w_row = sb("w_row", [P, S])
    part = sb("part", [P, 3, HC, S])
    mix_sum = sb("mix_sum", [P, HC, S])
    mix = sb("mix", [P, HC, S])
    SCALE = float(D) ** -0.5

    bias_loaded, loaded = sem("bias_loaded"), sem("loaded_a")
    pos_tensor = Steps(sem("pos_tensor"), ["p", "gap"])
    pos_scalar = Steps(sem("pos_scalar"), ["p", "rows"])
    pos_vector = Steps(sem("pos_vector"), ["bq", "gap_w", "p_gap", "gap"])
    norm_tensor = Steps(sem("norm_tensor_a"), ["mean", "var"])
    norm_scalar = Steps(sem("norm_scalar_a"), ["sq", "std"])
    norm_vector = Steps(sem("norm_vector_a"), ["xc", "rstd", "xn"])
    qkv_tensor = Steps(sem("qkv_tensor"), [f"o{o}" for o in range(3 * HC)])
    qkv_scalar = Steps(sem("qkv_scalar"), [f"o{o}" for o in range(3 * HC)])
    score_tensor = Steps(sem("score_tensor"), [f"s{i}" for i in range(PAIRS)])
    score_scalar = Steps(sem("score_scalar"), ["s"])
    score_vector = Steps(sem("score_vector"), [f"prod{i}" for i in range(PAIRS)])
    soft_tensor = Steps(sem("soft_tensor"), ["turn", "back"])
    soft_scalar = Steps(sem("soft_scalar"), ["exp", "w"])
    soft_vector = Steps(sem("soft_vector"), ["max", "sub", "sum", "rcp", "w"])
    mix_tensor = Steps(sem("mix_tensor"), [f"w{s}" for s in range(T)])
    out_tensor = Steps(sem("out_tensor"), ["out"])
    mix_vector = Steps(sem("mix_vector"), ["m0"] + [n for s in range(1, T) for n in (f"m{s}", f"a{s}")])
    res_vector = Steps(sem("res_vector"), ["res"])
    BIAS_LOADS, LOADS = 16 * 2, 16 * 7

    with nc.Block() as block:
        @block.sync
        def _(sp):
            for dst, src in (
                (qkv_b[:], a["qkv_b"]), (r_w[:], a["r_w"]),
            ):
                sp.dma_start(dst, src).then_inc(bias_loaded, 16)
            for dst, src in (
                (pos_w[:], a["pos_w"].rearrange("(c p) o -> p c o", p=P)),
                (pos_t[:], a["pos_t"].rearrange("(c p) o -> p c o", p=P)),
                (pos_b[:], a["pos_b"]), (o_b[:], a["o_b"]), (r_r[:], a["r_r"]),
                (heads[:], a["heads"]), (unheads[:], a["unheads"]),
            ):
                sp.dma_start(dst, src).then_inc(loaded, 16)
            for dst, src in ((g1_w[:], a["g1_w"].rearrange("(c p) o -> p c o", p=P)), (g1_b[:], a["g1_b"])):
                sp.dma_start(dst, src).then_inc(gate_loaded, 16)

        @block.tensor
        def _(pe):
            def mm(o, w, x, first, last):
                return nc.tensor.matmul(o, w, x, start=first, stop=last)

            def score(t, pairs):
                for i in pairs:
                    if i == 0 and (not isinstance(t, int) or t):
                        pe.wait_ge(score_scalar.sem, score_scalar.at(t - 1, "s"))
                    pe.wait_ge(score_vector.sem, score_vector.at(t, f"prod{i}"))
                    mm(ps[:, 0, :], heads[:, i, :], prod[:, i % AHEAD, :], i == 0, i == PAIRS - 1).then_inc(score_tensor.sem, 1)

            def turn(t):
                pe.wait_ge(score_scalar.sem, score_scalar.at(t, "s"))
                for n in range(4):
                    last = nc.tensor.transpose(ps[:, 1, n * P:(n + 1) * P], s_row[:, n * P:(n + 1) * P], ident[:])
                last.then_inc(soft_tensor.sem, 1)

            def turn_back(t):
                pe.wait_ge(soft_vector.sem, soft_vector.at(t, "w"))
                for n in range(4):
                    last = nc.tensor.transpose(ps[:, 1, n * P:(n + 1) * P], s_tok[:, n, :], ident[:])
                last.then_inc(soft_tensor.sem, 1)

            def weigh(t, s):
                if s == 0:
                    pe.wait_ge(soft_scalar.sem, soft_scalar.at(t, "w"))
                if s >= 2:
                    pe.wait_ge(mix_vector.sem, mix_vector.at(t, f"m{s - 2}"))
                elif not isinstance(t, int) or t:
                    pe.wait_ge(mix_vector.sem, mix_vector.at(t - 1, f"m{s - 2 + T}"))
                for c in range(HC):
                    last = mm(ps[:, 2 + 2 * (s % 2) + c, :], unheads[:, s * HC + c, :], w_row[:], True, True)
                last.then_inc(mix_tensor.sem, 1)

            def put_out(t):
                pe.wait_ge(mix_vector.sem, mix_vector.at(t, f"a{T - 1}"))
                if not isinstance(t, int) or t:
                    pe.wait_ge(res_vector.sem, res_vector.at(t - 1, "res"))
                for o in range(HC):
                    for c in range(HC):
                        last = mm(ps[:, 6 + o, :], o_w[:, c, o * P:(o + 1) * P], mix[:, c, :], c == 0, c == HC - 1)
                last.then_inc(out_tensor.sem, 1)

            def mean(t):
                if not isinstance(t, int):
                    pe.wait_ge(norm_vector.sem, norm_vector.at(t - 1, "xc"))
                for c in range(HC):
                    last = mm(ps[:, 0, :], means[:], hT[:, c, tok_cols(t)], c == 0, c == HC - 1)
                last.then_inc(norm_tensor.sem, 1)

            def variance(t):
                pe.wait_ge(norm_scalar.sem, norm_scalar.at(t, "sq"))
                for c in range(HC):
                    last = mm(ps[:, 1, :], means[:], sq[:, c, :], c == 0, c == HC - 1)
                last.then_inc(norm_tensor.sem, 1)

            def project(t, outs):
                for o in outs:
                    if not isinstance(t, int) or t:
                        pe.wait_ge(qkv_scalar.sem, qkv_scalar.at(t - 1, f"o{o}"))
                    for c in range(HC):
                        last = mm(ps[:, 2 + o, :], qkv_w[:, c, o * P:(o + 1) * P], qkv[:, 2 * HC + c, tok_cols(t)], c == 0, c == HC - 1)
                    last.then_inc(qkv_tensor.sem, 1)

            def project_beside_norm(t):
                mean(t + 1)
                pe.wait_ge(norm_vector.sem, norm_vector.at(t, "xn"))
                project(t, (0, 1))
                variance(t + 1)
                project(t, (2, 3, 4, 5))

            mean(0)
            variance(0)
            pe.wait_ge(norm_vector.sem, norm_vector.at(0, "xc"))
            pe.wait_ge(proj_loaded, 32)
            project_beside_norm(0)
            with pe.Fori(1, T - 1) as t:
                project_beside_norm(t)
            pe.wait_ge(norm_vector.sem, norm_vector.at(T - 1, "xn"))
            pe.wait_ge(loaded, LOADS)
            for o in range(HC):
                for c in range(HC):
                    last = mm(ps[:, o, 0:ROWS], pos_w[:, c, o * P:(o + 1) * P], pos_t[:, c, :], c == 0, c == HC - 1)
            last.then_inc(pos_tensor.sem, 1)
            project(T - 1, range(3 * HC))
            pe.wait_ge(pos_vector.sem, pos_vector.at(0, "p_gap"))
            for i in range(PAIRS):
                s, c = divmod(i, HC)
                last = mm(ps[:, 0, 0:T], heads[:, i, :], p_gap[:, c, s:s + T], i == 0, i == PAIRS - 1)
            last.then_inc(pos_tensor.sem, 1)
            pe.wait_ge(qkv_scalar.sem, qkv_scalar.at(T - 1, f"o{3 * HC - 1}"))
            pe.wait_ge(pos_vector.sem, pos_vector.at(0, "gap"))

            def queries(scored, softened, mixed):
                for s in range(T):
                    if mixed is not None:
                        weigh(mixed, s)
                    if scored is not None:
                        score(scored, range(s * HC, (s + 1) * HC))
                    if softened is not None and s == 0:
                        turn(softened)
                    if softened is not None and s == 5:
                        turn_back(softened)
                    if mixed is not None and (not isinstance(mixed, int) or mixed) and s == 3:
                        put_out(mixed - 1)

            queries(0, None, None)
            queries(1, 0, None)
            queries(2, 1, 0)
            with pe.Fori(3, T) as t:
                queries(t, t - 1, t - 2)
            queries(None, T - 1, T - 2)
            queries(None, None, T - 1)
            put_out(T - 1)

        @block.scalar
        def _(act):
            act.wait_ge(bias_loaded, BIAS_LOADS)
            act.wait_ge(pos_vector.sem, pos_vector.at(0, "bq"))

            def square(t):
                act.wait_ge(norm_vector.sem, norm_vector.at(t, "xc"))
                if not isinstance(t, int):
                    act.wait_ge(norm_tensor.sem, norm_tensor.at(t - 1, "var"))
                nc.scalar.activation(sq[:], qkv[:, 2 * HC:3 * HC, tok_cols(t)], ACT.Square).then_inc(norm_scalar.sem, 1)

            def deviation(t):
                act.wait_ge(norm_tensor.sem, norm_tensor.at(t, "var"))
                if not isinstance(t, int):
                    act.wait_ge(norm_vector.sem, norm_vector.at(t - 1, "xn"))
                nc.scalar.activation(rstd[:], ps[:, 1, :], ACT.Sqrt, bias=eps[:, 0:1]).then_inc(norm_scalar.sem, 1)

            def take(t, outs):
                for o in outs:
                    act.wait_ge(qkv_tensor.sem, qkv_tensor.at(t, f"o{o if o < 2 * HC else 3 * HC - 1}"))
                    nc.scalar.activation(qkv[:, o, tok_cols(t)], ps[:, 2 + o, :], ACT.Identity,
                                         bias=qkv_b[:, o:o + 1]).then_inc(qkv_scalar.sem, 1)

            def take_beside_norm(t):
                square(t + 1)
                take(t, (0, 1))
                deviation(t + 1)
                take(t, (2, 3, 4, 5))

            square(0)
            deviation(0)
            with act.Fori(0, T - 1) as t:
                take_beside_norm(t)
            act.wait_ge(loaded, LOADS)
            act.wait_ge(pos_tensor.sem, pos_tensor.at(0, "p"))
            for o in range(HC):
                last = nc.scalar.activation(p_row[:, o, :], ps[:, o, 0:ROWS], ACT.Identity, bias=pos_b[:, o:o + 1])
            last.then_inc(pos_scalar.sem, 1)
            act.wait_ge(pos_scalar.sem, pos_scalar.at(0, "p"))
            for t in range(T):
                last = nc.scalar.activation(p_at[:, :, :, t], p_row[:, :, T - 1 - t:2 * T - 1 - t], ACT.Copy)
            last.then_inc(pos_scalar.sem, 1)
            take(T - 1, range(3 * HC))
            act.wait_ge(pos_vector.sem, pos_vector.at(0, "gap"))

            def scale(t):
                act.wait_ge(score_tensor.sem, score_tensor.at(t, f"s{PAIRS - 1}"))
                nc.scalar.activation(s_row[:], ps[:, 0, :], ACT.Identity, scale=SCALE,
                                     bias=gap[:, bass.ds(T - 1 - t, 1)]).then_inc(score_scalar.sem, 1)

            def soften(t):
                act.wait_ge(soft_vector.sem, soft_vector.at(t, "sub"))
                nc.scalar.activation(s_tok[:], s_tok[:], ACT.Exp).then_inc(soft_scalar.sem, 1)
                act.wait_ge(soft_tensor.sem, soft_tensor.at(t, "back"))
                if not isinstance(t, int) or t:
                    act.wait_ge(mix_tensor.sem, mix_tensor.at(t - 1, f"w{T - 1}"))
                nc.scalar.activation(w_row[:], ps[:, 1, :], ACT.Copy).then_inc(soft_scalar.sem, 1)

            scale(0)
            soften(0)
            scale(1)
            with act.Fori(2, T) as t:
                soften(t - 1)
                scale(t)
            soften(T - 1)

        @block.vector
        def _(dve):
            V = nc.vector
            dve.wait_ge(bias_loaded, BIAS_LOADS)
            V.tensor_tensor(qkv_b[:, 0:HC], qkv_b[:, 0:HC], r_w[:], ALU.add).then_inc(pos_vector.sem, 1)
            with dve.Fori(0, T) as t:
                tokens = qkv[:, 2 * HC:3 * HC, tok_cols(t)]
                dve.wait_ge(norm_tensor.sem, norm_tensor.at(t, "mean"))
                V.tensor_tensor(tokens, hT[:, :, tok_cols(t)], spread_over(ps[:, 0, :], HC), ALU.subtract).then_inc(norm_vector.sem, 1)
                dve.wait_ge(norm_scalar.sem, norm_scalar.at(t, "std"))
                V.reciprocal(rstd[:], rstd[:]).then_inc(norm_vector.sem, 1)
                dve.wait_ge(norm_vector.sem, norm_vector.at(t, "rstd"))
                V.tensor_tensor(tokens, tokens, spread_over(rstd[:], HC), ALU.mult).then_inc(norm_vector.sem, 1)

            dve.wait_ge(loaded, LOADS)
            V.tensor_tensor(r_r[:], r_r[:], r_w[:], ALU.subtract).then_inc(pos_vector.sem, 1)
            dve.wait_ge(pos_vector.sem, pos_vector.at(0, "gap_w"))
            dve.wait_ge(pos_scalar.sem, pos_scalar.at(0, "p"))
            for c in range(HC):
                last = V.tensor_scalar(p_gap[:, c, :], p_row[:, c, :], r_r[:, c:c + 1], None, ALU.mult)
            last.then_inc(pos_vector.sem, 1)
            dve.wait_ge(pos_tensor.sem, pos_tensor.at(0, "gap"))
            V.tensor_scalar(gap[:], ps[:, 0, 0:T], SCALE, None, ALU.mult).then_inc(pos_vector.sem, 1)
            dve.wait_ge(pos_scalar.sem, pos_scalar.at(0, "rows"))

            def multiply(t, pairs):
                for i in pairs:
                    s, c = divmod(i, HC)
                    if i >= AHEAD:
                        dve.wait_ge(score_tensor.sem, score_tensor.at(t, f"s{i - AHEAD}"))
                    elif not isinstance(t, int) or t:
                        dve.wait_ge(score_tensor.sem, score_tensor.at(t - 1, f"s{i - AHEAD + PAIRS}"))
                    V.scalar_tensor_tensor(prod[:, i % AHEAD, :], qkv[:, HC + c, tok_cols(s)], p_at[:, c, s, bass.ds(t, 1)],
                                           qkv[:, c, tok_cols(t)], ALU.add, ALU.mult).then_inc(score_vector.sem, 1)

            by_key = s_tok[:].rearrange("p n (s h) -> p n s h", s=T)

            def over_keys(v):
                return v[:].rearrange("p n (o h) -> p n o h", o=1).to_broadcast([P, 4, T, NH])

            def below_peak(t):
                dve.wait_ge(soft_tensor.sem, soft_tensor.at(t, "turn"))
                V.tensor_reduce(peak[:], ps[:, 1, :].rearrange("p (n s h) -> p n h s", n=4, s=T), AX.X, ALU.max).then_inc(soft_vector.sem, 1)
                dve.wait_ge(soft_vector.sem, soft_vector.at(t, "max"))
                V.tensor_tensor(by_key, ps[:, 1, :].rearrange("p (n s h) -> p n s h", n=4, s=T), over_keys(peak), ALU.subtract).then_inc(soft_vector.sem, 1)

            def share(t):
                dve.wait_ge(soft_scalar.sem, soft_scalar.at(t, "exp"))
                V.tensor_reduce(total[:], s_tok[:].rearrange("p n (s h) -> p n h s", s=T), AX.X, ALU.add).then_inc(soft_vector.sem, 1)
                dve.wait_ge(soft_vector.sem, soft_vector.at(t, "sum"))
                V.reciprocal(total[:], total[:]).then_inc(soft_vector.sem, 1)
                dve.wait_ge(soft_vector.sem, soft_vector.at(t, "rcp"))
                V.tensor_tensor(by_key, by_key, over_keys(total), ALU.mult).then_inc(soft_vector.sem, 1)

            def mixing(t, s):
                dve.wait_ge(mix_tensor.sem, mix_tensor.at(t, f"w{s}"))
                if s == 1 and (not isinstance(t, int) or t):
                    dve.wait_ge(mix_vector.sem, mix_vector.at(t - 1, f"a{T - 1}"))
                V.tensor_tensor(part[:, s % 3], qkv[:, 2 * HC:3 * HC, tok_cols(s)], ps[:, 2 + 2 * (s % 2):4 + 2 * (s % 2), :],
                                ALU.mult).then_inc(mix_vector.sem, 1)
                if s:
                    dve.wait_ge(mix_vector.sem, mix_vector.at(t, f"m{s}"))
                    if s == T - 1 and (not isinstance(t, int) or t):
                        dve.wait_ge(out_tensor.sem, out_tensor.at(t - 1, "out"))
                    V.tensor_tensor(mix[:] if s == T - 1 else mix_sum[:], part[:, 0] if s == 1 else mix_sum[:], part[:, s % 3],
                                    ALU.add).then_inc(mix_vector.sem, 1)

            def add_out(t):
                dve.wait_ge(out_tensor.sem, out_tensor.at(t, "out"))
                for c in range(HC):
                    last = V.scalar_tensor_tensor(hT[:, c, tok_cols(t)], ps[:, 6 + c, :], o_b[:, c:c + 1],
                                                  hT[:, c, tok_cols(t)], ALU.add, ALU.add)
                last.then_inc(res_vector.sem, 1)

            dve.wait_ge(qkv_scalar.sem, qkv_scalar.at(T - 1, f"o{3 * HC - 1}"))
            def queries(scored, softened, mixed):
                if scored is not None:
                    multiply(scored, range(2 * HC))
                for s in range(T):
                    if mixed is not None:
                        mixing(mixed, s)
                    if mixed is not None and (not isinstance(mixed, int) or mixed) and s == 5:
                        add_out(mixed - 1)
                    if scored is not None and s < T - 2:
                        multiply(scored, range((s + 2) * HC, (s + 3) * HC))
                    if softened is not None and s == 0:
                        below_peak(softened)
                    if softened is not None and s == 3:
                        share(softened)

            queries(0, None, None)
            queries(1, 0, None)
            queries(2, 1, 0)
            with dve.Fori(3, T) as t:
                queries(t, t - 1, t - 2)
            queries(None, T - 1, T - 2)
            queries(None, None, T - 1)
            add_out(T - 1)


def modulated_ffn(nc, ctx, a, out, hT, means, eps, ps, res, g1_w, g1_b, gate_loaded):
    E, F, J = 8, 1024, 16
    FC = F // P
    COLS = H * F // J
    PIECE = 4 * 512
    NP = COLS // PIECE
    PIECES = 2 * NP

    def sb(name, shape, dt=F32):
        return ctx.enter_context(nc.sbuf_tensor(name, shape, dt))

    def sem(name):
        return ctx.enter_context(nc.semaphore(name))

    g2_rep = sb("g2_rep", [P, HC, P])
    g2_rep_b = sb("g2_rep_b", [P, 1])
    g2_w = sb("g2_w", [P, HC, E])
    g2_b = sb("g2_b", [E, 1])
    same = sb("same", [P, B, J])
    PARTS = 3
    PART_SLOTS = 4
    base_f = sb("base_f", [P, P])
    base = sb("base", [P, P], BF16)
    base_part = sb("base_part", [P, PARTS, PIECE], BF16)
    w_base = sb("w_base", [P, PART_SLOTS, PIECE], BF16)
    tb1 = sb("tb1", [E, F])
    tb2 = sb("tb2", [E, H])
    b1 = sb("b1", [P, FC])
    b2 = sb("b2", [P, HC])
    msum = sb("msum", [P, HC, B])
    g_rep = sb("g_rep", [P, B])
    g_e = sb("g_e", [E, B])
    kron = sb("kron", [P, B, J])
    mb = sb("mb", [P, FC + HC, B])
    xn = sb("xn_f", [P, HC, B * S])
    sq = sb("sq_f", [P, HC, S])
    rstd = sb("rstd_f", [P, S])
    mixed = sb("mixed", [P, 2, PIECE])
    SLOTS = 9
    tw = sb("tw", [P, SLOTS, PIECE])
    whole = (mixed[:, 0, :], tw[:, SLOTS - 1, :])
    w1 = tw[:, 0:2, :].rearrange("p a (c f) -> p a c f", c=HC)
    w2 = tw[:, 2:4, :].rearrange("p a (f h) -> p a f h", f=FC)
    hid = tw[:, 4:6, :].rearrange("p a (f s) -> p (a f) s", s=S)
    part_w = [nc.dram_tensor(f"part_w{n}", [PARTS, J, COLS], BF16, kind="Internal").ap() for n in (1, 2)]
    own_w = [nc.dram_tensor(f"own_w{n}", [P, COLS], F32, kind="Internal").ap() for n in (1, 2)]

    loaded, base_zeroed, weight_zeroed = sem("loaded_f"), sem("base_zeroed"), sem("weight_zeroed")
    base_loaded, part_stored = sem("base_loaded"), sem("part_stored")
    base_made = Steps(sem("base_made"), ["base"])
    split = Steps(sem("split"), ["hi", "rest1", "mid", "rest2", "lo"])
    tw_loaded = [sem(f"tw_loaded{i}") for i in range(SLOTS)]
    part_loaded = [sem(f"part_loaded{i}") for i in range(PART_SLOTS)]
    whole_loaded, own_stored, own_up_loaded, own_down_loaded, stored = (
        [sem(f"{name}{i}") for i in range(2)] for name in ("whole_loaded", "own_stored", "own_up_loaded", "own_down_loaded", "stored"))
    mean_tensor = Steps(sem("mean_tensor"), ["mean"])
    var_tensor = Steps(sem("var_tensor"), ["var"])
    norm_scalar = Steps(sem("norm_scalar"), ["sq", "std"])
    centre_vector = Steps(sem("centre_vector"), ["xc"])
    norm_vector = Steps(sem("norm_vector"), ["rstd", "xn"])
    relu_tensor = Steps(sem("relu_tensor"), [f"o{o}" for o in range(HC)])
    relu_scalar = Steps(sem("relu_scalar"), [f"o{o}" for o in range(HC)])
    gate_tensor = Steps(sem("gate_tensor"), ["g", "b"])
    gate_scalar = Steps(sem("gate_scalar"), ["g"])
    gate_vector = Steps(sem("gate_vector"), ["kron", "mb1", "mb2"])
    weight_tensor = Steps(sem("weight_tensor"), ["w"])
    weight_copied = Steps(sem("weight_copied"), ["w"])
    ffn_tensor = Steps(sem("ffn_tensor"), [n for f in range(FC) for n in [f"up{f}"]] + ["down"])
    ffn_scalar = Steps(sem("ffn_scalar"), [f"gelu{f}" for f in range(FC)])
    ffn_vector = Steps(sem("ffn_vector"), ["res"])
    LOADS = 16 * 9

    with nc.Block() as block:
        @block.sync
        def _(sp):
            def load_up(b):
                sp.dma_start(w1[:, b % 2], own_w[0][b * J:(b + 1) * J, :].rearrange("j (i f) -> (j i) f", f=F)
                             .rearrange("(c p) f -> p c f", p=P)).then_inc(own_up_loaded[b % 2], 16)

            def load_down(b):
                sp.dma_start(w2[:, b % 2], own_w[1][b * J:(b + 1) * J, :].rearrange("j (i h) -> (j i) h", h=H)
                             .rearrange("(c p) h -> p c h", p=P)).then_inc(own_down_loaded[b % 2], 16)

            def load_tw(n):
                cols = slice(n % NP * PIECE, (n % NP + 1) * PIECE)
                sp.dma_start(tw[:, n % SLOTS, :], a["tw1" if n < NP else "tw2"][:, cols]).then_inc(tw_loaded[n % SLOTS], 16)

            for n in range(2):
                sp.dma_start(whole[n], a[f"fw{n + 1}"].rearrange("j (r c) -> (j r) c", c=PIECE)).then_inc(whole_loaded[n], 16)
            for dst, src in (
                (g2_rep[:], a["g2_rep"].rearrange("(c p) o -> p c o", p=P)), (g2_rep_b[:], a["g2_rep_b"]),
                (g2_w[:], a["g2_w"].rearrange("(c p) o -> p c o", p=P)), (g2_b[:], a["g2_b"]),
                (same[:], a["same"]),
                (tb1[:], a["tb1"]), (tb2[:], a["tb2"]), (b1[:], a["b1"]), (b2[:], a["b2"]),
            ):
                sp.dma_start(dst, src).then_inc(loaded, 16)
            sp.wait_ge(base_zeroed, 1)
            for q in range(PARTS):
                sp.dma_start(base_f[32 * q:32 * q + J, :], a["same"][0:J].rearrange("p b j -> p (b j)")).then_inc(base_loaded, 16)
            for n in range(SLOTS - 1):
                load_tw(n)
            def load_parts(n):
                cols = slice(n % NP * PIECE, (n % NP + 1) * PIECE)
                for q in range(PARTS):
                    sp.dma_start(w_base[32 * q:32 * q + J, n % PART_SLOTS, :], part_w[n // NP][q, :, cols])\
                        .then_inc(part_loaded[n % PART_SLOTS], 16)

            sp.wait_ge(weight_zeroed, 1)
            sp.wait_ge(part_stored, 16 * PARTS)
            for n in range(PART_SLOTS):
                load_parts(n)
            sp.wait_ge(split.sem, split.at(1, "lo"))
            load_tw(SLOTS - 1)
            for n in range(2, PIECES):
                sp.wait_ge(weight_tensor.sem, weight_tensor.at(n - 2, "w"))
                if n - 2 + PART_SLOTS == NP:
                    sp.wait_ge(part_stored, 16 * 2 * PARTS)
                if n - 2 + PART_SLOTS < PIECES:
                    load_parts(n - 2 + PART_SLOTS)
                if n - 2 + SLOTS < PIECES:
                    load_tw(n - 2 + SLOTS)
                if n == NP + 5:
                    for i in range(2):
                        sp.wait_ge(own_stored[i], 16 * NP // 2)
                    for b in range(2):
                        load_up(b)
            for i in range(2):
                sp.wait_ge(own_stored[i], 16 * PIECES // 2)
            for b in range(B):
                if b >= 2:
                    sp.wait_ge(ffn_tensor.sem, ffn_tensor.at(b - 2, "down"))
                    load_up(b)
                load_down(b)

        @block.gpsimd
        def _(pool):
            G = nc.gpsimd
            G.memset(base_f[:], 0.0).then_inc(base_zeroed, 1)
            G.memset(w_base[:], 0.0).then_inc(weight_zeroed, 1)
            pool.wait_ge(base_loaded, 16 * PARTS)
            G.tensor_copy(base[:], base_f[:]).then_inc(base_made.sem, 1)
            for n in range(2):
                pool.wait_ge(whole_loaded[n], 16)
                if n:
                    pool.wait_ge(part_stored, 16 * PARTS)
                for q, (part, rest) in enumerate((("hi", "rest1"), ("mid", "rest2"), ("lo", None))):
                    G.tensor_copy(base_part[:, q, :], whole[n]).then_inc(split.sem, 1)
                    pool.wait_ge(split.sem, split.at(n, part))
                    pool.dma_start(part_w[n][q].rearrange("j (r c) -> (j r) c", c=PIECE), base_part[:, q, :]).then_inc(part_stored, 16)
                    if rest:
                        G.tensor_tensor(whole[n], whole[n], base_part[:, q, :], ALU.subtract).then_inc(split.sem, 1)
                        pool.wait_ge(split.sem, split.at(n, rest))
            for b in range(B):
                pool.wait_ge(ffn_vector.sem, ffn_vector.at(b, "res"))
                pool.dma_start(out[:, :, b * S:(b + 1) * S].rearrange("c p s -> p c s"), res[:, b % 2]).then_inc(stored[b % 2], 16)
            for i in range(2):
                pool.wait_ge(stored[i], 16 * B // 2)

        @block.tensor
        def _(pe):
            def mm(o, w, x, first, last):
                return nc.tensor.matmul(o, w, x, start=first, stop=last)

            pe.wait_ge(gate_loaded, 32)

            def mean(b):
                if not isinstance(b, int) or b:
                    pe.wait_ge(centre_vector.sem, centre_vector.at(b - 1, "xc"))
                for c in range(HC):
                    last = mm(ps[:, 0, :], means[:], hT[:, c, tok_cols(b)], c == 0, c == HC - 1)
                last.then_inc(mean_tensor.sem, 1)

            def variance(b):
                pe.wait_ge(norm_scalar.sem, norm_scalar.at(b, "sq"))
                if not isinstance(b, int) or b:
                    pe.wait_ge(norm_scalar.sem, norm_scalar.at(b - 1, "std"))
                for c in range(HC):
                    last = mm(ps[:, 1, :], means[:], sq[:, c, :], c == 0, c == HC - 1)
                last.then_inc(var_tensor.sem, 1)

            def gate(b, o):
                pe.wait_ge(norm_vector.sem, norm_vector.at(b, "xn"))
                if not isinstance(b, int) or b:
                    pe.wait_ge(relu_scalar.sem, relu_scalar.at(b - 1, f"o{o}"))
                for c in range(HC):
                    last = mm(ps[:, 2 + o, :], g1_w[:, c, o * P:(o + 1) * P], xn[:, c, tok_cols(b)], c == 0, c == HC - 1)
                last.then_inc(relu_tensor.sem, 1)

            mean(0)
            mean(1)
            variance(0)
            mean(2)
            variance(1)

            def gate_beside_norm(b):
                mean(b + 3)
                gate(b, 0)
                variance(b + 2)
                gate(b, 1)

            gate_beside_norm(0)
            with pe.Fori(1, B - 3) as b:
                gate_beside_norm(b)
            gate(B - 3, 0)
            variance(B - 1)
            gate(B - 3, 1)
            for b in (B - 2, B - 1):
                gate(b, 0)
                gate(b, 1)
            pe.wait_ge(relu_scalar.sem, relu_scalar.at(B - 1, "o1"))
            pe.wait_ge(loaded, LOADS)
            for c in range(HC):
                mm(ps[:, 0, 0:B], g2_rep[:, c, :], msum[:, c, :], c == 0, c == HC - 1)
            for c in range(HC):
                last = mm(ps[0:E, 1, 0:B], g2_w[:, c, :], msum[:, c, :], c == 0, c == HC - 1)
            last.then_inc(gate_tensor.sem, 1)
            pe.wait_ge(gate_scalar.sem, gate_scalar.at(0, "g"))
            for f in range(FC):
                mm(ps[:, 2, f * B:(f + 1) * B], tb1[:, f * P:(f + 1) * P], g_e[:], True, True)
            for c in range(HC):
                last = mm(ps[:, 3, c * B:(c + 1) * B], tb2[:, c * P:(c + 1) * P], g_e[:], True, True)
            last.then_inc(gate_tensor.sem, 1)
            pe.wait_ge(gate_vector.sem, gate_vector.at(0, "mb2"))
            pe.wait_ge(base_made.sem, base_made.at(0, "base"))
            for n in range(PIECES):
                pe.wait_ge(tw_loaded[n % SLOTS], 16 * (n // SLOTS + 1))
                pe.wait_ge(part_loaded[n % PART_SLOTS], 16 * PARTS * (n // PART_SLOTS + 1))
                if n >= 2:
                    pe.wait_ge(weight_copied.sem, weight_copied.at(n - 2, "w"))
                for i in range(4):
                    cols = slice(i * 512, (i + 1) * 512)
                    bank = 4 * (n % 2) + i
                    mm(ps[:, bank, :], kron[:].rearrange("p b j -> p (b j)"), tw[:, n % SLOTS, cols], True, False)
                    last = mm(ps[:, bank, :], base[:], w_base[:, n % PART_SLOTS, cols], False, True)
                last.then_inc(weight_tensor.sem, 1)
            pe.wait_ge(weight_copied.sem, weight_copied.at(PIECES - 1, "w"))
            for b in range(B):
                pe.wait_ge(own_up_loaded[b % 2], 16 * (b // 2 + 1))
                for f in range(FC):
                    if f >= 4:
                        pe.wait_ge(ffn_scalar.sem, ffn_scalar.at(b, f"gelu{f - 4}"))
                    elif b:
                        pe.wait_ge(ffn_scalar.sem, ffn_scalar.at(b - 1, f"gelu{f + 4}"))
                    for c in range(HC):
                        last = mm(ps[:, f % 4, :], w1[:, b % 2, c, f * P:(f + 1) * P], xn[:, c, tok_cols(b)], c == 0, c == HC - 1)
                    last.then_inc(ffn_tensor.sem, 1)
                pe.wait_ge(own_down_loaded[b % 2], 16 * (b // 2 + 1))
                if b >= 2:
                    pe.wait_ge(ffn_vector.sem, ffn_vector.at(b - 2, "res"))
                for f in range(FC):
                    pe.wait_ge(ffn_scalar.sem, ffn_scalar.at(b, f"gelu{f}"))
                    for o in range(HC):
                        last = mm(ps[:, 4 + 2 * (b % 2) + o, :], w2[:, b % 2, f, o * P:(o + 1) * P], hid[:, f, :], f == 0, f == FC - 1)
                last.then_inc(ffn_tensor.sem, 1)

        @block.scalar
        def _(act):
            act.wait_ge(gate_loaded, 32)

            def square(b):
                act.wait_ge(centre_vector.sem, centre_vector.at(b, "xc"))
                if not isinstance(b, int) or b:
                    act.wait_ge(var_tensor.sem, var_tensor.at(b - 1, "var"))
                nc.scalar.activation(sq[:], xn[:, :, tok_cols(b)], ACT.Square).then_inc(norm_scalar.sem, 1)

            def deviation(b):
                act.wait_ge(var_tensor.sem, var_tensor.at(b, "var"))
                if not isinstance(b, int) or b:
                    act.wait_ge(norm_vector.sem, norm_vector.at(b - 1, "xn"))
                nc.scalar.activation(rstd[:], ps[:, 1, :], ACT.Sqrt, bias=eps[:, 0:1]).then_inc(norm_scalar.sem, 1)

            def relu(b, o):
                act.wait_ge(relu_tensor.sem, relu_tensor.at(b, f"o{o}"))
                if not isinstance(b, int) or b:
                    act.wait_ge(relu_scalar.sem, relu_scalar.at(b - 1, f"o{o}"))
                nc.scalar.activation(res[:, 0, o, :], ps[:, 2 + o, :], ACT.Relu, bias=g1_b[:, o:o + 1],
                                     accum_out=msum[:, o, bass.ds(b, 1)]).then_inc(relu_scalar.sem, 1)

            def relu_beside_norm(b):
                relu(b, 0)
                deviation(b + 2)
                square(b + 3)
                relu(b, 1)

            square(0)
            deviation(0)
            square(1)
            deviation(1)
            square(2)
            relu_beside_norm(0)
            with act.Fori(1, B - 3) as b:
                relu_beside_norm(b)
            relu(B - 3, 0)
            deviation(B - 1)
            relu(B - 3, 1)
            for b in (B - 2, B - 1):
                relu(b, 0)
                relu(b, 1)
            act.wait_ge(loaded, LOADS)
            act.wait_ge(gate_tensor.sem, gate_tensor.at(0, "g"))
            nc.scalar.activation(g_rep[:], ps[:, 0, 0:B], ACT.Identity, scale=1.0 / S, bias=g2_rep_b[:, 0:1])
            nc.scalar.activation(g_e[:], ps[0:E, 1, 0:B], ACT.Identity, scale=1.0 / S, bias=g2_b[:, 0:1]).then_inc(gate_scalar.sem, 1)
            for n in range(PIECES):
                cols = slice(n % NP * PIECE, (n % NP + 1) * PIECE)
                act.wait_ge(weight_copied.sem, weight_copied.at(n, "w"))
                act.dma_start(own_w[n // NP][:, cols], mixed[:, n % 2, :]).then_inc(own_stored[n % 2], 16)
            for b in range(B):
                if b == 0:
                    act.wait_ge(gate_vector.sem, gate_vector.at(0, "mb2"))
                for f in range(FC):
                    act.wait_ge(ffn_tensor.sem, ffn_tensor.at(b, f"up{f}"))
                    if f == 0 and b:
                        act.wait_ge(ffn_tensor.sem, ffn_tensor.at(b - 1, "down"))
                    nc.scalar.activation(hid[:, f, :], ps[:, f % 4, :], ACT.Gelu_apprx_tanh, bias=mb[:, f, b:b + 1]).then_inc(ffn_scalar.sem, 1)

        @block.vector
        def _(dve):
            V = nc.vector

            def centre(b):
                dve.wait_ge(mean_tensor.sem, mean_tensor.at(b, "mean"))
                V.tensor_tensor(xn[:, :, tok_cols(b)], hT[:, :, tok_cols(b)], spread_over(ps[:, 0, :], HC), ALU.subtract).then_inc(centre_vector.sem, 1)

            def normalise(b):
                dve.wait_ge(norm_scalar.sem, norm_scalar.at(b, "std"))
                V.reciprocal(rstd[:], rstd[:]).then_inc(norm_vector.sem, 1)
                dve.wait_ge(norm_vector.sem, norm_vector.at(b, "rstd"))
                V.tensor_tensor(xn[:, :, tok_cols(b)], xn[:, :, tok_cols(b)], spread_over(rstd[:], HC), ALU.mult).then_inc(norm_vector.sem, 1)

            centre(0)
            with dve.Fori(0, B - 1) as b:
                centre(b + 1)
                normalise(b)
            normalise(B - 1)
            dve.wait_ge(loaded, LOADS)
            dve.wait_ge(gate_scalar.sem, gate_scalar.at(0, "g"))
            V.tensor_tensor(kron[:], same[:], g_rep[:].rearrange("p (b o) -> p b o", o=1).to_broadcast([P, B, J]), ALU.mult).then_inc(gate_vector.sem, 1)
            dve.wait_ge(gate_tensor.sem, gate_tensor.at(0, "b"))
            V.tensor_tensor(mb[:, 0:FC, :], ps[:, 2, 0:FC * B].rearrange("p (f b) -> p f b", b=B),
                            b1[:].rearrange("p (f o) -> p f o", o=1).to_broadcast([P, FC, B]), ALU.add).then_inc(gate_vector.sem, 1)
            V.tensor_tensor(mb[:, FC:, :], ps[:, 3, 0:HC * B].rearrange("p (f b) -> p f b", b=B),
                            b2[:].rearrange("p (f o) -> p f o", o=1).to_broadcast([P, HC, B]), ALU.add).then_inc(gate_vector.sem, 1)
            for n in range(PIECES):
                dve.wait_ge(weight_tensor.sem, weight_tensor.at(n, "w"))
                if n >= 2:
                    dve.wait_ge(own_stored[n % 2], 16 * (n // 2))
                if n == 0:
                    dve.wait_ge(split.sem, split.at(0, "lo"))
                half = 4 * (n % 2)
                V.tensor_copy(mixed[:, n % 2, :], ps[:, half:half + 4, :].rearrange("p a b -> p (a b)")).then_inc(weight_copied.sem, 1)
            dve.wait_ge(gate_vector.sem, gate_vector.at(0, "mb2"))
            for b in range(B):
                dve.wait_ge(ffn_tensor.sem, ffn_tensor.at(b, "down"))
                if b >= 2:
                    dve.wait_ge(stored[b % 2], 16 * (b // 2))
                for c in range(HC):
                    last = V.scalar_tensor_tensor(res[:, b % 2, c, :], ps[:, 4 + 2 * (b % 2) + c, :], mb[:, FC + c, b:b + 1],
                                                  hT[:, c, tok_cols(b)], ALU.add, ALU.add)
                last.then_inc(ffn_vector.sem, 1)


def lay_out(i):
    f = lambda n: np.asarray(i[n])
    a = {}
    B,S,H,D = f('x').shape
    x = f('x').transpose(0,3,2,1).reshape(B, D*H//P, P, S).transpose(0,2,1,3)
    a['x'] = np.ascontiguousarray(x)
    a['ident'] = np.eye(P, dtype=np.float32)
    a['means'] = np.full((P,P), 1/H, np.float32)
    a['eps'] = np.full((P,1), 1e-5, np.float32)
    a['ws_t'] = f('L0_tok_weighted_sum').T
    a['tok_v'] = f('L0_tok_weight').T
    a['w_in'] = f('L0_attn_W_in'); a['w_out'] = f('L0_attn_W_out')
    wx = f('L0_attn_W_xproj'); bcw = wx[:, 16:]
    a['w_x'] = np.concatenate([bcw, bcw, bcw, wx[:, :16]], 1)
    a['w_dt'] = f('L0_attn_W_dt')
    a['up'] = f('L0_ffn_expert_up').transpose(1,0,2).reshape(H, -1)
    a['down'] = f('L0_ffn_expert_down')
    a['sup'] = f('L0_ffn_shared_up'); a['sdown'] = f('L0_ffn_shared_down')
    a['gate'] = f('L0_ffn_gate_weight').T
    ch = lambda v: np.moveaxis(v.reshape((-1, P) + v.shape[1:]), 0, 1)
    a['taps'] = ch(f('L0_attn_conv_w')[:,0,:]); a['tap_b'] = ch(f('L0_attn_conv_b')); a['b_dt'] = ch(f('L0_attn_b_dt'))
    a['d_skip'] = ch(f('L0_attn_D_skip')); a['a_log'] = ch(f('L0_attn_A_log'))
    E=16
    a['lower'] = np.broadcast_to(np.tril(np.ones((E,E),np.float32), -1), (P,E,E))
    a['picks'] = np.zeros((P, 48), np.float32)
    for part in range(3):
        a['picks'][32 * part:32 * part + 32, 0:32] = np.eye(32)
        a['picks'][16 * part:16 * part + 16, 32:48] = np.eye(16)
    fl = lambda v: ch(np.asarray(v).reshape(-1))
    a['qkv_w'] = f('L1_attn_in_proj_weight').T; a['qkv_b'] = fl(f('L1_attn_in_proj_bias'))
    a['pos_w'] = f('L1_attn_pos_proj_weight').T; a['pos_b'] = fl(f('L1_attn_pos_proj_bias'))
    a['o_w'] = f('L1_attn_out_proj_weight').T; a['o_b'] = fl(f('L1_attn_out_proj_bias'))
    a['pos_t'] = f('L1_attn_pos')[:15, 0].T
    a['r_w'] = fl(f('L1_attn_r_w_bias')); a['r_r'] = fl(f('L1_attn_r_r_bias'))
    hd = np.zeros((P, 8, 2, 8, 16), np.float32)
    for s in range(8):
        for c in range(2):
            for p in range(P): hd[p, s, c, s, c*8 + p//16] = 1
    hd = hd.reshape(P, 16, P)
    a['heads'] = hd; a['unheads'] = hd.transpose(2,1,0)
    a['g1_w'] = f('L1_ffn_gate_w1').T; a['g1_b'] = fl(f('L1_ffn_gate_b1'))
    g2 = f('L1_ffn_gate_w2')
    a['g2_rep'] = np.repeat(g2.T, 16, 1); a['g2_rep_b'] = np.repeat(f('L1_ffn_gate_b2'), 16)[:,None]
    a['g2_w'] = g2.T; a['g2_b'] = f('L1_ffn_gate_b2')[:,None]
    a['same'] = np.broadcast_to(np.tile(np.eye(16, dtype=np.float32), (8,1))[:,None,:], (P,8,16))
    a['tb1'] = f('L1_ffn_Tb1'); a['tb2'] = f('L1_ffn_Tb2')
    a['b1'] = fl(f('L1_ffn_b1')); a['b2'] = fl(f('L1_ffn_b2'))
    a['tw1'] = f('L1_ffn_TW1').transpose(0,2,1).reshape(P, -1); a['fw1'] = f('L1_ffn_W1').T.reshape(16, -1)
    a['tw2'] = f('L1_ffn_TW2').transpose(0,2,1).reshape(P, -1); a['fw2'] = f('L1_ffn_W2').T.reshape(16, -1)
    return {k: np.ascontiguousarray(v) for k,v in a.items()}


def kernel(**inputs):
    import concourse.bacc as _bacc
    from concourse.bass_utils import run_bass_kernel_spmd as _run

    nc = _bacc.Bacc("TRN2", target_bir_lowering=False, num_devices=1)
    arrays, aps = {}, {}
    for name, a in lay_out(inputs).items():
        arrays[f"in_{name}_dram"] = a
        aps[name] = nc.dram_tensor(f"in_{name}_dram", a.shape, mybir.dt.from_np(a.dtype), kind="ExternalInput").ap()
    out = nc.dram_tensor("out_0_dram", (HC, P, B * S), F32, kind="ExternalOutput").ap()
    vit_tower(nc, aps, out)
    r = _run(nc, [arrays], core_ids=[0])
    got = r.results[0]["out_0_dram"]
    return np.ascontiguousarray(got.reshape(H, B, S).transpose(1, 2, 0))
```
